# Optimizing a Trainium2 kernel written in Bass

```python
import numpy as np
import jax
import jax.numpy as jnp

def _softmax(x, axis=-1):
    return jax.nn.softmax(x, axis=axis)

def _gelu(x):
    return jax.nn.gelu(x, approximate=True)

def _silu(x):
    return jax.nn.silu(x)

def _sigmoid(x):
    return jax.nn.sigmoid(x)

def _layernorm(x, axis=-1, eps=1e-05):
    m = jnp.mean(x, axis=axis, keepdims=True)
    v = jnp.var(x, axis=axis, keepdims=True)
    return (x - m) / jnp.sqrt(v + eps)

def _scatter_add(tgt, idx, src, axis=0):
    return tgt.at[idx].add(src)

def _segment_sum(src, seg, n):
    return jax.ops.segment_sum(src, seg, n)
kernel_name = 'mk_perceiver_d2_seqx_r4_aa8592'

def setup_inputs(seed: int=0):
    np.random.seed(seed)
    _w = jnp.asarray

    def _rec_inputs():
        import jax
        import jax.numpy as jnp
        _rk = jax.random.key(seed)
        x = -0.0002928 + 1 * jax.random.normal(jax.random.fold_in(_rk, 1), (8, 64, 256), jnp.float32)
        _lenS = 64 - jax.random.randint(jax.random.fold_in(_rk, 7), (8,), 0, max(1, 64 // 4) + 1, jnp.int32)
        _lenS2 = 1601 - jax.random.randint(jax.random.fold_in(_rk, 8), (8,), 0, max(1, 1601 // 4) + 1, jnp.int32)
        _ctx_1024P = jax.random.normal(jax.random.fold_in(_rk, 11), (8, 16, 256), jnp.float32)
        _ctx_1024c = jax.random.dirichlet(jax.random.fold_in(_rk, 511), 0.3 * jnp.ones((16,), jnp.float32), (8, 1601))
        _ctx_1024t = jnp.einsum('bsk,bkd->bsd', _ctx_1024c, _ctx_1024P)
        _ctx_1024t = _ctx_1024t * jax.lax.rsqrt(jnp.mean(jnp.square(_ctx_1024t)) + 1e-12) * 0.953939
        ctx_1024 = -1.39393e-06 + 0.999914 * (_ctx_1024t + 0.3 * jax.random.normal(jax.random.fold_in(_rk, 611), (8, 1601, 256), jnp.float32))
        _validS = jnp.arange(64)[None, :] < _lenS[:, None]
        _validS2 = jnp.arange(1601)[None, :] < _lenS2[:, None]
        _causal = jnp.tril(jnp.ones((64, 64), dtype=bool))
        mask_BxS2_bf0 = jnp.logical_not(jnp.ones((8, 1601), dtype=bool))
        return (x, ctx_1024, mask_BxS2_bf0)
    x, ctx_1024, mask_BxS2_bf0 = _rec_inputs()

    def _L0_xattn_setup():
        import jax, jax.numpy as jnp
        import numpy as np
        EMBED_DIM = 256
        NUM_HEADS = 16
        HEAD_DIM = EMBED_DIM // NUM_HEADS
        B, T, S = (2, 512, 512)
        key = jax.random.key(seed)
        ks = jax.random.split(key, 12)
        xavier = lambda k: jax.random.uniform(k, (EMBED_DIM, EMBED_DIM), jnp.float32, -np.sqrt(6.0 / (2 * EMBED_DIM)), np.sqrt(6.0 / (2 * EMBED_DIM)))
        return {'query': jax.random.normal(ks[0], (B, T, EMBED_DIM), jnp.float32), 'key': jax.random.normal(ks[1], (B, S, EMBED_DIM), jnp.float32), 'value': jax.random.normal(ks[2], (B, S, EMBED_DIM), jnp.float32), 'key_padding_mask': jnp.zeros((B, S), dtype=bool), 'Wq': xavier(ks[3]), 'bq': jnp.zeros((EMBED_DIM,), jnp.float32), 'Wk': xavier(ks[4]), 'bk': jnp.zeros((EMBED_DIM,), jnp.float32), 'Wv': xavier(ks[5]), 'bv': jnp.zeros((EMBED_DIM,), jnp.float32), 'Wo': xavier(ks[6]), 'bo': jnp.zeros((EMBED_DIM,), jnp.float32)}
    _L0_xattn_all = _L0_xattn_setup()
    _L0_xattn_in = {k: v for k, v in _L0_xattn_all.items() if k in ('Wq', 'bq', 'Wk', 'bk', 'Wv', 'bv', 'Wo', 'bo')}
    del _L0_xattn_all

    def _L0_attn_setup():
        import jax, jax.numpy as jnp
        import numpy as np
        D, STATE, CONV = (256, 16, 4)
        B_, L_ = (8, 512)

        def _ssm_forward(x, conv_w, conv_b, Wd, bd, Wb, Wc, log_a, Wg, bg, Wo, bo):
            b, l, d = x.shape
            xt = jnp.transpose(x, (0, 2, 1))
            xc = jax.lax.conv_general_dilated(xt, conv_w, window_strides=(1,), padding=[(CONV - 1, 0)], feature_group_count=d, dimension_numbers=('NCH', 'OIH', 'NCH'))
            xc = jnp.transpose(xc + conv_b[None, :, None], (0, 2, 1))
            xc = jax.nn.silu(xc)
            delta = jax.nn.softplus(jnp.einsum('bld,ed->ble', xc, Wd) + bd)
            Bm = jnp.einsum('bld,nd->bln', xc, Wb)
            Cm = jnp.einsum('bld,nd->bln', xc, Wc)
            A = -jnp.exp(log_a)

            def step(h, inputs):
                dt, bt, ct, xt_ = inputs
                decay = jnp.exp(A[None] * dt[:, :, None])
                inp = dt[:, :, None] * xt_[:, :, None] * bt[:, None, :]
                h = decay * h + inp
                y = jnp.einsum('bdn,bn->bd', h, ct)
                return (h, y)
            h0 = jnp.zeros((b, d, STATE), dtype=x.dtype)
            seq = (jnp.moveaxis(delta, 1, 0), jnp.moveaxis(Bm, 1, 0), jnp.moveaxis(Cm, 1, 0), jnp.moveaxis(xc, 1, 0))
            _, ys = jax.lax.scan(step, h0, seq)
            y = jnp.moveaxis(ys, 0, 1)
            gate = jax.nn.sigmoid(jnp.einsum('bld,ed->ble', x, Wg) + bg)
            return jnp.einsum('bld,ed->ble', y * gate, Wo) + bo
        key = jax.random.key(seed)
        ks = jax.random.split(key, 12)
        s = 0.02
        return {'x': jax.random.normal(ks[0], (B_, L_, D), dtype=jnp.float32), 'conv_w': jax.random.normal(ks[1], (D, 1, CONV), dtype=jnp.float32) * s, 'conv_b': jnp.zeros((D,), dtype=jnp.float32), 'Wd': jax.random.normal(ks[2], (D, D), dtype=jnp.float32) * s, 'bd': jnp.zeros((D,), dtype=jnp.float32), 'Wb': jax.random.normal(ks[3], (STATE, D), dtype=jnp.float32) * s, 'Wc': jax.random.normal(ks[4], (STATE, D), dtype=jnp.float32) * s, 'log_a': jnp.log(jnp.tile(jnp.linspace(1.0, STATE, STATE, dtype=jnp.float32), (D, 1))), 'Wg': jax.random.normal(ks[5], (D, D), dtype=jnp.float32) * s, 'bg': jnp.zeros((D,), dtype=jnp.float32), 'Wo': jax.random.normal(ks[6], (D, D), dtype=jnp.float32) * s, 'bo': jnp.zeros((D,), dtype=jnp.float32)}
    _L0_attn_all = _L0_attn_setup()
    _L0_attn_in = {k: v for k, v in _L0_attn_all.items() if k in ('conv_w', 'conv_b', 'Wd', 'bd', 'Wb', 'Wc', 'log_a', 'Wg', 'bg', 'Wo', 'bo')}
    del _L0_attn_all

    def _L0_ffn_setup():
        import jax, jax.numpy as jnp
        import numpy as np
        D_MODEL = 256
        D_FF = 1024
        NUM_EXPERTS = 8
        B, N = (16, 256)
        key = jax.random.key(seed)
        ks = jax.random.split(key, 7)
        s_in = 1.0 / np.sqrt(D_MODEL)
        s_ff = 1.0 / np.sqrt(D_FF)
        return {'x': jax.random.normal(ks[0], (B, N, D_MODEL), dtype=jnp.float32), 'Wr': jax.random.uniform(ks[1], (D_MODEL, NUM_EXPERTS), jnp.float32, -s_in, s_in), 'br': jax.random.uniform(ks[2], (NUM_EXPERTS,), jnp.float32, -s_in, s_in), 'W1': jax.random.uniform(ks[3], (NUM_EXPERTS, D_MODEL, D_FF), jnp.float32, -s_in, s_in), 'b1': jax.random.uniform(ks[4], (NUM_EXPERTS, D_FF), jnp.float32, -s_in, s_in), 'W2': jax.random.uniform(ks[5], (NUM_EXPERTS, D_FF, D_MODEL), jnp.float32, -s_ff, s_ff), 'b2': jax.random.uniform(ks[6], (NUM_EXPERTS, D_MODEL), jnp.float32, -s_ff, s_ff)}
    _L0_ffn_all = _L0_ffn_setup()
    _L0_ffn_in = {k: v for k, v in _L0_ffn_all.items() if k in ('Wr', 'br', 'W1', 'b1', 'W2', 'b2')}
    del _L0_ffn_all

    def _L1_xattn_setup():
        import jax, jax.numpy as jnp
        import numpy as np
        DIM = 256
        EPS_DENOM = 1e-06
        EPS_LN = 1e-05

        def _layernorm(x, gamma, beta):
            mu = jnp.mean(x, axis=-1, keepdims=True)
            var = jnp.var(x, axis=-1, keepdims=True)
            return (x - mu) * jax.lax.rsqrt(var + EPS_LN) * gamma + beta
        key = jax.random.key(seed)
        ks = jax.random.split(key, 12)
        B, T, D = (8, 1024, DIM)
        s = 1.0 / np.sqrt(D)
        return {'audio': jax.random.normal(ks[0], (B, T, D), jnp.float32), 'video': jax.random.normal(ks[1], (B, T, D), jnp.float32), 'Wq': jax.random.normal(ks[2], (D, D), jnp.float32) * s, 'bq': jax.random.normal(ks[3], (D,), jnp.float32) * 0.02, 'Wk': jax.random.normal(ks[4], (D, D), jnp.float32) * s, 'bk': jax.random.normal(ks[5], (D,), jnp.float32) * 0.02, 'Wv': jax.random.normal(ks[6], (D, D), jnp.float32) * s, 'bv': jax.random.normal(ks[7], (D,), jnp.float32) * 0.02, 'Wo': jax.random.normal(ks[8], (D, D), jnp.float32) * s, 'bo': jax.random.normal(ks[9], (D,), jnp.float32) * 0.02, 'gamma': jnp.ones((D,), jnp.float32), 'beta': jnp.zeros((D,), jnp.float32)}
    _L1_xattn_all = _L1_xattn_setup()
    _L1_xattn_in = {k: v for k, v in _L1_xattn_all.items() if k in ('Wq', 'bq', 'Wk', 'bk', 'Wv', 'bv', 'Wo', 'bo', 'gamma', 'beta')}
    del _L1_xattn_all

    def _L1_attn_setup():
        import jax, jax.numpy as jnp
        import numpy as np
        D_MODEL, D_STATE, EXPAND = (256, 16, 2)
        D_INNER = EXPAND * D_MODEL
        BATCH, SEQ = (4, 1024)
        key = jax.random.key(seed)
        ks = jax.random.split(key, 9)
        s = 0.02
        return {'x': jax.random.normal(ks[0], (BATCH, SEQ, D_MODEL), jnp.float32), 'W_in': jax.random.normal(ks[1], (D_MODEL, 2 * D_INNER), jnp.float32) * s, 'conv_w': jax.random.normal(ks[2], (D_INNER, 1, 3), jnp.float32) * s, 'conv_b': jax.random.normal(ks[3], (D_INNER,), jnp.float32) * s, 'W_B': jax.random.normal(ks[4], (D_INNER, D_STATE), jnp.float32) * s, 'W_C': jax.random.normal(ks[5], (D_INNER, D_STATE), jnp.float32) * s, 'A': jax.random.normal(ks[6], (D_STATE,), jnp.float32), 'D': jnp.ones((D_INNER,), jnp.float32), 'W_out': jax.random.normal(ks[7], (D_INNER, D_MODEL), jnp.float32) * s}
    _L1_attn_all = _L1_attn_setup()
    _L1_attn_in = {k: v for k, v in _L1_attn_all.items() if k in ('W_in', 'conv_w', 'conv_b', 'W_B', 'W_C', 'A', 'D', 'W_out')}
    del _L1_attn_all

    def _L1_ffn_setup():
        import jax, jax.numpy as jnp
        import numpy as np
        EMB_DIM = 256
        HIDDEN = int(2 / 3 * 4 * EMB_DIM)
        NUM_EXPERTS = 8
        TOP_K = 2
        B, S = (4, 256)
        key = jax.random.key(seed)
        ks = jax.random.split(key, 5)
        sc = 1.0 / np.sqrt(EMB_DIM)
        sh = 1.0 / np.sqrt(HIDDEN)
        return {'x': jax.random.normal(ks[0], (B, S, EMB_DIM), dtype=jnp.float32), 'Wg': jax.random.normal(ks[1], (NUM_EXPERTS, EMB_DIM), dtype=jnp.float32) * sc, 'W1': jax.random.normal(ks[2], (NUM_EXPERTS, HIDDEN, EMB_DIM), dtype=jnp.float32) * sc, 'W2': jax.random.normal(ks[3], (NUM_EXPERTS, HIDDEN, EMB_DIM), dtype=jnp.float32) * sc, 'W3': jax.random.normal(ks[4], (NUM_EXPERTS, EMB_DIM, HIDDEN), dtype=jnp.float32) * sh}
    _L1_ffn_all = _L1_ffn_setup()
    _L1_ffn_in = {k: v for k, v in _L1_ffn_all.items() if k in ('Wg', 'W1', 'W2', 'W3')}
    del _L1_ffn_all
    return {'x': x, 'ctx_1024': ctx_1024, 'mask_BxS2_bf0': mask_BxS2_bf0, 'L0_xattn_Wq': _L0_xattn_in['Wq'], 'L0_xattn_bq': _L0_xattn_in['bq'], 'L0_xattn_Wk': _L0_xattn_in['Wk'], 'L0_xattn_bk': _L0_xattn_in['bk'], 'L0_xattn_Wv': _L0_xattn_in['Wv'], 'L0_xattn_bv': _L0_xattn_in['bv'], 'L0_xattn_Wo': _L0_xattn_in['Wo'], 'L0_xattn_bo': _L0_xattn_in['bo'], 'L0_attn_conv_w': _L0_attn_in['conv_w'], 'L0_attn_conv_b': _L0_attn_in['conv_b'], 'L0_attn_Wd': _L0_attn_in['Wd'], 'L0_attn_bd': _L0_attn_in['bd'], 'L0_attn_Wb': _L0_attn_in['Wb'], 'L0_attn_Wc': _L0_attn_in['Wc'], 'L0_attn_log_a': _L0_attn_in['log_a'], 'L0_attn_Wg': _L0_attn_in['Wg'], 'L0_attn_bg': _L0_attn_in['bg'], 'L0_attn_Wo': _L0_attn_in['Wo'], 'L0_attn_bo': _L0_attn_in['bo'], 'L0_ffn_Wr': _L0_ffn_in['Wr'], 'L0_ffn_br': _L0_ffn_in['br'], 'L0_ffn_W1': _L0_ffn_in['W1'], 'L0_ffn_b1': _L0_ffn_in['b1'], 'L0_ffn_W2': _L0_ffn_in['W2'], 'L0_ffn_b2': _L0_ffn_in['b2'], 'L1_xattn_Wq': _L1_xattn_in['Wq'], 'L1_xattn_bq': _L1_xattn_in['bq'], 'L1_xattn_Wk': _L1_xattn_in['Wk'], 'L1_xattn_bk': _L1_xattn_in['bk'], 'L1_xattn_Wv': _L1_xattn_in['Wv'], 'L1_xattn_bv': _L1_xattn_in['bv'], 'L1_xattn_Wo': _L1_xattn_in['Wo'], 'L1_xattn_bo': _L1_xattn_in['bo'], 'L1_xattn_gamma': _L1_xattn_in['gamma'], 'L1_xattn_beta': _L1_xattn_in['beta'], 'L1_attn_W_in': _L1_attn_in['W_in'], 'L1_attn_conv_w': _L1_attn_in['conv_w'], 'L1_attn_conv_b': _L1_attn_in['conv_b'], 'L1_attn_W_B': _L1_attn_in['W_B'], 'L1_attn_W_C': _L1_attn_in['W_C'], 'L1_attn_A': _L1_attn_in['A'], 'L1_attn_D': _L1_attn_in['D'], 'L1_attn_W_out': _L1_attn_in['W_out'], 'L1_ffn_Wg': _L1_ffn_in['Wg'], 'L1_ffn_W1': _L1_ffn_in['W1'], 'L1_ffn_W2': _L1_ffn_in['W2'], 'L1_ffn_W3': _L1_ffn_in['W3']}

def reference(x, ctx_1024, mask_BxS2_bf0, L0_xattn_Wq, L0_xattn_bq, L0_xattn_Wk, L0_xattn_bk, L0_xattn_Wv, L0_xattn_bv, L0_xattn_Wo, L0_xattn_bo, L0_attn_conv_w, L0_attn_conv_b, L0_attn_Wd, L0_attn_bd, L0_attn_Wb, L0_attn_Wc, L0_attn_log_a, L0_attn_Wg, L0_attn_bg, L0_attn_Wo, L0_attn_bo, L0_ffn_Wr, L0_ffn_br, L0_ffn_W1, L0_ffn_b1, L0_ffn_W2, L0_ffn_b2, L1_xattn_Wq, L1_xattn_bq, L1_xattn_Wk, L1_xattn_bk, L1_xattn_Wv, L1_xattn_bv, L1_xattn_Wo, L1_xattn_bo, L1_xattn_gamma, L1_xattn_beta, L1_attn_W_in, L1_attn_conv_w, L1_attn_conv_b, L1_attn_W_B, L1_attn_W_C, L1_attn_A, L1_attn_D, L1_attn_W_out, L1_ffn_Wg, L1_ffn_W1, L1_ffn_W2, L1_ffn_W3):
    import jax
    import jax.numpy as jnp

    def _L0_xattn_ref(query, key, value, key_padding_mask, Wq, bq, Wk, bk, Wv, bv, Wo, bo):
        import jax, jax.numpy as jnp
        import numpy as np
        EMBED_DIM = 256
        NUM_HEADS = 16
        HEAD_DIM = EMBED_DIM // NUM_HEADS
        B, T, S = (2, 512, 512)
        bsz, tgt_len, _ = query.shape
        src_len = key.shape[1]
        q = (query @ Wq.T + bq).reshape(bsz, tgt_len, NUM_HEADS, HEAD_DIM).transpose(0, 2, 1, 3)
        k = (key @ Wk.T + bk).reshape(bsz, src_len, NUM_HEADS, HEAD_DIM).transpose(0, 2, 1, 3)
        v = (value @ Wv.T + bv).reshape(bsz, src_len, NUM_HEADS, HEAD_DIM).transpose(0, 2, 1, 3)
        scale = HEAD_DIM ** (-0.5)
        scores = jnp.einsum('bhtd,bhsd->bhts', q, k) * scale
        causal_mask = jnp.triu(jnp.ones((tgt_len, src_len), dtype=bool), k=1)
        neg_inf = jnp.finfo(scores.dtype).min
        scores = jnp.where(causal_mask[None, None], neg_inf, scores)
        scores = jnp.where(key_padding_mask[:, None, None, :], neg_inf, scores)
        attn = jax.nn.softmax(scores, axis=-1)
        out = jnp.einsum('bhts,bhsd->bhtd', attn, v)
        out = out.transpose(0, 2, 1, 3).reshape(bsz, tgt_len, EMBED_DIM)
        return out @ Wo.T + bo

    def _L0_attn_ref(x, conv_w, conv_b, Wd, bd, Wb, Wc, log_a, Wg, bg, Wo, bo):
        import jax, jax.numpy as jnp
        import numpy as np
        D, STATE, CONV = (256, 16, 4)
        B_, L_ = (8, 512)

        def _ssm_forward(x, conv_w, conv_b, Wd, bd, Wb, Wc, log_a, Wg, bg, Wo, bo):
            b, l, d = x.shape
            xt = jnp.transpose(x, (0, 2, 1))
            xc = jax.lax.conv_general_dilated(xt, conv_w, window_strides=(1,), padding=[(CONV - 1, 0)], feature_group_count=d, dimension_numbers=('NCH', 'OIH', 'NCH'))
            xc = jnp.transpose(xc + conv_b[None, :, None], (0, 2, 1))
            xc = jax.nn.silu(xc)
            delta = jax.nn.softplus(jnp.einsum('bld,ed->ble', xc, Wd) + bd)
            Bm = jnp.einsum('bld,nd->bln', xc, Wb)
            Cm = jnp.einsum('bld,nd->bln', xc, Wc)
            A = -jnp.exp(log_a)

            def step(h, inputs):
                dt, bt, ct, xt_ = inputs
                decay = jnp.exp(A[None] * dt[:, :, None])
                inp = dt[:, :, None] * xt_[:, :, None] * bt[:, None, :]
                h = decay * h + inp
                y = jnp.einsum('bdn,bn->bd', h, ct)
                return (h, y)
            h0 = jnp.zeros((b, d, STATE), dtype=x.dtype)
            seq = (jnp.moveaxis(delta, 1, 0), jnp.moveaxis(Bm, 1, 0), jnp.moveaxis(Cm, 1, 0), jnp.moveaxis(xc, 1, 0))
            _, ys = jax.lax.scan(step, h0, seq)
            y = jnp.moveaxis(ys, 0, 1)
            gate = jax.nn.sigmoid(jnp.einsum('bld,ed->ble', x, Wg) + bg)
            return jnp.einsum('bld,ed->ble', y * gate, Wo) + bo
        return _ssm_forward(x, conv_w, conv_b, Wd, bd, Wb, Wc, log_a, Wg, bg, Wo, bo)

    def _L0_ffn_ref(x, Wr, br, W1, b1, W2, b2):
        import jax, jax.numpy as jnp
        import numpy as np
        D_MODEL = 256
        D_FF = 1024
        NUM_EXPERTS = 8
        B, N = (16, 256)
        scores = jnp.einsum('bh,he->be', x.mean(axis=1), Wr) + br
        top1 = jnp.argmax(scores, axis=-1)
        w1 = W1[top1]
        c1 = b1[top1]
        w2 = W2[top1]
        c2 = b2[top1]
        h = jax.nn.relu(jnp.einsum('bnh,bhf->bnf', x, w1) + c1[:, None, :])
        out = jnp.einsum('bnf,bfh->bnh', h, w2) + c2[:, None, :]
        return out

    def _L1_xattn_ref(audio, video, Wq, bq, Wk, bk, Wv, bv, Wo, bo, gamma, beta):
        import jax, jax.numpy as jnp
        import numpy as np
        DIM = 256
        EPS_DENOM = 1e-06
        EPS_LN = 1e-05

        def _layernorm(x, gamma, beta):
            mu = jnp.mean(x, axis=-1, keepdims=True)
            var = jnp.var(x, axis=-1, keepdims=True)
            return (x - mu) * jax.lax.rsqrt(var + EPS_LN) * gamma + beta
        Q = audio @ Wq.T + bq
        K = video @ Wk.T + bk
        V = video @ Wv.T + bv
        Q = jax.nn.elu(Q) + 1.0
        K = jax.nn.elu(K) + 1.0
        KV = jnp.einsum('btd,bte->bde', K, V)
        K_sum = K.sum(axis=1)
        attn_num = jnp.einsum('btd,bde->bte', Q, KV)
        attn_denom = Q * K_sum[:, None, :] + EPS_DENOM
        attn_out = attn_num / attn_denom
        attn_out = attn_out @ Wo.T + bo
        return _layernorm(audio + attn_out, gamma, beta)

    def _L1_attn_ref(x, W_in, conv_w, conv_b, W_B, W_C, A, D, W_out):
        import jax, jax.numpy as jnp
        import numpy as np
        D_MODEL, D_STATE, EXPAND = (256, 16, 2)
        D_INNER = EXPAND * D_MODEL
        BATCH, SEQ = (4, 1024)
        d_inner = conv_w.shape[0]
        xr = jnp.einsum('bld,de->ble', x, W_in)
        x_main, res = (xr[..., :d_inner], xr[..., d_inner:])
        xc = jax.lax.conv_general_dilated(x_main.transpose(0, 2, 1), conv_w, (1,), [(1, 1)], dimension_numbers=('NCH', 'OIH', 'NCH'), feature_group_count=d_inner)
        xc = (xc + conv_b[None, :, None]).transpose(0, 2, 1)
        xc = jax.nn.silu(xc)
        Bt = jnp.einsum('bli,is->bls', xc, W_B)
        Ct = jnp.einsum('bli,is->bls', xc, W_C)
        decay = jnp.exp(-jax.nn.softplus(A))

        def step(state, bc):
            b_t, c_t = bc
            state = state * decay + b_t
            return (state, jnp.sum(state * c_t, axis=-1))
        _, ys = jax.lax.scan(step, jnp.zeros_like(Bt[:, 0]), (Bt.transpose(1, 0, 2), Ct.transpose(1, 0, 2)))
        ys = ys.T
        y = ys[..., None] + xc * D
        y = y * jax.nn.silu(res)
        return jnp.einsum('bli,id->bld', y, W_out)

    def _L1_ffn_ref(x, Wg, W1, W2, W3):
        import jax, jax.numpy as jnp
        import numpy as np
        EMB_DIM = 256
        HIDDEN = int(2 / 3 * 4 * EMB_DIM)
        NUM_EXPERTS = 8
        TOP_K = 2
        B, S = (4, 256)
        gate_logits = jnp.einsum('bsd,ed->bse', x, Wg)
        top_v, top_i = jax.lax.top_k(gate_logits, TOP_K)
        mask = jnp.any(top_i[..., :, None] == jnp.arange(NUM_EXPERTS), axis=-2)
        sparse_logits = jnp.where(mask, gate_logits, -jnp.inf)
        gating = jax.nn.softmax(sparse_logits, axis=-1)
        h1 = jnp.einsum('bsd,ehd->bseh', x, W1)
        h2 = jnp.einsum('bsd,ehd->bseh', x, W2)
        hidden = jax.nn.silu(h1) * h2
        expert_out = jnp.einsum('bseh,edh->bsed', hidden, W3)
        return jnp.einsum('bsed,bse->bsd', expert_out, gating)
    x = x + _L0_xattn_ref(_layernorm(x, axis=-1), ctx_1024, ctx_1024, mask_BxS2_bf0, L0_xattn_Wq, L0_xattn_bq, L0_xattn_Wk, L0_xattn_bk, L0_xattn_Wv, L0_xattn_bv, L0_xattn_Wo, L0_xattn_bo)
    x = x + _L0_attn_ref(_layernorm(x, axis=-1), L0_attn_conv_w, L0_attn_conv_b, L0_attn_Wd, L0_attn_bd, L0_attn_Wb, L0_attn_Wc, L0_attn_log_a, L0_attn_Wg, L0_attn_bg, L0_attn_Wo, L0_attn_bo)
    x = x + _L0_ffn_ref(_layernorm(x, axis=-1), L0_ffn_Wr, L0_ffn_br, L0_ffn_W1, L0_ffn_b1, L0_ffn_W2, L0_ffn_b2)
    x = x + _L1_xattn_ref(_layernorm(x, axis=-1), ctx_1024, L1_xattn_Wq, L1_xattn_bq, L1_xattn_Wk, L1_xattn_bk, L1_xattn_Wv, L1_xattn_bv, L1_xattn_Wo, L1_xattn_bo, L1_xattn_gamma, L1_xattn_beta)
    x = x + _L1_attn_ref(_layernorm(x, axis=-1), L1_attn_W_in, L1_attn_conv_w, L1_attn_conv_b, L1_attn_W_B, L1_attn_W_C, L1_attn_A, L1_attn_D, L1_attn_W_out)
    x = x + _L1_ffn_ref(_layernorm(x, axis=-1), L1_ffn_Wg, L1_ffn_W1, L1_ffn_W2, L1_ffn_W3)
    return x

_drawn_inputs = setup_inputs


def setup_inputs(seed=0):
    import zlib

    import numpy as np

    out = dict(_drawn_inputs(seed))
    spreads = {'L0_xattn_bq': (0.0, 0.1),
     'L0_xattn_bk': (0.0, 2.0),
     'L0_xattn_bv': (0.0, 0.1),
     'L0_xattn_bo': (0.0, 0.1),
     'L0_attn_conv_b': (0.0, 0.8),
     'L0_attn_bd': (0.0, 0.8),
     'L0_attn_bg': (0.0, 0.8),
     'L0_attn_bo': (0.0, 0.1),
     'L1_xattn_gamma': (1.0, 0.2),
     'L1_xattn_beta': (0.0, 0.1),
     'L1_attn_D': (1.0, 0.6)}
    factors = {'L0_attn_conv_w': 8.0,
     'L0_attn_Wd': 8.0,
     'L0_attn_Wb': 8.0,
     'L0_attn_Wc': 8.0,
     'L0_attn_log_a': 8.0,
     'L0_attn_Wg': 8.0,
     'L0_attn_Wo': 8.0,
     'L1_xattn_bo': 200.0,
     'L1_attn_W_in': 8.0,
     'L1_attn_conv_w': 8.0,
     'L1_attn_conv_b': 8.0,
     'L1_attn_W_B': 8.0,
     'L1_attn_W_C': 8.0,
     'L1_attn_A': 8.0,
     'L1_attn_W_out': 8.0,
     'L0_ffn_b1': 8.0,
     'L0_ffn_b2': 8.0,
     'L1_xattn_bq': 8.0,
     'L1_xattn_bk': 8.0,
     'L1_xattn_bv': 3.402,
     'L1_ffn_Wg': 8.0,
     'L1_ffn_W1': 8.0,
     'L1_ffn_W2': 8.0,
     'L1_ffn_W3': 8.0}
    for name, (base, spread) in spreads.items():
        noise = np.random.default_rng([zlib.crc32(name.encode()), seed]).standard_normal(out[name].shape)
        drawn = base * np.exp(spread * noise) if base else spread * noise
        out[name] = jnp.asarray(drawn.astype(out[name].dtype))
    for name, factor in factors.items():
        out[name] = (out[name] * factor).astype(out[name].dtype)
    return out
```

```python
from contextlib import ExitStack

import concourse.bass as bass
import numpy as np
from concourse import mybir

B, T, D = 8, 64, 256
S = 1601
TOK = B * T
NT = TOK // 128
NC = D // 128
REST = S - T
KT = 13
KLAST = S - 12 * 128
G = 7
H, HD = 16, 16
N = 16
E = 8
F0 = 1024
F1 = 682
F1C = [128] * 5 + [F1 - 5 * 128]
DI = 512
FMAX = float(np.finfo(np.float32).max)



def _places(sizes):
    at, out = 0, {}
    for name, n in sizes:
        out[name] = (at, n)
        at += n
    return out, at


COLS, NCOLS = _places([
    ("bq0", 2), ("bk0", 2), ("bv0", 2), ("conv0", 8), ("conv0b", 2), ("bd", 2), ("bg", 2),
    ("log_a", 32), ("bq1", 2), ("conv1", 12), ("conv1b", 4), ("D1", 4), ("A1", 1)])
ROWS, NROWS = _places([
    ("bo0", D), ("boa", D), ("bk1", D), ("bv1", D), ("bo1", D), ("gamma", D), ("beta", D), ("br", E)])
CONSTS, NCONSTS = _places([
    ("ident", 128), ("causal", T), ("parity", 2), ("iota", E), ("eps", 1), ("one", 1), ("minus1", 1),
    ("batch", NT * 128), ("state", 2 * N), ("ones", 128)])
W0N = NC * F0 + (F0 // 128) * D + F0 // 128 + NC
W1N = 2 * NC * F1 + 6 * D
NAT = KT * (D + 1)
CTT = NC * S


def perceiver(nc, x, first_ctx, ctx_t, ctx_n, mask, cols, rows, consts, w_x0, w_m0, w_bc0, w_r, w0,
              w_x1, w_in, w_out, w_bc1, w_g1, w1, out):
    f32, bf16, u8, u32 = mybir.dt.float32, mybir.dt.bfloat16, mybir.dt.uint8, mybir.dt.uint32
    i32 = mybir.dt.int32
    ALU, ACT, AX = mybir.AluOpType, mybir.ActivationFunctionType, mybir.AxisListType
    ctx = ExitStack()

    def sb(name, shape, dt=f32):
        return ctx.enter_context(nc.sbuf_tensor(name, shape, dt))

    def sem(name):
        return ctx.enter_context(nc.semaphore(name))

    def spread(ap, axis, n):
        ap = ap.unsqueeze(axis)
        shape = list(ap.shape)
        shape[axis] = n
        return ap.broadcast_to(shape)

    with ctx:
        x_tok = sb("x_tok", [128, NT, D])
        xb = sb("xb", [128, NT, D])
        xn = sb("xn", [128, NT, D])
        xnT = sb("xnT", [128, NC, TOK])
        stats = sb("stats", [128, NT, 6])
        mv = sb("mv", [128, NT, 2])
        lnv = sb("lnv", [128, NT])
        rstd = sb("rstd", [128, NT])
        cst = sb("cst", [128, NCONSTS])
        col = sb("col", [128, NCOLS])
        row = sb("row", [128, NROWS])
        wx0 = sb("wx0", [128, 4, NC, D])
        wm0 = sb("wm0", [128, 3, NC, D])
        wbc0 = sb("wbc0", [128, NC, 2 * N])
        wr = sb("wr", [128, NC, E])
        wx1 = sb("wx1", [128, 4, NC, D])
        win = sb("win", [128, NC, 2 * DI])
        wout = sb("wout", [128, DI // 128, D])
        wbc1 = sb("wbc1", [128, DI // 128, 2 * N])
        wg1 = sb("wg1", [128, NC, E])
        arena = sb("arena", [128, 2 * W0N + 2 * W1N])
        cT = [arena[:, k * NAT:k * NAT + CTT].rearrange("p (c s) -> p c s", c=NC) for k in range(2)]
        cN = [arena[:, (2 + k) * NAT:(3 + k) * NAT].rearrange("p (k d) -> p k d", d=D + 1) for k in range(2)]
        cT2 = [arena[:, (2 + k) * NAT:(2 + k) * NAT + CTT].rearrange("p (c s) -> p c s", c=NC) for k in range(2)]
        wf0 = [arena[:, k * W0N:(k + 1) * W0N] for k in range(2)]
        wf1 = [arena[:, 2 * W0N + k * W1N:2 * W0N + (k + 1) * W1N] for k in range(2)]
        tail = arena[:, 4 * NAT:4 * NAT + 6 * 512]
        inp = [tail[:, c * 512:(c + 1) * 512] for c in range(NC)]
        hst = [tail[:, (2 + c) * 512:(3 + c) * 512] for c in range(NC)]
        zk = [tail[:, (4 + k) * 512:(5 + k) * 512] for k in range(2)]
        ktc = sb("ktc", [128, B, NC, D + 1])
        work = sb("work", [128, 14720])

        def area(at, *shape):
            n = int(np.prod(shape))
            v = work[:, at:at + n]
            names = "abcd"[:len(shape)]
            if len(shape) == 1:
                return v
            return v.rearrange(f"p ({' '.join(names)}) -> p {' '.join(names)}",
                               **{k: s for k, s in zip(names[1:], shape[1:])})

        c0T = area(0, NC, TOK)
        qT = area(1024, NC, TOK)
        kb2 = area(2048, NC, B, 2, T)
        vbd = area(4096, B, 8, 34)
        P = area(6272, NT, 4, 256)
        PT = area(10368, NT, 4, 256)
        vr8 = area(14464, D)
        maskf = sb("maskf", [128, NT, T])
        mask8 = sb("mask8", [128, NT, T], u8)
        csum = sb("csum", [128, NC, B])
        mx = sb("mx", [128, NT, 4, 4])
        rest = sb("rest", [128, NT, 4, 4])
        den = sb("den", [128, NT, H])
        vro = area(6272, NT, D)
        oa = area(6272 + 1024, NT, D)
        oT = area(1024, NC, TOK)
        xc = area(0, NC, TOK)
        dt = area(1024, NC, TOK)
        dtx = area(2048, NC, TOK)
        gate = area(3072, NC, TOK)
        dec = [[area(4096 + (2 * m + c) * 512, 512) for c in range(NC)] for m in range(2)]
        hc = [[area(6144 + (2 * m + c) * 512, 512) for c in range(NC)] for m in range(2)]
        ym = area(8192, NC, TOK)
        ek = [area(9216 + k * 512, 512) for k in range(2)]
        kk = [area(10240 + k * 512, 512) for k in range(2)]
        tmp = area(11264, NC, TOK)
        bc = area(12288, 512)
        r1 = area(12800, 512)
        aneg = sb("aneg", [128, NC, N])
        bcs = sb("bcs", [96, TOK], bf16)
        mid = sb("mid", [32, TOK], bf16)
        sel = wx0[0:96, :, :, :].rearrange("p a b c -> p (a b c)").bitcast(bf16).rearrange("p (n m) -> p n m", m=128)
        msum = sb("msum", [128, NC, B])
        sc = sb("sc", [B, E])
        m8 = sb("m8", [128, NT, 8])
        i8 = sb("i8", [128, NT, 8], u32)
        topf = sb("topf", [B, 1])
        top = sb("top", [1, B], i32)
        hf = [area(k * 512, 8, T) for k in range(2)]
        hr = [area(1024 + k * 512, 8, T) for k in range(2)]
        yT = area(2048, NC, TOK)
        QT = area(0, NC, TOK)
        z1 = area(1024, NC, TOK)
        e1 = area(2048, NC, TOK)
        GT = area(3072, NC, TOK)
        sr = area(4096, TOK)
        dn = area(4608, NC, TOK)
        aT = area(5632, NC, TOK)
        y1 = area(6656, NT, D)
        sres = area(0, 4, TOK)
        xc1 = area(2048, 4, TOK)
        xs1 = area(4096, 4, TOK)
        y2 = area(6144, 4, TOK)
        st1 = area(8192, TOK)
        pr1 = area(8704, TOK)
        dec1 = area(9216, TOK)
        da1 = sb("da1", [N, 2])
        sg = [area(k * 512, 512) for k in range(2)]
        hid = [area(1024 + k * 512, 512) for k in range(2)]
        gt = sb("gt", [128, NT, E])
        gtmp = sb("gtmp", [128, NT, E])
        g2 = sb("g2", [128, NT, 3])
        ixf = sb("ixf", [128, NT, 2])

        bank = [ctx.enter_context(nc.psum_tensor(f"bank{i}", [128, 512], f32)) for i in range(8)]

        def C(name, i=0, n=None, p=128):
            a, w = CONSTS[name]
            return cst[0:p, a + i:a + (w if n is None else i + n)]

        def L(name, i=0, n=1, p=128):
            a, _ = COLS[name]
            return col[0:p, a + i:a + i + n]

        def R(name, p=128):
            a, w = ROWS[name]
            return row[0:p, a:a + w]

        ident = C("ident")

        s_in = sem("s_in")
        s_w = sem("s_w")
        s_w2 = sem("s_w2")
        s_ctxT = [sem(f"s_ctxT{k}") for k in range(4)]
        s_sum_act = sem("s_sum_act")
        s_sum_dve = sem("s_sum_dve")
        s_ctxN = [sem(f"s_ctxN{k}") for k in range(2)]
        s_wf0 = [sem(f"s_wf0{k}") for k in range(2)]
        s_wf1 = [sem(f"s_wf1{k}") for k in range(2)]
        s_dve = sem("s_dve")
        s_act = sem("s_act")
        s_pool = sem("s_pool")
        s_var = sem("s_var")
        s_rstd = sem("s_rstd")
        s_xn = sem("s_xn")
        s_xnT_ps = sem("s_xnT_ps")
        s_xnT = sem("s_xnT")
        s_xb = sem("s_xb")
        s_x = sem("s_x")
        s_k_ps, s_v_ps, s_q_ps = sem("s_k_ps"), sem("s_v_ps"), sem("s_q_ps")
        s_kb, s_vbd, s_vz, s_qT = sem("s_kb"), sem("s_vbd"), sem("s_vz"), sem("s_qT")
        s_sc_ps, s_sc = sem("s_sc_ps"), sem("s_sc")
        s_diff, s_exp = sem("s_diff"), sem("s_exp")
        s_PT_ps, s_PT = sem("s_PT_ps"), sem("s_PT")
        s_pv, s_vr, s_vr8, s_vrb = sem("s_pv"), sem("s_vr"), sem("s_vr8"), sem("s_vrb")
        s_o, s_oT_ps, s_oT, s_proj0 = sem("s_o"), sem("s_oT_ps"), sem("s_oT"), sem("s_proj0")

        s_conv0, s_xc0 = sem("s_conv0"), sem("s_xc0")
        s_m0_ps = sem("s_m0_ps")
        s_abs = sem("s_abs")
        s_sp, s_ge = sem("s_sp"), sem("s_ge")
        s_bc_ps, s_bcs, s_sel = sem("s_bc_ps"), sem("s_bcs"), sem("s_sel")
        s_an, s_aneg = sem("s_an"), sem("s_aneg")
        s_dtx = sem("s_dtx")
        s_loop = sem("s_loop")
        s_decay = sem("s_decay")
        s_ssm = sem("s_ssm")
        s_yadd = sem("s_yadd")
        s_B, s_C = sem("s_B"), sem("s_C")
        s_z = sem("s_z")
        s_e = sem("s_e")
        s_kt = sem("s_kt")
        s_kp = sem("s_kp")
        s_kfree = sem("s_kfree")
        s_ktc = sem("s_ktc")
        s_yg, s_proj1 = sem("s_yg"), sem("s_proj1")

        s_ms, s_rt_ps, s_topf, s_topT, s_top = (sem("s_ms"), sem("s_rt_ps"), sem("s_topf"), sem("s_topT"),
                                                sem("s_top"))
        s_h_ps, s_hb, s_hr, s_y_ps, s_y, s_f0T = (sem("s_h_ps"), sem("s_hb"), sem("s_hr"), sem("s_y_ps"),
                                                  sem("s_y"), sem("s_f0T"))

        s_q1_ps, s_z1, s_e1, s_Q1, s_G_ps, s_GT, s_num = (sem("s_q1_ps"), sem("s_z1"), sem("s_e1"), sem("s_Q1"),
                                                          sem("s_G_ps"), sem("s_GT"), sem("s_num"))
        s_aT, s_proj2, s_var1, s_rstd1, s_x3b = (sem("s_aT"), sem("s_proj2"), sem("s_var1"), sem("s_rstd1"),
                                                 sem("s_x3b"))

        s_in_ps, s_res, s_cv1, s_xs1, s_bc1, s_pr1, s_ys, s_y2, s_proj3 = (
            sem("s_in_ps"), sem("s_res"), sem("s_cv1"), sem("s_xs1"), sem("s_bc1"), sem("s_pr1"), sem("s_ys"),
            sem("s_y2"), sem("s_proj3"))
        s_ea1 = sem("s_ea1")

        s_lg, s_gd, s_ge1, s_gate = sem("s_lg"), sem("s_gd"), sem("s_ge1"), sem("s_gate")
        s_h12, s_sg, s_hid, s_hfree, s_o_ps, s_ofree = (
            sem("s_h12"), sem("s_sg"), sem("s_hid"), sem("s_hfree"), sem("s_o_ps"), sem("s_ofree"))
        s_out = sem("s_out")

        block = ctx.enter_context(nc.Block())
        ORDER = [7, 6, 5, 4, 3, 2, 1, 0]
        SLOT = [0, 1, 2, 3, 2, 3, 1, 0]
        slots = [cT[0], cT[1], cT2[0], cT2[1]]
        seen = [sum(1 for j in range(i) if SLOT[j] == SLOT[i]) for i in range(8)]
        IN = 16 * 8
        GROUPS = B * G

        @block.sync
        def _(sp):
            def store():
                sp.wait_ge(s_x, 6)
                sp.dma_start(out, x_tok[:]).then_inc(s_out, 16)
                sp.wait_ge(s_out, 16)

            for dst, src in ((x_tok[:], x), (c0T, first_ctx), (wx0[:], w_x0), (cst[:], consts), (col[:], cols),
                             (row[:], rows.broadcast_to([128, NROWS]))):
                sp.dma_start(dst, src).then_inc(s_in, 16)
            for h in range(2):
                sp.dma_start(mask8[64 * h:64 * h + 64, :, :],
                             mask.rearrange("(t h) s -> h t s", h=2)[h].unsqueeze(0).broadcast_to([64, NT, T])
                             ).then_inc(s_in, 16)
            for i, b in enumerate(ORDER):
                if seen[i]:
                    last = max(j for j in range(i) if SLOT[j] == SLOT[i])
                    sp.wait_ge(s_sum_act, last + 1)
                    sp.wait_ge(s_sum_dve, last + 1)
                sp.dma_start(slots[SLOT[i]], ctx_t[b]).then_inc(s_ctxT[SLOT[i]], 16)
                if i == 3:
                    for dst, src in ((wm0[:], w_m0), (wbc0[:], w_bc0)):
                        sp.dma_start(dst, src).then_inc(s_w, 16)
            sp.dma_start(wx1[:], w_x1).then_inc(s_w, 16)
            for k in range(2):
                if k == 0:
                    sp.wait_ge(s_sum_act, 6)
                    sp.wait_ge(s_sum_dve, 6)
                sp.dma_start(cN[k][:, :, 0:D], ctx_n[k]).then_inc(s_ctxN[k], 16)
            for dst, src in ((wr[:], w_r), (win[:], w_in), (wout[:], w_out), (wbc1[:], w_bc1), (wg1[:], w_g1)):
                sp.dma_start(dst, src).then_inc(s_w2, 16)
            with sp.Fori(1, B // 2) as j:
                for k in range(2):
                    sp.wait_ge(s_kp, 2 * G * j + (G * k - G))
                    sp.dma_start(cT[k], ctx_t[bass.ds(2 * j + k, 1)].rearrange("o p c s -> (o p) c s")
                                 ).then_inc(s_ctxT[k], 16)
                    sp.wait_ge(s_kfree, 2 * G * j + (G * k - G + 2))
                    sp.dma_start(cN[k][:, :, 0:D], ctx_n[bass.ds(2 * j + k, 1)].rearrange("o p k d -> (o p) k d")
                                 ).then_inc(s_ctxN[k], 16)
            sp.wait_ge(s_top, 1)
            with sp.Fori(0, B // 2) as j:
                for k in range(2):
                    sp.wait_ge(s_y, 2 * j + (k + 1))
                    e = sp.value_load(top[0:1, bass.ds(2 * j + k, 1)], min_val=0, max_val=E - 1)
                    sp.dma_start(wf0[k], w0[bass.ds(e, 1)].rearrange("o p n -> (o p) n")).then_inc(s_wf0[k], 16)
            for k in range(2):
                sp.dma_start(wf1[k], w1[k]).then_inc(s_wf1[k], 16)
            with sp.Fori(1, E // 2) as j:
                for k in range(2):
                    sp.wait_ge(s_hfree, 12 * j + (6 * k - 4))
                    sp.dma_start(wf1[k], w1[bass.ds(2 * j + k, 1)].rearrange("o p n -> (o p) n")
                                 ).then_inc(s_wf1[k], 16)
            store()

        @block.gpsimd
        def _(pool):
            gp = nc.gpsimd
            gp.memset(vbd[:], 0.0).then_inc(s_vz, 1)
            pool.wait_ge(s_vz, 1)
            gp.memset(vbd[0:64, :, :, 32:33], 1.0).then_inc(s_pool, 1)
            pool.wait_ge(s_pool, 1)
            gp.memset(vbd[64:128, :, :, 33:34], 1.0).then_inc(s_vz, 1)
            pool.wait_ge(s_vz, 2)
            pool.wait_ge(s_in, IN)
            gp.tensor_tensor(xb[:], x_tok[:], spread(R("bo0"), 1, NT), ALU.add).then_inc(s_xb, 1)
            pool.wait_ge(s_x, 1)
            gp.tensor_copy(sel[:], spread(C("state", p=96), 2, 128)).then_inc(s_sel, 1)
            gp.tensor_tensor(xb[:], x_tok[:], spread(R("boa"), 1, NT), ALU.add).then_inc(s_xb, 1)
            gp.memset(ym[:], 0.0).then_inc(s_yadd, 2)
            for m in range(2):
                for c in range(NC):
                    gp.memset(dec[m][c].rearrange("p (b t) -> p b t", t=T)[:, :, 0:1], 0.0).then_inc(s_yadd, 1)
            pool.wait_ge(s_sum_act, 6)
            pool.wait_ge(s_sum_dve, 6)
            for k in range(2):
                gp.memset(cN[k][:, :, D:D + 1], 1.0).then_inc(s_yadd, 1)
            pool.wait_ge(s_yadd, 8)
            with pool.Fori(0, N // 4) as j:
                for k in range(2):
                    for m in range(2):
                        for c in range(NC):
                            n = 4 * j + (2 * k + m)
                            pool.wait_ge(s_ssm, 6 * n + (12 + 5 + c))
                            pool.wait_ge(s_yadd, 2 * n + (8 + c - 1))
                            gp.tensor_tensor(ym[:, c, :], ym[:, c, :], hc[m][c], ALU.add).then_inc(s_yadd, 1)
            pool.wait_ge(s_xn, 4 * NT)
            gp.tensor_tensor(xb[:], xn[:], spread(R("bo1"), 1, NT), ALU.add).then_inc(s_xb, 1)
            gp.tensor_tensor(x_tok[:], x_tok[:], spread(R("beta"), 1, NT), ALU.add).then_inc(s_x3b, 1)

        @block.scalar
        def _(act):
            sa = nc.scalar
            steps = [0]

            def own(ins):
                steps[0] += 1
                ins.then_inc(s_act, 1)
                act.wait_ge(s_act, steps[0])

            def rstd_of(n, s_ready, s_done):
                act.wait_ge(s_ready, n)
                own(sa.activation(lnv[:], mv[:, :, 1], ACT.Ln, bias=C("eps")))
                sa.activation(rstd[:], lnv[:], ACT.Exp, scale=-0.5).then_inc(s_done, 1)

            def xnT_evac(n):
                act.wait_ge(s_xnT_ps, n)
                sa.copy(xnT[:, 0, :], bank[6][:]).then_inc(s_xnT, 1)

            def sums(i):
                b = ORDER[i]
                act.wait_ge(s_ctxT[SLOT[i]], 16 * (seen[i] + 1))
                v = slots[SLOT[i]][:, 0, 0:S]
                sa.activation(v[:, 0:REST], v[:, 0:REST], ACT.Copy, accum_out=csum[:, 0, b:b + 1]).then_inc(s_sum_act, 1)

            sa.preload_act_table_set("natural_log_exp_and_others")
            act.wait_ge(s_in, IN)
            act.wait_ge(s_vz, 2)
            act.wait_ge(s_v_ps, 1)
            vb = vbd.rearrange("p (t h) n w -> p t h n w", h=2)
            for i in range(2):
                v = bank[2 + i][:].rearrange("p (t n e) -> p t n e", t=2, e=2 * HD)
                for h in range(2):
                    for a in range(2):
                        sa.copy(vb[64 * a:64 * a + 64, 2 * i:2 * i + 2, h, :, HD * a:HD * a + HD],
                                v[64 * h:64 * h + 64, :, :, HD * a:HD * a + HD]).then_inc(s_vbd, 1)
            rstd_of(1, s_var, s_rstd)
            xnT_evac(1)
            sums(0)
            sums(1)
            for r in range(2):
                if r == 1:
                    sums(2)
                for j in range(4):
                    act.wait_ge(s_diff, 4 * r + j + 1)
                    p = P[:, 2 * r:2 * r + 2, j, :]
                    sa.activation(p, p, ACT.Exp).then_inc(s_exp, 1)
            sums(3)
            for r in range(2):
                for j in (0, 2):
                    act.wait_ge(s_PT_ps, 4 * r + j + 1)
                    sa.copy(PT[:, 2 * r:2 * r + 2, j, :],
                            bank[[2, 3, 4, 5][j] if r == 0 else [6, 7, 0, 1][j]][:].rearrange("p (t n) -> p t n", t=2)
                            ).then_inc(s_PT, 1)
            for i in range(4, 8):
                sums(i)
            act.wait_ge(s_vr, 1)
            sa.copy(vr8[0:B, :], bank[0][0:B, 0:D]).then_inc(s_vr8, 1)
            act.wait_ge(s_oT_ps, 1)
            sa.activation(oT[:, 0, :], bank[6][:], ACT.Identity, bias=L("bv0", 0)).then_inc(s_oT, 1)

            sa.activation(aneg[:], L("log_a", 0, 32), ACT.Exp).then_inc(s_an, 1)
            rstd_of(2, s_var, s_rstd)
            xnT_evac(2)
            for c in range(NC):
                act.wait_ge(s_conv0, c + 1)
                sa.activation(xc[:, c, :], tmp[:, c, :], ACT.Silu).then_inc(s_xc0, 1)
            for c in range(NC):
                act.wait_ge(s_m0_ps, c + 1)
                act.wait_ge(s_aneg, 2)
                sa.activation(gate[:, c, :], bank[c][:], ACT.Exp, scale=-1.0, bias=g2[:, c, 0:1]).then_inc(s_ge, 1)
            for c in range(NC):
                act.wait_ge(s_abs, c + 1)
                own(sa.activation(dtx[:, c, :], dt[:, c, :], ACT.Abs))
                own(sa.activation(dtx[:, c, :], dtx[:, c, :], ACT.Exp, scale=-1.0))
                sa.activation(dtx[:, c, :], dtx[:, c, :], ACT.Ln, bias=C("one")).then_inc(s_sp, 1)
            act.wait_ge(s_loop, 1)
            act.wait_ge(s_yadd, 8)
            sa.copy(lnv[:, 0:1], rstd[:, 0:1]).then_inc(s_ktc, 4)
            with act.Fori(0, B // 2) as j:
                for k in range(2):
                    def decay(m):
                        n = 4 * j + (2 * k + m)
                        for c in range(NC):
                            act.wait_ge(s_ssm, 6 * n + (3 + c))
                            d3 = dec[m][c].rearrange("p (b t) -> p b t", t=T)[:, :, 1:T]
                            dt3 = dt[:, c, :].rearrange("p (b t) -> p b t", t=T)[:, :, 1:T]
                            sa.activation(d3, dt3, ACT.Exp, scale=aneg[:, c, bass.ds(n, 1)]).then_inc(s_decay, 1)

                    decay(0)
                    for g in range(G):
                        i = (G * k + g) % 2
                        gg = 2 * G * j + (G * k + g)
                        p, w = (128, 512) if g < G - 1 else (KLAST, D)
                        act.wait_ge(s_z, gg + 3)
                        act.wait_ge(s_kt, gg + 1)
                        sa.activation(ek[i][0:p, 0:w], zk[i][0:p, 0:w], ACT.Exp, bias=C("minus1", p=p)).then_inc(s_e, 1)
                        if g == 2:
                            decay(1)
                    act.wait_ge(s_kfree, 2 * G * j + (G * k + G + 2))
                    for c in range(NC):
                        sa.copy(ktc[:, bass.ds(2 * j + k, 1), c, :].rearrange("p o d -> p (o d)"),
                                bank[2 + 2 * k + c][:, 0:D + 1]).then_inc(s_ktc, 1)
            rstd_of(3, s_var, s_rstd)
            xnT_evac(3)
            with act.Fori(0, B // 2) as j:
                for k in range(2):
                    b = 2 * j + k
                    act.wait_ge(s_hb, b + 1)
                    act.wait_ge(s_y, b + 1)
                    sa.activation(hr[k], hf[k], ACT.Relu).then_inc(s_hr, 1)
            rstd_of(4, s_var, s_rstd)
            xnT_evac(4)
            for c in range(NC):
                act.wait_ge(s_z1, c + 1)
                sa.activation(e1[:, c, :], z1[:, c, :], ACT.Exp, bias=C("minus1")).then_inc(s_e1, 1)
            act.wait_ge(s_G_ps, 1)
            sa.copy(GT[:, 0, :], bank[2][:]).then_inc(s_GT, 1)
            act.wait_ge(s_G_ps, 3)
            sa.copy(sr[0:1, :], bank[4][0:1, :]).then_inc(s_GT, 1)
            rstd_of(1, s_var1, s_rstd1)
            sa.activation(da1[:, 0:1], L("A1", p=N), ACT.Exp).then_inc(s_ea1, 1)
            rstd_of(5, s_var, s_rstd)
            xnT_evac(5)
            for c in range(4):
                act.wait_ge(s_in_ps, 5 + c)
                sa.activation(sres[:, c, :], bank[4 + c][:], ACT.Silu).then_inc(s_res, 1)
            for c in range(4):
                act.wait_ge(s_cv1, c + 1)
                sa.activation(xs1[:, c, :], xc1[:, c, :], ACT.Silu).then_inc(s_xs1, 1)
            rstd_of(6, s_var, s_rstd)
            xnT_evac(6)
            act.wait_ge(s_gd, 1)
            sa.activation(g2[:, :, 1], g2[:, :, 0], ACT.Exp).then_inc(s_ge1, 1)
            sa.preload_act_table(ACT.Silu)
            with act.Fori(0, E // 2) as j:
                for q in range(12):
                    i, w = q % 2, F1C[q % 6]
                    act.wait_ge(s_h12, 12 * j + (q + 1))
                    act.wait_ge(s_hid, 12 * j + (q + 1))
                    sa.activation(sg[i][0:w, :], bank[2 * i][0:w, :], ACT.Silu).then_inc(s_sg, 1)

        @block.vector
        def _(dve):
            v = nc.vector
            steps = [0]

            def mark(ins):
                steps[0] += 1
                ins.then_inc(s_dve, 1)
                return steps[0]

            def own(ins):
                dve.wait_ge(s_dve, mark(ins))

            def moments(src, done):
                for t in range(NT):
                    last = mark(v.bn_stats(stats[:, t, :], src[:, t, :]))
                dve.wait_ge(s_dve, last)
                for t in range(NT):
                    ins = v.bn_aggr(mv[:, t, :], stats[:, t, :])
                    if t == NT - 1:
                        ins.then_inc(done, 1)
                    else:
                        mark(ins)

            def normalise(n):
                moments(x_tok, s_var)
                dve.wait_ge(s_rstd, n)
                dve.wait_ge(s_var, n)
                for t in range(NT):
                    v.tensor_scalar(xn[:, t, :], x_tok[:, t, :], mv[:, t, 0:1], rstd[:, t:t + 1],
                                    ALU.subtract, ALU.mult).then_inc(s_xn, 1)
                dve.wait_ge(s_xnT_ps, n)
                v.tensor_copy(xnT[:, 1, :], bank[7][:]).then_inc(s_xnT, 1)

            def sums(i):
                b = ORDER[i]
                dve.wait_ge(s_ctxT[SLOT[i]], 16 * (seen[i] + 1))
                v.reduce_sum(csum[:, 1, b:b + 1], slots[SLOT[i]][:, 1, 0:REST], AX.X).then_inc(s_sum_dve, 1)

            dve.wait_ge(s_in, IN)
            own(v.tensor_scalar(maskf[:], mask8[:], -FMAX, None, ALU.mult))
            own(v.tensor_tensor(maskf[:], maskf[:], spread(C("causal"), 1, NT), ALU.min))
            for c in range(NC):
                dve.wait_ge(s_k_ps, c + 1)
                for h in range(2):
                    v.tensor_scalar(kb2[:, c, :, h, :], bank[c][:].rearrange("p (b s) -> p b s", s=T),
                                    L("bk0", c), C("parity", h, 1), ALU.add, ALU.mult).then_inc(s_kb, 1)
            normalise(1)
            for c in range(NC):
                dve.wait_ge(s_q_ps, c + 1)
                v.tensor_scalar(qT[:, c, :], bank[c][:], L("bq0", c), HD ** -0.5, ALU.add, ALU.mult).then_inc(s_qT, 1)
            sums(0)
            sums(1)
            for r in range(2):
                banks = [2, 3, 4, 5] if r == 0 else [6, 7, 0, 1]
                ready = []
                for j in range(4):
                    dve.wait_ge(s_sc_ps, 4 * r + j + 1)
                    v.tensor_tensor(
                        P[:, 2 * r:2 * r + 2, j, :].rearrange("p t (g s) -> p t g s", s=T),
                        bank[banks[j]][:].rearrange("p (t g s) -> p t g s", t=2, s=T),
                        spread(maskf[:, 2 * r:2 * r + 2, :], 2, 4), ALU.add).then_inc(s_sc, 1)
                for j in range(4):
                    dve.wait_ge(s_sc, 4 * r + j + 1)
                    ready.append(mark(v.tensor_reduce(
                        mx[:, 2 * r:2 * r + 2, j, :],
                        P[:, 2 * r:2 * r + 2, j, :].rearrange("p t (g s) -> p t g s", s=T), AX.X, ALU.max)))
                for j in range(4):
                    dve.wait_ge(s_dve, ready[j])
                    p4 = P[:, 2 * r:2 * r + 2, j, :].rearrange("p t (g s) -> p t g s", s=T)
                    v.tensor_tensor(p4, p4, spread(mx[:, 2 * r:2 * r + 2, j, :], 3, T), ALU.subtract).then_inc(s_diff, 1)
                if r == 0:
                    sums(2)
            own(v.tensor_scalar(rest[:], mx[:], -FMAX, None, ALU.is_le))
            sums(3)
            for r in range(2):
                for j in (1, 3):
                    dve.wait_ge(s_PT_ps, 4 * r + j + 1)
                    v.tensor_copy(PT[:, 2 * r:2 * r + 2, j, :],
                                  bank[[2, 3, 4, 5][j] if r == 0 else [6, 7, 0, 1][j]][:].rearrange("p (t n) -> p t n", t=2)
                                  ).then_inc(s_PT, 1)
            for i in range(4, 8):
                sums(i)
            dve.wait_ge(s_pv, NT)
            def heads(ap):
                return ap.rearrange("p j (c a) -> p c j a", a=2)
            for t in range(NT):
                d4 = den[:, t, :].rearrange("p (c j a) -> p c j a", c=2, a=2)
                last = mark(v.scalar_tensor_tensor(
                    den[:, t, 0:8].rearrange("p (j a) -> p j a", a=2), rest[:, t, :, 0:2], float(REST),
                    bank[2 + t][:, 0:272].rearrange("p (n w) -> p n w", w=34)[:, 0:4, 32:34], ALU.mult, ALU.add))
                last = mark(v.scalar_tensor_tensor(
                    den[:, t, 8:16].rearrange("p (j a) -> p j a", a=2), rest[:, t, :, 2:4], float(REST),
                    bank[2 + t][:, 0:272].rearrange("p (n w) -> p n w", w=34)[:, 4:8, 32:34], ALU.mult, ALU.add))
            dve.wait_ge(s_dve, last)
            own(v.reciprocal(den[:], den[:]))
            dve.wait_ge(s_vrb, 1)
            for t in range(NT):
                for c in range(NC):
                    last = mark(v.tensor_tensor(
                        vro[:, t, 128 * c:128 * c + 128].rearrange("p (j a e) -> p j a e", j=4, a=2),
                        bank[t // 2][:, 256 * (t % 2) + 128 * c:256 * (t % 2) + 128 * c + 128].rearrange(
                            "p (j a e) -> p j a e", j=4, a=2),
                        spread(rest[:, t, :, 2 * c:2 * c + 2], 3, HD), ALU.mult))
            dve.wait_ge(s_dve, last)
            for t in range(NT):
                last = mark(v.tensor_tensor(
                    vro[:, t, :].rearrange("p (n e) -> p n e", e=32), vro[:, t, :].rearrange("p (n e) -> p n e", e=32),
                    bank[2 + t][:, 0:272].rearrange("p (n w) -> p n w", w=34)[:, :, 0:32], ALU.add))
            dve.wait_ge(s_dve, last)
            for t in range(NT):
                v.tensor_tensor(oa[:, t, :].rearrange("p (h e) -> p h e", e=HD),
                                vro[:, t, :].rearrange("p (h e) -> p h e", e=HD),
                                spread(den[:, t, :], 2, HD), ALU.mult).then_inc(s_o, 1)
            dve.wait_ge(s_oT_ps, 1)
            v.tensor_scalar(oT[:, 1, :], bank[7][:], L("bv0", 1), None, ALU.add).then_inc(s_oT, 1)
            dve.wait_ge(s_xb, 1)
            for t in range(NT):
                dve.wait_ge(s_proj0, t + 1)
                ins = v.tensor_tensor(x_tok[:, t, :], xb[:, t, :], bank[t][:, 0:D], ALU.add)
                if t < NT - 1:
                    mark(ins)
            ins.then_inc(s_x, 1)
            dve.wait_ge(s_x, 1)
            dve.wait_ge(s_dve, steps[0])

            dve.wait_ge(s_an, 1)
            v.tensor_scalar(aneg[:], aneg[:], -1.0, None, ALU.mult).then_inc(s_aneg, 1)
            v.tensor_scalar(g2[:, 0:NC, 0:1], L("bg", 0, 2).unsqueeze(2), -1.0, None, ALU.mult).then_inc(s_aneg, 1)
            mark(v.tensor_scalar(R("bk1"), R("bk1"), 1.0, None, ALU.add))
            normalise(2)
            dve.wait_ge(s_xnT, 4)
            x3 = [xnT[:, c, :].rearrange("p (b t) -> p b t", t=T) for c in range(NC)]
            t3 = [tmp[:, c, :].rearrange("p (b t) -> p b t", t=T) for c in range(NC)]
            last = [None] * NC
            for c in range(NC):
                last[c] = mark(v.tensor_scalar(t3[c], x3[c], L("conv0", 4 * c + 3), L("conv0b", c), ALU.mult, ALU.add))
            for s in range(1, 4):
                for c in range(NC):
                    dve.wait_ge(s_dve, last[c])
                    ins = v.scalar_tensor_tensor(t3[c][:, :, s:T], x3[c][:, :, 0:T - s], L("conv0", 4 * c + 3 - s),
                                                 t3[c][:, :, s:T], ALU.mult, ALU.add)
                    if s < 3:
                        last[c] = mark(ins)
                    else:
                        ins.then_inc(s_conv0, 1)
            for c in range(NC):
                dve.wait_ge(s_ge, c + 1)
                own(v.tensor_scalar(gate[:, c, :], gate[:, c, :], 1.0, None, ALU.add))
                mark(v.reciprocal(gate[:, c, :], gate[:, c, :]))
            for c in range(NC):
                dve.wait_ge(s_m0_ps, c + 3)
                v.tensor_scalar(dt[:, c, :], bank[2 + c][:], L("bd", c), None, ALU.add).then_inc(s_abs, 1)
            dve.wait_ge(s_bc_ps, 1)
            own(v.tensor_copy(bc[0:32, :], bank[4][0:32, :]))
            own(v.tensor_copy(bcs[0:32, :], bc[0:32, :]))
            own(v.tensor_tensor(r1[0:32, :], bc[0:32, :], bcs[0:32, :], ALU.subtract))
            own(v.tensor_copy(mid[:], r1[0:32, :]))
            v.tensor_copy(bcs[32:64, :], mid[:]).then_inc(s_bcs, 1)
            v.tensor_tensor(bcs[64:96, :], r1[0:32, :], mid[:], ALU.subtract).then_inc(s_bcs, 1)
            for c in range(NC):
                dve.wait_ge(s_sp, c + 1)
                mark(v.scalar_tensor_tensor(dt[:, c, :], dt[:, c, :], 0.0, dtx[:, c, :], ALU.max, ALU.add))
            dve.wait_ge(s_dve, steps[0])
            v.tensor_tensor(dtx[:, 0, :], dt[:, 0, :], xc[:, 0, :], ALU.mult).then_inc(s_ssm, 6)
            v.tensor_tensor(dtx[:, 1, :], dt[:, 1, :], xc[:, 1, :], ALU.mult).then_inc(s_ssm, 6)
            dve.wait_ge(s_ssm, 12)
            v.memset(ek[0], 0.0).then_inc(s_z, 2)
            v.memset(ek[1], 0.0).then_inc(s_kt, 2)
            dve.wait_ge(s_z, 2)
            dve.wait_ge(s_kt, 2)
            v.memset(stats[:, 0, 0:1], 0.0).then_inc(s_loop, 1)
            with dve.Fori(0, B // 2) as j:
                for k in range(2):
                    def ssm(q):
                        m, op, c = q // 6, (q % 6) // 2, q % 2
                        n = 4 * j + (2 * k + m)
                        if op == 0:
                            dve.wait_ge(s_B, n + 1)
                            v.tensor_tensor(inp[c], dtx[:, c, :], bank[6][:], ALU.mult).then_inc(s_ssm, 1)
                        elif op == 1:
                            dve.wait_ge(s_decay, 2 * n + (c + 1))
                            dve.wait_ge(s_ssm, 6 * n + (12 + 1 + c))
                            v.tensor_tensor_scan(hst[c], dec[m][c], inp[c], 0.0, ALU.mult, ALU.add).then_inc(s_ssm, 1)
                        else:
                            dve.wait_ge(s_C, n + 1)
                            dve.wait_ge(s_ssm, 6 * n + (12 + 3 + c))
                            dve.wait_ge(s_yadd, 2 * n + (8 - 3 + c))
                            v.tensor_tensor(hc[m][c], hst[c], bank[7][:], ALU.mult).then_inc(s_ssm, 1)

                    for g in range(G):
                        i = (G * k + g) % 2
                        gg = 2 * G * j + (G * k + g)
                        p, w = (128, 512) if g < G - 1 else (KLAST, D)
                        reps = w // D
                        dve.wait_ge(s_kp, gg + 1)
                        v.tensor_tensor(zk[i][0:p, 0:w].rearrange("p (r d) -> p r d", r=reps),
                                        bank[i][0:p, 0:w].rearrange("p (r d) -> p r d", r=reps),
                                        spread(R("bk1", p=p), 1, reps), ALU.add).then_inc(s_z, 1)
                        if g < 6:
                            ssm(2 * g)
                        dve.wait_ge(s_e, gg + 1)
                        dve.wait_ge(s_kfree, gg + 1)
                        dve.wait_ge(s_z, gg + 3)
                        v.scalar_tensor_tensor(kk[i][0:p, 0:w], ek[i][0:p, 0:w], 1.0, zk[i][0:p, 0:w],
                                               ALU.min, ALU.max).then_inc(s_kt, 1)
                        if g < 6:
                            ssm(2 * g + 1)
            dve.wait_ge(s_yadd, 8 + 2 * N)
            for c in range(NC):
                v.tensor_tensor(ym[:, c, :], ym[:, c, :], gate[:, c, :], ALU.mult).then_inc(s_yg, 1)
            dve.wait_ge(s_xb, 2)
            for t in range(NT):
                dve.wait_ge(s_proj1, t + 1)
                ins = v.tensor_tensor(x_tok[:, t, :], xb[:, t, :], bank[t][:, 0:D], ALU.add)
                if t < NT - 1:
                    mark(ins)
            ins.then_inc(s_x, 1)
            dve.wait_ge(s_x, 2)
            dve.wait_ge(s_dve, steps[0])

            normalise(3)
            dve.wait_ge(s_xnT, 6)
            for c in range(NC):
                v.reduce_sum(msum[:, c, :], xnT[:, c, :].rearrange("p (b t) -> p b t", t=T), AX.X).then_inc(s_ms, 1)
            dve.wait_ge(s_rt_ps, 1)
            own(v.scalar_tensor_tensor(sc[:], bank[0][0:B, 0:E], 1.0 / T, R("br", p=B), ALU.mult, ALU.add))
            own(v.max(m8[0:B, 0, :], sc[:]))
            own(v.max_index(i8[0:B, 0, :], m8[0:B, 0, :], sc[:]))
            v.tensor_copy(topf[:], i8[0:B, 0, 0:1]).then_inc(s_topf, 1)
            dve.wait_ge(s_topT, 1)
            v.tensor_copy(top[:], bank[1][0:1, 0:B]).then_inc(s_top, 1)
            v.memset(yT[:, 0, 0:1], 0.0).then_inc(s_y, 2)
            dve.wait_ge(s_y, 2)
            with dve.Fori(0, B // 2) as j:
                for k in range(2):
                    b = 2 * j + k
                    dve.wait_ge(s_h_ps, b + 1)
                    dve.wait_ge(s_wf0[k], 16 * j + 16)
                    v.tensor_tensor(hf[k], bank[2 + k][:].rearrange("p (f t) -> p f t", t=T),
                                    spread(wf0[k][:, W0N - 10:W0N - 2], 2, T), ALU.add).then_inc(s_hb, 1)
                    dve.wait_ge(s_y_ps, b + 1)
                    v.tensor_tensor(yT[:, :, bass.ds(b * T, T)], bank[4 + k][:, 0:128].rearrange("p (c t) -> p c t", t=T),
                                    spread(wf0[k][:, W0N - 2:W0N], 2, T), ALU.add).then_inc(s_y, 1)
            for t in range(NT):
                dve.wait_ge(s_f0T, t + 1)
                ins = v.tensor_tensor(x_tok[:, t, :], x_tok[:, t, :], bank[t][:, 0:D], ALU.add)
                if t < NT - 1:
                    mark(ins)
            ins.then_inc(s_x, 1)
            dve.wait_ge(s_x, 3)
            dve.wait_ge(s_dve, steps[0])

            normalise(4)
            for c in range(NC):
                dve.wait_ge(s_q1_ps, c + 1)
                v.tensor_scalar(z1[:, c, :], bank[c][:], L("bq1", c), 1.0, ALU.add, ALU.add).then_inc(s_z1, 1)
            dve.wait_ge(s_z1, 2)
            for c in range(NC):
                dve.wait_ge(s_e1, c + 1)
                v.scalar_tensor_tensor(QT[:, c, :], e1[:, c, :], 1.0, z1[:, c, :], ALU.min, ALU.max).then_inc(s_Q1, 1)
            dve.wait_ge(s_Q1, 2)
            for c in range(NC):
                last = mark(v.tensor_tensor(dn[:, c, :].rearrange("p (b t) -> p b t", t=T),
                                            QT[:, c, :].rearrange("p (b t) -> p b t", t=T),
                                            spread(ktc[:, :, c, D], 2, T), ALU.mult))
            dve.wait_ge(s_dve, last)
            own(v.tensor_scalar(dn[:], dn[:], 1e-6, None, ALU.add))
            mark(v.reciprocal(dn[:], dn[:]))
            dve.wait_ge(s_G_ps, 2)
            v.tensor_copy(GT[:, 1, :], bank[3][:]).then_inc(s_GT, 1)
            dve.wait_ge(s_dve, steps[0])
            for c in range(NC):
                dve.wait_ge(s_num, c + 1)
                v.tensor_tensor(aT[:, c, :], dn[:, c, :], bank[c][:], ALU.mult).then_inc(s_aT, 1)
            dve.wait_ge(s_xb, 3)
            for t in range(NT):
                dve.wait_ge(s_proj2, t + 1)
                last = mark(v.tensor_tensor(y1[:, t, :], xb[:, t, :], bank[2 + t][:, 0:D], ALU.add))
            dve.wait_ge(s_dve, last)
            moments(y1, s_var1)
            dve.wait_ge(s_rstd1, 1)
            dve.wait_ge(s_var1, 1)
            for t in range(NT):
                last = mark(v.tensor_scalar(y1[:, t, :], y1[:, t, :], mv[:, t, 0:1], rstd[:, t:t + 1],
                                            ALU.subtract, ALU.mult))
            dve.wait_ge(s_dve, last)
            own(v.tensor_tensor(y1[:], y1[:], spread(R("gamma"), 1, NT), ALU.mult))
            dve.wait_ge(s_x3b, 1)
            v.tensor_tensor(x_tok[:], x_tok[:], y1[:], ALU.add).then_inc(s_x, 1)
            dve.wait_ge(s_x, 4)

            dve.wait_ge(s_ea1, 1)
            own(v.tensor_scalar(da1[:, 0:1], da1[:, 0:1], 1.0, None, ALU.add))
            own(v.reciprocal(da1[:, 1:2], da1[:, 0:1]))
            own(v.tensor_copy(dec1[0:N, :], da1[:, 1:2].broadcast_to([N, TOK])))
            mark(v.memset(dec1[0:N, :].rearrange("p (b t) -> p b t", t=T)[:, :, 0:1], 0.0))
            normalise(5)
            for c in range(4):
                dve.wait_ge(s_in_ps, c + 1)
                xm = bank[c][:].rearrange("p (b t) -> p b t", t=T)
                xo = xc1[:, c, :].rearrange("p (b t) -> p b t", t=T)
                own(v.tensor_scalar(xo, xm, L("conv1", 3 * c + 1), L("conv1b", c), ALU.mult, ALU.add))
                own(v.scalar_tensor_tensor(xo[:, :, 1:T], xm[:, :, 0:T - 1], L("conv1", 3 * c), xo[:, :, 1:T],
                                           ALU.mult, ALU.add))
                v.scalar_tensor_tensor(xo[:, :, 0:T - 1], xm[:, :, 1:T], L("conv1", 3 * c + 2), xo[:, :, 0:T - 1],
                                       ALU.mult, ALU.add).then_inc(s_cv1, 1)
            dve.wait_ge(s_bc1, 1)
            own(v.tensor_tensor_scan(st1[0:N, :], dec1[0:N, :], bank[4][0:N, :], 0.0, ALU.mult, ALU.add))
            v.tensor_tensor(pr1[0:N, :], st1[0:N, :], bank[5][0:N, :], ALU.mult).then_inc(s_pr1, 1)
            dve.wait_ge(s_ys, 1)
            for c in range(4):
                last = mark(v.scalar_tensor_tensor(y2[:, c, :], xs1[:, c, :], L("D1", c), bank[6][:], ALU.mult, ALU.add))
            dve.wait_ge(s_dve, last)
            for c in range(4):
                v.tensor_tensor(y2[:, c, :], y2[:, c, :], sres[:, c, :], ALU.mult).then_inc(s_y2, 1)
            for t in range(NT):
                dve.wait_ge(s_proj3, t + 1)
                ins = v.tensor_tensor(x_tok[:, t, :], x_tok[:, t, :], bank[t][:, 0:D], ALU.add)
                if t < NT - 1:
                    mark(ins)
            ins.then_inc(s_x, 1)
            dve.wait_ge(s_x, 5)
            dve.wait_ge(s_dve, steps[0])

            v.memset(hid[0], 0.0).then_inc(s_hid, 2)
            dve.wait_ge(s_hid, 2)
            normalise(6)
            dve.wait_ge(s_lg, 1)
            v.tensor_copy(gtmp[:], bank[4][:, 0:NT * E].rearrange("p (t e) -> p t e", e=E)).then_inc(s_ofree, NT)
            dve.wait_ge(s_ofree, NT)
            for t in range(NT):
                last = mark(v.max(m8[:, t, :], gtmp[:, t, :]))
            dve.wait_ge(s_dve, last)
            v.tensor_tensor(g2[:, :, 0], m8[:, :, 1], m8[:, :, 0], ALU.subtract).then_inc(s_gd, 1)
            for t in range(NT):
                last = mark(v.max_index(i8[:, t, :], m8[:, t, :], gtmp[:, t, :]))
            dve.wait_ge(s_dve, last)
            own(v.tensor_copy(ixf[:], i8[:, :, 0:2]))
            dve.wait_ge(s_ge1, 1)
            own(v.tensor_scalar(g2[:, :, 2], g2[:, :, 1], 1.0, None, ALU.add))
            own(v.reciprocal(g2[:, :, 2], g2[:, :, 2]))
            own(v.tensor_tensor(g2[:, :, 1], g2[:, :, 1], g2[:, :, 2], ALU.mult))
            for t in range(NT):
                last = mark(v.tensor_scalar(gt[:, t, :], C("iota"), ixf[:, t, 0:1], g2[:, t, 2:3], ALU.is_equal, ALU.mult))
                last = mark(v.tensor_scalar(gtmp[:, t, :], C("iota"), ixf[:, t, 1:2], g2[:, t, 1:2], ALU.is_equal, ALU.mult))
            dve.wait_ge(s_dve, last)
            v.tensor_tensor(gt[:], gt[:], gtmp[:], ALU.add).then_inc(s_gate, 1)
            dve.wait_ge(s_gate, 1)
            with dve.Fori(0, E // 2) as j:
                def gather(k):
                    for t in range(NT):
                        if t < NT - 1:
                            dve.wait_ge(s_o_ps, 6 * j + (3 * k + t + 1))
                        else:
                            dve.wait_ge(s_hfree, 12 * j + (6 * k + 8))
                        dve.wait_ge(s_ofree, 8 * j + (4 * k + t + 1))
                        v.scalar_tensor_tensor(x_tok[:, t, :], bank[4 + t][:, 0:D], gt[:, t, bass.ds(2 * j + k, 1)],
                                               x_tok[:, t, :], ALU.mult, ALU.add).then_inc(s_ofree, 1)

                for q in range(12):
                    i, w = q % 2, F1C[q % 6]
                    dve.wait_ge(s_sg, 12 * j + (q + 1))
                    dve.wait_ge(s_hfree, 12 * j + (q + 1))
                    v.tensor_tensor(hid[i][0:w, :], sg[i][0:w, :], bank[2 * i + 1][0:w, :], ALU.mult).then_inc(s_hid, 1)
                    if q == 6:
                        gather(0)
                gather(1)
            dve.wait_ge(s_ofree, 4 + 4 * E)
            v.memset(stats[:, 0, 0:1], 0.0).then_inc(s_x, 1)

        @block.tensor
        def _(pe):
            te = nc.tensor
            mm = te.matmul

            def transposes(n):
                for t in range(NT):
                    pe.wait_ge(s_xn, NT * (n - 1) + t + 1)
                    for c in range(NC):
                        last = te.transpose(bank[6 + c][:, 128 * t:128 * t + 128], xn[:, t, 128 * c:128 * c + 128], ident)
                last.then_inc(s_xnT_ps, 1)
                pe.wait_ge(s_xnT, 2 * n)

            def project(dst, w, moving, m=0):
                for d in range(NC):
                    last = mm(dst, w[:, d, m:m + 128], moving[:, d, :], start=(d == 0), stop=(d == NC - 1))
                return last

            def token_major(dst, src, w, t, n=NC, at=0):
                for d in range(n):
                    last = mm(dst[:, at:at + D], src[:, d, 128 * t:128 * t + 128], w[:, d, :], start=(d == 0), stop=(d == n - 1))
                return last

            pe.wait_ge(s_in, IN)
            for c in range(NC):
                project(bank[c][:], wx0[:, 1], c0T, 128 * c).then_inc(s_k_ps, 1)
            for t in range(NT):
                last = token_major(bank[2 + t // 2], c0T, wx0[:, 2], t, at=D * (t % 2))
            last.then_inc(s_v_ps, 1)
            transposes(1)
            pe.wait_ge(s_kb, 4)
            for c in range(NC):
                project(bank[c][:], wx0[:, 0], xnT, 128 * c).then_inc(s_q_ps, 1)
            pe.wait_ge(s_qT, 2)
            pe.wait_ge(s_vbd, 8)
            for r in range(2):
                banks = [2, 3, 4, 5] if r == 0 else [6, 7, 0, 1]
                for j in range(4):
                    for tt in range(2):
                        for h in range(2):
                            b = 4 * r + 2 * tt + h
                            for c in range(NC):
                                at = 256 * tt + 128 * c
                                last = mm(bank[banks[j]][64 * h:64 * h + 64, at:at + 128],
                                          qT[32 * j:32 * j + 32, c, T * b:T * b + T],
                                          kb2[32 * j:32 * j + 32, c, b, :, :], start=True, stop=True)
                    last.then_inc(s_sc_ps, 1)
            for r in range(2):
                banks = [2, 3, 4, 5] if r == 0 else [6, 7, 0, 1]
                for j in range(4):
                    pe.wait_ge(s_exp, 4 * r + j + 1)
                    for tt in range(2):
                        for c in range(NC):
                            at = 256 * tt + 128 * c
                            last = te.transpose(bank[banks[j]][:, at:at + 128], P[:, 2 * r + tt, j, 128 * c:128 * c + 128],
                                                ident)
                    last.then_inc(s_PT_ps, 1)
            pe.wait_ge(s_PT, 8)
            for t in range(NT):
                for h in range(2):
                    for c in range(NC):
                        for j in range(4):
                            n = 4 * c + j
                            last = mm(bank[2 + t][64 * h:64 * h + 64, 34 * n:34 * n + 34],
                                      PT[:, t, j, 128 * c + 64 * h:128 * c + 64 * h + 64],
                                      vbd[:, 2 * t + h, n, :], start=True, stop=True)
                last.then_inc(s_pv, 1)
            pe.wait_ge(s_sum_act, 8)
            pe.wait_ge(s_sum_dve, 8)
            for d in range(NC):
                last = mm(bank[0][0:B, 0:D], csum[:, d, :], wx0[:, 2, d, :], start=(d == 0), stop=(d == 1))
            last.then_inc(s_vr, 1)
            pe.wait_ge(s_vr8, 1)
            for t in range(NT):
                last = mm(bank[t // 2][:, D * (t % 2):D * (t % 2) + D], C("batch", 128 * t, 128, p=B), vr8[0:B, :],
                          start=True, stop=True)
            last.then_inc(s_vrb, 1)
            for t in range(NT):
                pe.wait_ge(s_o, t + 1)
                for c in range(NC):
                    last = te.transpose(bank[6 + c][:, 128 * t:128 * t + 128], oa[:, t, 128 * c:128 * c + 128], ident)
            last.then_inc(s_oT_ps, 1)
            pe.wait_ge(s_oT, 2)
            for t in range(NT):
                token_major(bank[t], oT, wx0[:, 3], t).then_inc(s_proj0, 1)

            transposes(2)
            pe.wait_ge(s_w, 16 * 3)
            pe.wait_ge(s_x, 1)
            for c in range(NC):
                project(bank[c][:], wm0[:, 1], xnT, 128 * c).then_inc(s_m0_ps, 1)
            pe.wait_ge(s_xc0, 2)
            for c in range(NC):
                project(bank[2 + c][:], wm0[:, 0], xc, 128 * c).then_inc(s_m0_ps, 1)
            for d in range(NC):
                last = mm(bank[4][0:2 * N, :], wbc0[:, d, :], xc[:, d, :], start=(d == 0), stop=(d == 1))
            last.then_inc(s_bc_ps, 1)
            pe.wait_ge(s_bcs, 2)
            pe.wait_ge(s_sel, 1)
            pe.wait_ge(s_loop, 1)
            pe.wait_ge(s_yadd, 8)
            pe.sem_inc(s_kfree, 2)
            with pe.Fori(0, B // 2) as j:
                for k in range(2):
                    def broadcast_b(m):
                        n = 4 * j + (2 * k + m)
                        pe.wait_ge(s_ssm, 6 * n + 8)
                        mm(bank[6][:], sel[:, bass.ds(n, 1), :].rearrange("p o m -> p (o m)"), bcs[:],
                           start=True, stop=True).then_inc(s_B, 1)

                    def broadcast_c(m):
                        n = 4 * j + (2 * k + m)
                        pe.wait_ge(s_ssm, 6 * n + 12)
                        mm(bank[7][:], sel[:, bass.ds(n + N, 1), :].rearrange("p o m -> p (o m)"), bcs[:],
                           start=True, stop=True).then_inc(s_C, 1)

                    pe.wait_ge(s_ctxT[k], 16 * j + 32)
                    for g in range(G + 1):
                        if g == 0:
                            broadcast_b(0)
                        if g < G:
                            i = (G * k + g) % 2
                            gg = 2 * G * j + (G * k + g)
                            pe.wait_ge(s_z, gg + 1)
                            for a in range(2 if g < G - 1 else 1):
                                kt = 2 * g + a
                                p = 128 if kt < KT - 1 else KLAST
                                for d in range(NC):
                                    last = mm(bank[i][0:p, D * a:D * a + D], cT[k][:, d, 128 * kt:128 * kt + p],
                                              wx1[:, 1, d, :], start=(d == 0), stop=(d == 1))
                            last.then_inc(s_kp, 1)
                        if g:
                            gg = 2 * G * j + (G * k + g - 1)
                            i = (G * k + g - 1) % 2
                            if g == 1:
                                pe.wait_ge(s_ctxN[k], 16 * j + 16)
                                pe.wait_ge(s_ktc, 4 * j + (2 * k + 2))
                            pe.wait_ge(s_kt, gg + 3)
                            for a in range(2 if g < G else 1):
                                kt = 2 * (g - 1) + a
                                p = 128 if kt < KT - 1 else KLAST
                                for c in range(NC):
                                    last = mm(bank[2 + 2 * k + c][:, 0:D + 1], kk[i][0:p, D * a + 128 * c:D * a + 128 * c + 128],
                                              cN[k][0:p, kt, :], start=(kt == 0), stop=(kt == KT - 1))
                            last.then_inc(s_kfree, 1)
                        if g == 1:
                            broadcast_c(0)
                        if g == 2:
                            broadcast_b(1)
                        if g == 4:
                            broadcast_c(1)
            pe.wait_ge(s_yg, 2)
            for t in range(NT):
                token_major(bank[t], ym, wm0[:, 2], t).then_inc(s_proj1, 1)

            transposes(3)
            pe.wait_ge(s_ms, 2)
            pe.wait_ge(s_w2, 16 * 5)
            pe.wait_ge(s_x, 2)
            for d in range(NC):
                last = mm(bank[0][0:B, 0:E], msum[:, d, :], wr[:, d, :], start=(d == 0), stop=(d == 1))
            last.then_inc(s_rt_ps, 1)
            pe.wait_ge(s_topf, 1)
            te.transpose(bank[1][0:1, 0:B], topf[:], C("ident", 0, B, p=B)).then_inc(s_topT, 1)
            with pe.Fori(0, B // 2) as j:
                for k in range(2):
                    b = 2 * j + k
                    fw1 = wf0[k][:, 0:NC * F0].rearrange("p (c f) -> p c f", c=NC)
                    fw2 = wf0[k][:, NC * F0:NC * F0 + 8 * D].rearrange("p (f d) -> p f d", f=8)
                    pe.wait_ge(s_wf0[k], 16 * j + 16)
                    pe.wait_ge(s_y, b + 1)
                    for f in range(8):
                        for d in range(NC):
                            last = mm(bank[2 + k][:, T * f:T * f + T], fw1[:, d, 128 * f:128 * f + 128],
                                      xnT[:, d, bass.ds(b * T, T)], start=(d == 0), stop=(d == 1))
                    last.then_inc(s_h_ps, 1)
                    pe.wait_ge(s_hr, b + 1)
                    for c in range(NC):
                        for f in range(8):
                            last = mm(bank[4 + k][:, T * c:T * c + T], fw2[:, f, 128 * c:128 * c + 128], hr[k][:, f, :],
                                      start=(f == 0), stop=(f == 7))
                    last.then_inc(s_y_ps, 1)
            pe.wait_ge(s_y, 2 + B)
            for t in range(NT):
                for c in range(NC):
                    last = te.transpose(bank[t][:, 128 * c:128 * c + 128], yT[:, c, 128 * t:128 * t + 128], ident)
                last.then_inc(s_f0T, 1)

            transposes(4)
            pe.wait_ge(s_x, 3)
            for c in range(NC):
                project(bank[c][:], wx1[:, 0], xnT, 128 * c).then_inc(s_q1_ps, 1)
            pe.wait_ge(s_Q1, 2)
            pe.wait_ge(s_ktc, 4 + 2 * B)
            for m in range(NC + 1):
                for b in range(B):
                    for e in range(NC):
                        w = 128 if m < NC else 1
                        last = mm(bank[2 + m][0:w, T * b:T * b + T], ktc[:, b, e, 128 * m:128 * m + w],
                                  QT[:, e, T * b:T * b + T], start=(e == 0), stop=(e == 1))
                last.then_inc(s_G_ps, 1)
            pe.wait_ge(s_GT, 3)
            for c in range(NC):
                for d in range(NC):
                    mm(bank[c][:], wx1[:, 2, d, 128 * c:128 * c + 128], GT[:, d, :], start=(d == 0), stop=False)
                mm(bank[c][:], R("bv1", p=1)[:, 128 * c:128 * c + 128], sr[0:1, :], start=False, stop=True).then_inc(s_num, 1)
            pe.wait_ge(s_aT, 2)
            for t in range(NT):
                token_major(bank[2 + t], aT, wx1[:, 3], t).then_inc(s_proj2, 1)

            transposes(5)
            for m in range(8):
                project(bank[m][:], win, xnT, 128 * m).then_inc(s_in_ps, 1)
            pe.wait_ge(s_xs1, 4)
            pe.wait_ge(s_res, 4)
            for h in range(2):
                for i in range(4):
                    last = mm(bank[4 + h][0:N, :], wbc1[:, i, N * h:N * h + N], xs1[:, i, :], start=(i == 0), stop=(i == 3))
            last.then_inc(s_bc1, 1)
            pe.wait_ge(s_pr1, 1)
            mm(bank[6][:], C("ones", p=N), pr1[0:N, :], start=True, stop=True).then_inc(s_ys, 1)
            pe.wait_ge(s_y2, 4)
            for t in range(NT):
                token_major(bank[t], y2, wout, t, 4).then_inc(s_proj3, 1)

            transposes(6)
            for t in range(NT):
                for d in range(NC):
                    last = mm(bank[4][:, E * t:E * t + E], xnT[:, d, 128 * t:128 * t + 128], wg1[:, d, :],
                              start=(d == 0), stop=(d == 1))
            last.then_inc(s_lg, 1)
            pe.sem_inc(s_hfree, 2)
            with pe.Fori(0, E // 2) as j:
                def hidden(q):
                    i, k, f = q % 2, q // 6, q % 6
                    w = F1C[f]
                    if f == 0:
                        pe.wait_ge(s_wf1[k], 16 * j + 16)
                    pe.wait_ge(s_hid, 12 * j + (q + 1))
                    for h in range(2):
                        for d in range(NC):
                            at = (NC * h + d) * F1 + 128 * f
                            last = mm(bank[2 * i + h][0:w, :], wf1[k][:, at:at + w], xnT[:, d, :],
                                      start=(d == 0), stop=(d == 1))
                    last.then_inc(s_h12, 1)

                def output(q):
                    i, k, f = q % 2, q // 6, q % 6
                    w = F1C[f]
                    pe.wait_ge(s_hid, 12 * j + (q + 3))
                    at = 2 * NC * F1 + f * D
                    for t in range(NT):
                        if f == 0:
                            pe.wait_ge(s_ofree, 8 * j + (4 * k + t + 1))
                        last = mm(bank[4 + t][:, 0:D], hid[i][0:w, 128 * t:128 * t + 128], wf1[k][0:w, at:at + D],
                                  start=(f == 0), stop=(f == 5))
                        if f == 5 and t < NT - 1:
                            last.then_inc(s_o_ps, 1)
                    last.then_inc(s_hfree, 1)

                hidden(0)
                for q in range(12):
                    if q < 11:
                        hidden(q + 1)
                    output(q)


_OUT = ((128, NT, D), "float32")


def kernel(**inputs):
    import ml_dtypes
    import numpy as np
    import concourse.bacc as bacc
    from concourse import mybir
    from concourse.bass_utils import run_bass_kernel_spmd

    a = {k: np.asarray(v) for k, v in inputs.items()}

    def feature_rows(w, n):
        return w.reshape(n, 128, -1).transpose(1, 0, 2)

    def columns(v):
        return v.reshape(-1, 128).T

    ctx = np.concatenate([a["ctx_1024"][:, T:], a["ctx_1024"][:, :T]], axis=1)
    ctx_t = ctx.transpose(0, 2, 1).reshape(B, NC, 128, S).transpose(0, 2, 1, 3)
    ctx_n = np.zeros((B, KT * 128, D), np.float32)
    ctx_n[:, :S] = ctx
    ctx_n = ctx_n.reshape(B, KT, 128, D).transpose(0, 2, 1, 3)
    first = a["ctx_1024"][:, :T].reshape(TOK, D).T

    a1 = np.zeros((128, 1), np.float32)
    a1[:N, 0] = a["L1_attn_A"]
    cols = {
        "bq0": columns(a["L0_xattn_bq"]), "bk0": columns(a["L0_xattn_bk"]), "bv0": columns(a["L0_xattn_bv"]),
        "conv0": feature_rows(a["L0_attn_conv_w"].reshape(D, 4), 2).reshape(128, 8),
        "conv0b": columns(a["L0_attn_conv_b"]), "bd": columns(a["L0_attn_bd"]), "bg": columns(a["L0_attn_bg"]),
        "log_a": feature_rows(a["L0_attn_log_a"], 2).reshape(128, 32), "bq1": columns(a["L1_xattn_bq"]),
        "conv1": feature_rows(a["L1_attn_conv_w"].reshape(DI, 3), 4).reshape(128, 12),
        "conv1b": columns(a["L1_attn_conv_b"]), "D1": columns(a["L1_attn_D"]), "A1": a1}
    rows = {"bo0": a["L0_xattn_bo"], "boa": a["L0_attn_bo"], "bk1": a["L1_xattn_bk"], "bv1": a["L1_xattn_bv"],
            "bo1": a["L1_xattn_bo"], "gamma": a["L1_xattn_gamma"], "beta": a["L1_xattn_beta"], "br": a["L0_ffn_br"]}

    p = np.arange(128)
    batch = np.zeros((128, NT, 128), np.float32)
    for t in range(NT):
        batch[2 * t + p // 64, t, p] = 1
    state = np.zeros((128, 2 * N), np.float32)
    state[p[:96], p[:96] % 32] = 1
    consts = {
        "ident": np.eye(128, dtype=np.float32),
        "causal": np.where(np.arange(T)[None] > (p % T)[:, None], -FMAX, 0).astype(np.float32),
        "parity": np.stack([(p // HD) % 2 == 0, (p // HD) % 2 == 1], 1).astype(np.float32),
        "iota": np.tile(np.arange(E, dtype=np.float32), (128, 1)),
        "eps": np.full((128, 1), 1e-5, np.float32), "one": np.ones((128, 1), np.float32),
        "minus1": np.full((128, 1), -1, np.float32), "batch": batch.reshape(128, -1), "state": state,
        "ones": np.ones((128, 128), np.float32)}

    def three(*names):
        return np.stack([feature_rows(a[n].T, 2) for n in names], 1)

    w0 = np.concatenate([
        a["L0_ffn_W1"].reshape(E, NC, 128, F0).transpose(0, 2, 1, 3).reshape(E, 128, -1),
        a["L0_ffn_W2"].reshape(E, 8, 128, D).transpose(0, 2, 1, 3).reshape(E, 128, -1),
        a["L0_ffn_b1"].reshape(E, 8, 128).transpose(0, 2, 1),
        a["L0_ffn_b2"].reshape(E, NC, 128).transpose(0, 2, 1)], 2)
    w3 = np.zeros((E, 6 * 128, D), np.float32)
    w3[:, :F1] = a["L1_ffn_W3"].transpose(0, 2, 1)
    w1 = np.concatenate(
        [a[n].transpose(0, 2, 1).reshape(E, NC, 128, F1).transpose(0, 2, 1, 3).reshape(E, 128, -1)
         for n in ("L1_ffn_W1", "L1_ffn_W2")] + [w3.reshape(E, 6, 128, D).transpose(0, 2, 1, 3).reshape(E, 128, -1)], 2)

    arrays = {
        "x": a["x"].reshape(NT, 128, D).transpose(1, 0, 2),
        "first_ctx": feature_rows(first, 2), "ctx_t": ctx_t, "ctx_n": ctx_n,
        "mask": a["mask_BxS2_bf0"][:, :T],
        "cols": np.concatenate([cols[n] for n in COLS], 1),
        "rows": np.concatenate([rows[n] for n in ROWS])[None],
        "consts": np.concatenate([consts[n] for n in CONSTS], 1),
        "w_x0": three("L0_xattn_Wq", "L0_xattn_Wk", "L0_xattn_Wv", "L0_xattn_Wo"),
        "w_m0": three("L0_attn_Wd", "L0_attn_Wg", "L0_attn_Wo"),
        "w_bc0": feature_rows(np.concatenate([a["L0_attn_Wb"], a["L0_attn_Wc"]], 0).T, 2),
        "w_r": feature_rows(a["L0_ffn_Wr"], 2), "w0": w0,
        "w_x1": three("L1_xattn_Wq", "L1_xattn_Wk", "L1_xattn_Wv", "L1_xattn_Wo"),
        "w_in": feature_rows(a["L1_attn_W_in"], 2), "w_out": feature_rows(a["L1_attn_W_out"], 4),
        "w_bc1": feature_rows(np.concatenate([a["L1_attn_W_B"], a["L1_attn_W_C"]], 1), 4),
        "w_g1": feature_rows(a["L1_ffn_Wg"].T, 2), "w1": w1}

    nc = bacc.Bacc("TRN2", target_bir_lowering=False, num_devices=1)
    fed, args = {}, []
    for name, v in arrays.items():
        v = np.ascontiguousarray(v)
        fed[f"in_{name}"] = v
        args.append(nc.dram_tensor(f"in_{name}", v.shape, mybir.dt.from_np(v.dtype), kind="ExternalInput").ap())
    shape, dtype = _OUT
    out = nc.dram_tensor("out", shape, mybir.dt.from_np(np.dtype(dtype)), kind="ExternalOutput").ap()
    perceiver(nc, *args, out)
    got = run_bass_kernel_spmd(nc, [fed], core_ids=[0]).results[0]["out"]
    return np.asarray(got).transpose(1, 0, 2).reshape(B, T, D)
```

```python
from contextlib import ExitStack

import concourse.bass as bass
import numpy as np
from concourse import mybir

B, T, D = 8, 64, 256
S = 1601
TOK = B * T
NT = TOK // 128
NC = D // 128
REST = S - T
KT = 13
KLAST = S - 12 * 128
G = 7
H, HD = 16, 16
N = 16
E = 8
F0 = 1024
F1 = 682
F1C = [128] * 5 + [F1 - 5 * 128]
DI = 512
FMAX = float(np.finfo(np.float32).max)



def _places(sizes):
    at, out = 0, {}
    for name, n in sizes:
        out[name] = (at, n)
        at += n
    return out, at


COLS, NCOLS = _places([
    ("bq0", 2), ("bk0", 2), ("bv0", 2), ("conv0", 8), ("conv0b", 2), ("bd", 2), ("bg", 2),
    ("log_a", 32), ("bq1", 2), ("conv1", 12), ("conv1b", 4), ("D1", 4), ("A1", 1)])
ROWS, NROWS = _places([
    ("bo0", D), ("boa", D), ("bk1", D), ("bv1", D), ("bo1", D), ("gamma", D), ("beta", D), ("br", E)])
CONSTS, NCONSTS = _places([
    ("ident", 128), ("causal", T), ("parity", 2), ("iota", E), ("eps", 1), ("one", 1), ("minus1", 1),
    ("batch", NT * 128), ("state", 2 * N), ("ones", 128)])
W0N = NC * F0 + (F0 // 128) * D + F0 // 128
W1N = 2 * NC * F1 + 6 * D
PIECES = 4
WP = W1N // PIECES
ARENA = 2 * W0N + 2 * W1N
NAT = KT * (D + 1)
CTT = NC * S


def perceiver(nc, x, first_ctx, ctx_t, ctx_n, mask, cols, rows, consts, w_x0, w_m0, w_bc0, w_r, w0, b_f0,
              w_x1, w_in, w_out, w_bc1, w_g1, w1, out):
    f32, bf16, u8, u32 = mybir.dt.float32, mybir.dt.bfloat16, mybir.dt.uint8, mybir.dt.uint32
    i32, f32r = mybir.dt.int32, mybir.dt.float32r
    ALU, ACT, AX = mybir.AluOpType, mybir.ActivationFunctionType, mybir.AxisListType
    ctx = ExitStack()

    def sb(name, shape, dt=f32):
        return ctx.enter_context(nc.sbuf_tensor(name, shape, dt))

    def over(name, base, at, *shape):
        return nc.alloc_sbuf_tensor_at(name, [128, *shape], f32r, offset=base + 4 * at)

    def sem(name):
        return ctx.enter_context(nc.semaphore(name))

    def spread(ap, axis, n):
        ap = ap.unsqueeze(axis)
        shape = list(ap.shape)
        shape[axis] = n
        return ap.broadcast_to(shape)

    with ctx:
        x_tok = sb("x_tok", [128, NT, D])
        xb = sb("xb", [128, NT, D])
        xn = sb("xn", [128, NT, D])
        xnT = sb("xnT", [128, NC, TOK])
        stats = sb("stats", [128, NT, 6])
        mv = sb("mv", [128, NT, 2])
        lnv = sb("lnv", [128, NT])
        rstd = sb("rstd", [128, NT])
        cst = sb("cst", [128, NCONSTS])
        col = sb("col", [128, NCOLS])
        row = sb("row", [128, NROWS])
        wx0 = sb("wx0", [128, 4, NC, D])
        wx0_at = nc.sbuf_base - 4 * 4 * NC * D
        wm0 = sb("wm0", [128, 3, NC, D])
        wbc0 = sb("wbc0", [128, NC, 2 * N])
        wr = sb("wr", [128, NC, E])
        wx1 = sb("wx1", [128, 4, NC, D])
        win = sb("win", [128, NC, 2 * DI])
        wout = sb("wout", [128, DI // 128, D])
        wbc1 = sb("wbc1", [128, DI // 128, 2 * N])
        wg1 = sb("wg1", [128, NC, E])
        arena_work = sb("arena_work", [128, ARENA + 14720])
        arena_at = nc.sbuf_base - 4 * (ARENA + 14720)
        arena = arena_work[:, 0:ARENA]
        cT = [arena[:, k * NAT:k * NAT + CTT].rearrange("p (c s) -> p c s", c=NC) for k in range(2)]
        cN = [arena[:, (2 + k) * NAT:(3 + k) * NAT].rearrange("p (k d) -> p k d", d=D + 1) for k in range(2)]
        cT2 = [arena[:, (2 + k) * NAT:(2 + k) * NAT + CTT].rearrange("p (c s) -> p c s", c=NC) for k in range(2)]
        wf0 = [arena[:, k * W0N:(k + 1) * W0N] for k in range(4)]
        wf1 = [arena[:, k * W1N:(k + 1) * W1N] for k in range(2)]
        tail = arena[:, 4 * NAT:4 * NAT + 6 * 512]
        inp = [tail[:, c * 512:(c + 1) * 512] for c in range(NC)]
        hst = [tail[:, (2 + c) * 512:(3 + c) * 512] for c in range(NC)]
        zk = [tail[:, (4 + k) * 512:(5 + k) * 512] for k in range(2)]
        ktc = sb("ktc", [128, B, NC, D + 1])
        work = arena_work[:, ARENA:]

        def area(at, *shape):
            n = int(np.prod(shape))
            v = work[:, at:at + n]
            names = "abcd"[:len(shape)]
            if len(shape) == 1:
                return v
            return v.rearrange(f"p ({' '.join(names)}) -> p {' '.join(names)}",
                               **{k: s for k, s in zip(names[1:], shape[1:])})

        c0T = area(0, NC, TOK)
        qT = area(1024, NC, TOK)
        kb2 = area(2048, NC, B, 2, T)
        vbd = area(4096, B, 8, 34)
        P = area(6272, NT, 4, 256)
        PT = area(10368, NT, 4, 256)
        vr8 = area(14464, D)
        maskf = sb("maskf", [128, NT, T])
        mask8 = sb("mask8", [128, NT, T], u8)
        csum = sb("csum", [128, NC, B])
        mx = sb("mx", [128, NT, 4, 4])
        rest = sb("rest", [128, NT, 4, 4])
        den = sb("den", [128, NT, H])
        vro = area(6272, NT, D)
        oa = area(6272 + 1024, NT, D)
        oT = area(1024, NC, TOK)
        xc = area(0, NC, TOK)
        dt = area(1024, NC, TOK)
        dtx = area(2048, NC, TOK)
        gate = area(3072, NC, TOK)
        dec = [[area(4096 + (2 * m + c) * 512, 512) for c in range(NC)] for m in range(2)]
        hc = [[area(6144 + (2 * m + c) * 512, 512) for c in range(NC)] for m in range(2)]
        ym = area(8192, NC, TOK)
        ek = [area(9216 + k * 512, 512) for k in range(2)]
        kk = [area(10240 + k * 512, 512) for k in range(2)]
        tmp = area(11264, NC, TOK)
        bc = area(12288, 512)
        r1 = area(12800, 512)
        aneg = sb("aneg", [128, NC, N])
        bcs = sb("bcs", [96, TOK], bf16)
        mid = sb("mid", [32, TOK], bf16)
        sel = wx0[0:96, :, :, :].rearrange("p a b c -> p (a b c)").bitcast(bf16).rearrange("p (n m) -> p n m", m=128)
        msum = sb("msum", [128, NC, B])
        sc = sb("sc", [B, E])
        m8 = sb("m8", [128, NT, 8])
        i8 = sb("i8", [128, NT, 8], u32)
        topf = sb("topf", [B, 1])
        hot = sb("hot", [B, E])
        top = sb("top", [1, B], i32)
        b2t = sb("b2t", [E, D])
        hf = [area(k * F0, F0) for k in range(2)]
        hb = [area(2048 + k * F0, 8, 128) for k in range(2)]
        hr = [area(4096 + k * F0, 8, 128) for k in range(2)]
        hott = area(6144, TOK)
        QT = area(0, NC, TOK)
        z1 = area(1024, NC, TOK)
        e1 = area(2048, NC, TOK)
        GT = area(3072, NC, TOK)
        sr = area(4096, TOK)
        dn = area(4608, NC, TOK)
        aT = area(5632, NC, TOK)
        y1 = area(6656, NT, D)
        sres = area(0, 4, TOK)
        xc1 = area(2048, 4, TOK)
        xs1 = area(4096, 4, TOK)
        y2 = area(6144, 4, TOK)
        st1 = area(8192, TOK)
        pr1 = area(8704, TOK)
        dec1 = area(9216, TOK)
        da1 = sb("da1", [N, 2])
        wlo = [over(f"wlo{k}", arena_at, (2 + k) * W1N, W1N) for k in range(2)]
        whi = [over(f"whi{k}", arena_at, ARENA + at, W1N) for k, at in enumerate((9728, 4416))]
        xhi, xlo = (over(f"x_part{k}", wx0_at, k * NC * TOK, NC, TOK) for k in range(2))
        sg = [area(320 + k * 512, 512) for k in range(2)]
        hid = [area(1344 + k * 2560, 512) for k in range(2)]
        hhi = [over(f"hhi{k}", arena_at, ARENA + 1856 + k * 512, 512) for k in range(2)]
        hlo = [over(f"hlo{k}", arena_at, ARENA + 2880 + k * 512, 512) for k in range(2)]
        gt = sb("gt", [128, NT, E])
        gtmp = sb("gtmp", [128, NT, E])
        g2 = sb("g2", [128, NT, 3])
        ixf = sb("ixf", [128, NT, 2])

        bank = [ctx.enter_context(nc.psum_tensor(f"bank{i}", [128, 512], f32)) for i in range(8)]

        def C(name, i=0, n=None, p=128):
            a, w = CONSTS[name]
            return cst[0:p, a + i:a + (w if n is None else i + n)]

        def L(name, i=0, n=1, p=128):
            a, _ = COLS[name]
            return col[0:p, a + i:a + i + n]

        def R(name, p=128):
            a, w = ROWS[name]
            return row[0:p, a:a + w]

        ident = C("ident")

        s_in = sem("s_in")
        s_w = sem("s_w")
        s_w2 = sem("s_w2")
        s_ctxT = [sem(f"s_ctxT{k}") for k in range(4)]
        s_sum_act = sem("s_sum_act")
        s_sum_dve = sem("s_sum_dve")
        s_ctxN = [sem(f"s_ctxN{k}") for k in range(2)]
        s_wa0 = [sem(f"s_wa0{k}") for k in range(4)]
        s_wb0 = [sem(f"s_wb0{k}") for k in range(4)]
        s_wf1 = [sem(f"s_wf1{k}") for k in range(2)]
        s_dve = sem("s_dve")
        s_act = sem("s_act")
        s_pool = sem("s_pool")
        s_var = sem("s_var")
        s_rstd = sem("s_rstd")
        s_xn = sem("s_xn")
        s_xnT_ps = sem("s_xnT_ps")
        s_xnT = sem("s_xnT")
        s_xb = sem("s_xb")
        s_x = sem("s_x")
        s_k_ps, s_v_ps, s_q_ps = sem("s_k_ps"), sem("s_v_ps"), sem("s_q_ps")
        s_kb, s_vbd, s_vz, s_qT = sem("s_kb"), sem("s_vbd"), sem("s_vz"), sem("s_qT")
        s_sc_ps, s_sc = sem("s_sc_ps"), sem("s_sc")
        s_diff, s_exp = sem("s_diff"), sem("s_exp")
        s_PT_ps, s_PT = sem("s_PT_ps"), sem("s_PT")
        s_pv, s_vr, s_vr8, s_vrb = sem("s_pv"), sem("s_vr"), sem("s_vr8"), sem("s_vrb")
        s_o, s_oT_ps, s_oT, s_proj0 = sem("s_o"), sem("s_oT_ps"), sem("s_oT"), sem("s_proj0")

        s_conv0, s_xc0 = sem("s_conv0"), sem("s_xc0")
        s_m0_ps = sem("s_m0_ps")
        s_abs = sem("s_abs")
        s_sp, s_ge = sem("s_sp"), sem("s_ge")
        s_bc_ps, s_bcs, s_sel = sem("s_bc_ps"), sem("s_bcs"), sem("s_sel")
        s_an, s_aneg = sem("s_an"), sem("s_aneg")
        s_dtx = sem("s_dtx")
        s_loop = sem("s_loop")
        s_decay = sem("s_decay")
        s_ssm = sem("s_ssm")
        s_yadd = sem("s_yadd")
        s_B, s_C = sem("s_B"), sem("s_C")
        s_z = sem("s_z")
        s_e = sem("s_e")
        s_kt = sem("s_kt")
        s_kp = sem("s_kp")
        s_kfree = sem("s_kfree")
        s_ktc = sem("s_ktc")
        s_yg, s_proj1 = sem("s_yg"), sem("s_proj1")

        s_ms, s_rt_ps, s_topf, s_topT, s_top = (sem("s_ms"), sem("s_rt_ps"), sem("s_topf"), sem("s_topT"),
                                                sem("s_top"))
        s_hot, s_hot_ps, s_hott = sem("s_hot"), sem("s_hot_ps"), sem("s_hott")
        s_h_ps, s_hf0, s_hf1, s_hT_ps, s_hb, s_hr, s_y_ps = (sem("s_h_ps"), sem("s_hf0"), sem("s_hf1"), sem("s_hT_ps"), sem("s_hb"),
                                                     sem("s_hr"), sem("s_y_ps"))

        s_q1_ps, s_z1, s_e1, s_Q1, s_G_ps, s_GT, s_num = (sem("s_q1_ps"), sem("s_z1"), sem("s_e1"), sem("s_Q1"),
                                                          sem("s_G_ps"), sem("s_GT"), sem("s_num"))
        s_aT, s_proj2, s_var1, s_rstd1, s_x3b = (sem("s_aT"), sem("s_proj2"), sem("s_var1"), sem("s_rstd1"),
                                                 sem("s_x3b"))

        s_in_ps, s_res, s_cv1, s_xs1, s_bc1, s_pr1, s_ys, s_y2, s_proj3 = (
            sem("s_in_ps"), sem("s_res"), sem("s_cv1"), sem("s_xs1"), sem("s_bc1"), sem("s_pr1"), sem("s_ys"),
            sem("s_y2"), sem("s_proj3"))
        s_ea1 = sem("s_ea1")

        s_lg, s_gd, s_ge1, s_gate = sem("s_lg"), sem("s_gd"), sem("s_ge1"), sem("s_gate")
        s_whi, s_wlo = sem("s_whi"), sem("s_wlo")
        s_xhi, s_xlo = sem("s_xhi"), sem("s_xlo")
        s_h12, s_sg = sem("s_h12"), sem("s_sg")
        s_hid = sem("s_hid")
        s_hhi, s_hlo = sem("s_hhi"), sem("s_hlo")
        s_hfree = sem("s_hfree")
        s_o_ps, s_ofree = sem("s_o_ps"), sem("s_ofree")
        s_out = sem("s_out")

        block = ctx.enter_context(nc.Block())
        ORDER = [7, 6, 5, 4, 3, 2, 1, 0]
        SLOT = [0, 1, 2, 3, 2, 3, 1, 0]
        slots = [cT[0], cT[1], cT2[0], cT2[1]]
        seen = [sum(1 for j in range(i) if SLOT[j] == SLOT[i]) for i in range(8)]
        IN = 16 * 8
        GROUPS = B * G

        @block.sync
        def _(sp):
            def store():
                sp.wait_ge(s_x, 6)
                sp.dma_start(out, x_tok[:]).then_inc(s_out, 16)
                sp.wait_ge(s_out, 16)

            for dst, src in ((x_tok[:], x), (c0T, first_ctx), (wx0[:], w_x0), (cst[:], consts), (col[:], cols),
                             (row[:], rows.broadcast_to([128, NROWS]))):
                sp.dma_start(dst, src).then_inc(s_in, 16)
            for h in range(2):
                sp.dma_start(mask8[64 * h:64 * h + 64, :, :],
                             mask.rearrange("(t h) s -> h t s", h=2)[h].unsqueeze(0).broadcast_to([64, NT, T])
                             ).then_inc(s_in, 16)
            for i, b in enumerate(ORDER):
                if seen[i]:
                    last = max(j for j in range(i) if SLOT[j] == SLOT[i])
                    sp.wait_ge(s_sum_act, last + 1)
                    sp.wait_ge(s_sum_dve, last + 1)
                sp.dma_start(slots[SLOT[i]], ctx_t[b]).then_inc(s_ctxT[SLOT[i]], 16)
                if i == 3:
                    for dst, src in ((wm0[:], w_m0), (wbc0[:], w_bc0)):
                        sp.dma_start(dst, src).then_inc(s_w, 16)
            sp.dma_start(wx1[:], w_x1).then_inc(s_w, 16)
            for k in range(2):
                if k == 0:
                    sp.wait_ge(s_sum_act, 6)
                    sp.wait_ge(s_sum_dve, 6)
                sp.dma_start(cN[k][:, :, 0:D], ctx_n[k]).then_inc(s_ctxN[k], 16)
            for dst, src in ((wr[:], w_r), (b2t[:], b_f0), (win[:], w_in), (wout[:], w_out), (wbc1[:], w_bc1), (wg1[:], w_g1)):
                sp.dma_start(dst, src).then_inc(s_w2, 16)
            with sp.Fori(1, B // 2) as j:
                for k in range(2):
                    sp.wait_ge(s_kp, 2 * G * j + (G * k - G))
                    sp.dma_start(cT[k], ctx_t[bass.ds(2 * j + k, 1)].rearrange("o p c s -> (o p) c s")
                                 ).then_inc(s_ctxT[k], 16)
                    sp.wait_ge(s_kfree, 2 * G * j + (G * k - G + 2))
                    sp.dma_start(cN[k][:, :, 0:D], ctx_n[bass.ds(2 * j + k, 1)].rearrange("o p k d -> (o p) k d")
                                 ).then_inc(s_ctxN[k], 16)
            sp.wait_ge(s_top, 1)
            for t in range(NT):
                chosen = [sp.value_load(top[0:1, 2 * t + h:2 * t + h + 1], min_val=0, max_val=E - 1) for h in range(2)]
                for part, (lo, hi) in enumerate(((0, NC * F0), (NC * F0, W0N))):
                    if t >= 2:
                        sp.wait_ge((s_h_ps, s_y_ps)[part], (2 * (t - 1), t - 1)[part])
                    for h, e in enumerate(chosen):
                        k = (2 * t + h) % 4
                        sp.dma_start(wf0[k][:, lo:hi], w0[bass.ds(e, 1), :, lo:hi].rearrange("o p n -> (o p) n")
                                     ).then_inc((s_wa0, s_wb0)[part][k], 16)
            sp.wait_ge(s_y_ps, NT)
            for k in range(2):
                sp.dma_start(wf1[k], w1[k]).then_inc(s_wf1[k], 16)
            with sp.Fori(1, E // 2) as j:
                for k in range(2):
                    sp.wait_ge(s_wlo, 2 * PIECES * j + (k - 1) * PIECES)
                    sp.dma_start(wf1[k], w1[bass.ds(2 * j + k, 1)].rearrange("o p n -> (o p) n")
                                 ).then_inc(s_wf1[k], 16)
            store()

        @block.gpsimd
        def _(pool):
            gp = nc.gpsimd
            gp.memset(vbd[:], 0.0).then_inc(s_vz, 1)
            pool.wait_ge(s_vz, 1)
            gp.memset(vbd[0:64, :, :, 32:33], 1.0).then_inc(s_pool, 1)
            pool.wait_ge(s_pool, 1)
            gp.memset(vbd[64:128, :, :, 33:34], 1.0).then_inc(s_vz, 1)
            pool.wait_ge(s_vz, 2)
            pool.wait_ge(s_in, IN)
            gp.tensor_tensor(xb[:], x_tok[:], spread(R("bo0"), 1, NT), ALU.add).then_inc(s_xb, 1)
            pool.wait_ge(s_x, 1)
            gp.tensor_copy(sel[:], spread(C("state", p=96), 2, 128)).then_inc(s_sel, 1)
            gp.tensor_tensor(xb[:], x_tok[:], spread(R("boa"), 1, NT), ALU.add).then_inc(s_xb, 1)
            gp.memset(ym[:], 0.0).then_inc(s_yadd, 2)
            for m in range(2):
                for c in range(NC):
                    gp.memset(dec[m][c].rearrange("p (b t) -> p b t", t=T)[:, :, 0:1], 0.0).then_inc(s_yadd, 1)
            pool.wait_ge(s_sum_act, 6)
            pool.wait_ge(s_sum_dve, 6)
            for k in range(2):
                gp.memset(cN[k][:, :, D:D + 1], 1.0).then_inc(s_yadd, 1)
            pool.wait_ge(s_yadd, 8)
            with pool.Fori(0, N // 4) as j:
                for k in range(2):
                    for m in range(2):
                        for c in range(NC):
                            n = 4 * j + (2 * k + m)
                            pool.wait_ge(s_ssm, 6 * n + (12 + 5 + c))
                            pool.wait_ge(s_yadd, 2 * n + (8 + c - 1))
                            gp.tensor_tensor(ym[:, c, :], ym[:, c, :], hc[m][c], ALU.add).then_inc(s_yadd, 1)
            pool.wait_ge(s_xn, 4 * NT)
            gp.tensor_tensor(xb[:], xn[:], spread(R("bo1"), 1, NT), ALU.add).then_inc(s_xb, 1)
            gp.tensor_tensor(x_tok[:], x_tok[:], spread(R("beta"), 1, NT), ALU.add).then_inc(s_x3b, 1)

        @block.scalar
        def _(act):
            sa = nc.scalar
            steps = [0]

            def own(ins):
                steps[0] += 1
                ins.then_inc(s_act, 1)
                act.wait_ge(s_act, steps[0])

            def rstd_of(n, s_ready, s_done):
                act.wait_ge(s_ready, n)
                own(sa.activation(lnv[:], mv[:, :, 1], ACT.Ln, bias=C("eps")))
                sa.activation(rstd[:], lnv[:], ACT.Exp, scale=-0.5).then_inc(s_done, 1)

            def xnT_evac(n):
                act.wait_ge(s_xnT_ps, n)
                sa.copy(xnT[:, 0, :], bank[6][:]).then_inc(s_xnT, 1)

            def sums(i):
                b = ORDER[i]
                act.wait_ge(s_ctxT[SLOT[i]], 16 * (seen[i] + 1))
                v = slots[SLOT[i]][:, 0, 0:S]
                sa.activation(v[:, 0:REST], v[:, 0:REST], ACT.Copy, accum_out=csum[:, 0, b:b + 1]).then_inc(s_sum_act, 1)

            sa.preload_act_table_set("natural_log_exp_and_others")
            act.wait_ge(s_in, IN)
            act.wait_ge(s_vz, 2)
            act.wait_ge(s_v_ps, 1)
            vb = vbd.rearrange("p (t h) n w -> p t h n w", h=2)
            for i in range(2):
                v = bank[2 + i][:].rearrange("p (t n e) -> p t n e", t=2, e=2 * HD)
                for h in range(2):
                    for a in range(2):
                        sa.copy(vb[64 * a:64 * a + 64, 2 * i:2 * i + 2, h, :, HD * a:HD * a + HD],
                                v[64 * h:64 * h + 64, :, :, HD * a:HD * a + HD]).then_inc(s_vbd, 1)
            rstd_of(1, s_var, s_rstd)
            xnT_evac(1)
            sums(0)
            sums(1)
            for r in range(2):
                if r == 1:
                    sums(2)
                for j in range(4):
                    act.wait_ge(s_diff, 4 * r + j + 1)
                    p = P[:, 2 * r:2 * r + 2, j, :]
                    sa.activation(p, p, ACT.Exp).then_inc(s_exp, 1)
            sums(3)
            for r in range(2):
                for j in (0, 2):
                    act.wait_ge(s_PT_ps, 4 * r + j + 1)
                    sa.copy(PT[:, 2 * r:2 * r + 2, j, :],
                            bank[[2, 3, 4, 5][j] if r == 0 else [6, 7, 0, 1][j]][:].rearrange("p (t n) -> p t n", t=2)
                            ).then_inc(s_PT, 1)
            for i in range(4, 8):
                sums(i)
            act.wait_ge(s_vr, 1)
            sa.copy(vr8[0:B, :], bank[0][0:B, 0:D]).then_inc(s_vr8, 1)
            act.wait_ge(s_oT_ps, 1)
            sa.activation(oT[:, 0, :], bank[6][:], ACT.Identity, bias=L("bv0", 0)).then_inc(s_oT, 1)

            sa.activation(aneg[:], L("log_a", 0, 32), ACT.Exp).then_inc(s_an, 1)
            rstd_of(2, s_var, s_rstd)
            xnT_evac(2)
            for c in range(NC):
                act.wait_ge(s_conv0, c + 1)
                sa.activation(xc[:, c, :], tmp[:, c, :], ACT.Silu).then_inc(s_xc0, 1)
            for c in range(NC):
                act.wait_ge(s_m0_ps, c + 1)
                act.wait_ge(s_aneg, 2)
                sa.activation(gate[:, c, :], bank[c][:], ACT.Exp, scale=-1.0, bias=g2[:, c, 0:1]).then_inc(s_ge, 1)
            for c in range(NC):
                act.wait_ge(s_abs, c + 1)
                own(sa.activation(dtx[:, c, :], dt[:, c, :], ACT.Abs))
                own(sa.activation(dtx[:, c, :], dtx[:, c, :], ACT.Exp, scale=-1.0))
                sa.activation(dtx[:, c, :], dtx[:, c, :], ACT.Ln, bias=C("one")).then_inc(s_sp, 1)
            act.wait_ge(s_loop, 1)
            act.wait_ge(s_yadd, 8)
            sa.copy(lnv[:, 0:1], rstd[:, 0:1]).then_inc(s_ktc, 4)
            with act.Fori(0, B // 2) as j:
                for k in range(2):
                    def decay(m):
                        n = 4 * j + (2 * k + m)
                        for c in range(NC):
                            act.wait_ge(s_ssm, 6 * n + (3 + c))
                            d3 = dec[m][c].rearrange("p (b t) -> p b t", t=T)[:, :, 1:T]
                            dt3 = dt[:, c, :].rearrange("p (b t) -> p b t", t=T)[:, :, 1:T]
                            sa.activation(d3, dt3, ACT.Exp, scale=aneg[:, c, bass.ds(n, 1)]).then_inc(s_decay, 1)

                    decay(0)
                    for g in range(G):
                        i = (G * k + g) % 2
                        gg = 2 * G * j + (G * k + g)
                        p, w = (128, 512) if g < G - 1 else (KLAST, D)
                        act.wait_ge(s_z, gg + 3)
                        act.wait_ge(s_kt, gg + 1)
                        sa.activation(ek[i][0:p, 0:w], zk[i][0:p, 0:w], ACT.Exp, bias=C("minus1", p=p)).then_inc(s_e, 1)
                        if g == 2:
                            decay(1)
                    act.wait_ge(s_kfree, 2 * G * j + (G * k + G + 2))
                    for c in range(NC):
                        sa.copy(ktc[:, bass.ds(2 * j + k, 1), c, :].rearrange("p o d -> p (o d)"),
                                bank[2 + 2 * k + c][:, 0:D + 1]).then_inc(s_ktc, 1)
            rstd_of(3, s_var, s_rstd)
            xnT_evac(3)
            act.wait_ge(s_hot_ps, 1)
            sa.copy(hott[0:E, :], bank[2][0:E, :]).then_inc(s_hott, 1)
            for t in range(NT + 1):
                if t < NT:
                    act.wait_ge(s_h_ps, 2 * t + 1)
                    sa.copy(hf[t % 2][:, 0:512], bank[2 * (t % 2)][:]).then_inc(s_hf0, 1)
                if t:
                    for i in range(2):
                        act.wait_ge(s_hb, 4 * (t - 1) + 2 * i + 2)
                        sa.activation(hr[(t - 1) % 2][:, 4 * i:4 * i + 4, :], hb[(t - 1) % 2][:, 4 * i:4 * i + 4, :],
                                      ACT.Relu).then_inc(s_hr, 1)
            rstd_of(4, s_var, s_rstd)
            xnT_evac(4)
            for c in range(NC):
                act.wait_ge(s_z1, c + 1)
                sa.activation(e1[:, c, :], z1[:, c, :], ACT.Exp, bias=C("minus1")).then_inc(s_e1, 1)
            act.wait_ge(s_wf1[0], 16)
            for i in range(PIECES):
                sa.copy(whi[0][:, WP * i:WP * i + WP], wf1[0][:, WP * i:WP * i + WP]).then_inc(s_whi, 1)
            act.wait_ge(s_G_ps, 1)
            sa.copy(GT[:, 0, :], bank[2][:]).then_inc(s_GT, 1)
            act.wait_ge(s_G_ps, 3)
            sa.copy(sr[0:1, :], bank[4][0:1, :]).then_inc(s_GT, 1)
            rstd_of(1, s_var1, s_rstd1)
            sa.activation(da1[:, 0:1], L("A1", p=N), ACT.Exp).then_inc(s_ea1, 1)
            rstd_of(5, s_var, s_rstd)
            xnT_evac(5)
            for c in range(4):
                act.wait_ge(s_in_ps, 5 + c)
                sa.activation(sres[:, c, :], bank[4 + c][:], ACT.Silu).then_inc(s_res, 1)
            for c in range(4):
                act.wait_ge(s_cv1, c + 1)
                sa.activation(xs1[:, c, :], xc1[:, c, :], ACT.Silu).then_inc(s_xs1, 1)
            rstd_of(6, s_var, s_rstd)
            xnT_evac(6)
            act.wait_ge(s_xnT, 2 * 6)
            sa.copy(xhi[:, 0, :], xnT[:, 0, :]).then_inc(s_xhi, 1)
            sa.copy(xhi[:, 1, :], xnT[:, 1, :]).then_inc(s_xhi, 1)
            act.wait_ge(s_gd, 1)
            sa.activation(g2[:, :, 1], g2[:, :, 0], ACT.Exp).then_inc(s_ge1, 1)
            sa.preload_act_table(ACT.Silu)

            def expert(j, k, split):
                for f in range(6):
                    q, i, w = 6 * k + f, f % 2, F1C[f]
                    act.wait_ge(s_h12, 12 * j + (q + 1))
                    act.wait_ge(s_hid, 12 * j + (q + 1))
                    sa.activation(sg[i][0:w, :], bank[2 * i][0:w, :], ACT.Silu).then_inc(s_sg, 1)
                    if split and 1 <= f <= PIECES:
                        if f == 1:
                            act.wait_ge(s_wf1[1 - k], 16 * j + (16 + 16 * k))
                            act.wait_ge(s_hfree, 12 * j + (6 * k + 2))
                        at = WP * (f - 1)
                        sa.copy(whi[1 - k][:, at:at + WP], wf1[1 - k][:, at:at + WP]).then_inc(s_whi, 1)

            with act.Fori(0, E // 2 - 1) as j:
                for k in range(2):
                    expert(j, k, True)
            for k in range(2):
                expert(E // 2 - 1, k, k == 0)

        @block.vector
        def _(dve):
            v = nc.vector
            steps = [0]

            def mark(ins):
                steps[0] += 1
                ins.then_inc(s_dve, 1)
                return steps[0]

            def own(ins):
                dve.wait_ge(s_dve, mark(ins))

            def moments(src, done):
                for t in range(NT):
                    last = mark(v.bn_stats(stats[:, t, :], src[:, t, :]))
                dve.wait_ge(s_dve, last)
                for t in range(NT):
                    ins = v.bn_aggr(mv[:, t, :], stats[:, t, :])
                    if t == NT - 1:
                        ins.then_inc(done, 1)
                    else:
                        mark(ins)

            def normalise(n):
                moments(x_tok, s_var)
                dve.wait_ge(s_rstd, n)
                dve.wait_ge(s_var, n)
                for t in range(NT):
                    v.tensor_scalar(xn[:, t, :], x_tok[:, t, :], mv[:, t, 0:1], rstd[:, t:t + 1],
                                    ALU.subtract, ALU.mult).then_inc(s_xn, 1)
                dve.wait_ge(s_xnT_ps, n)
                v.tensor_copy(xnT[:, 1, :], bank[7][:]).then_inc(s_xnT, 1)

            def sums(i):
                b = ORDER[i]
                dve.wait_ge(s_ctxT[SLOT[i]], 16 * (seen[i] + 1))
                v.reduce_sum(csum[:, 1, b:b + 1], slots[SLOT[i]][:, 1, 0:REST], AX.X).then_inc(s_sum_dve, 1)

            def split_low(k, i, n):
                dve.wait_ge(s_whi, n)
                at = WP * i
                v.tensor_tensor(wlo[k][:, at:at + WP], wf1[k][:, at:at + WP], whi[k][:, at:at + WP].bitcast(f32),
                                ALU.subtract).then_inc(s_wlo, 1)

            dve.wait_ge(s_in, IN)
            own(v.tensor_scalar(maskf[:], mask8[:], -FMAX, None, ALU.mult))
            own(v.tensor_tensor(maskf[:], maskf[:], spread(C("causal"), 1, NT), ALU.min))
            for c in range(NC):
                dve.wait_ge(s_k_ps, c + 1)
                for h in range(2):
                    v.tensor_scalar(kb2[:, c, :, h, :], bank[c][:].rearrange("p (b s) -> p b s", s=T),
                                    L("bk0", c), C("parity", h, 1), ALU.add, ALU.mult).then_inc(s_kb, 1)
            normalise(1)
            for c in range(NC):
                dve.wait_ge(s_q_ps, c + 1)
                v.tensor_scalar(qT[:, c, :], bank[c][:], L("bq0", c), HD ** -0.5, ALU.add, ALU.mult).then_inc(s_qT, 1)
            sums(0)
            sums(1)
            for r in range(2):
                banks = [2, 3, 4, 5] if r == 0 else [6, 7, 0, 1]
                ready = []
                for j in range(4):
                    dve.wait_ge(s_sc_ps, 4 * r + j + 1)
                    v.tensor_tensor(
                        P[:, 2 * r:2 * r + 2, j, :].rearrange("p t (g s) -> p t g s", s=T),
                        bank[banks[j]][:].rearrange("p (t g s) -> p t g s", t=2, s=T),
                        spread(maskf[:, 2 * r:2 * r + 2, :], 2, 4), ALU.add).then_inc(s_sc, 1)
                for j in range(4):
                    dve.wait_ge(s_sc, 4 * r + j + 1)
                    ready.append(mark(v.tensor_reduce(
                        mx[:, 2 * r:2 * r + 2, j, :],
                        P[:, 2 * r:2 * r + 2, j, :].rearrange("p t (g s) -> p t g s", s=T), AX.X, ALU.max)))
                for j in range(4):
                    dve.wait_ge(s_dve, ready[j])
                    p4 = P[:, 2 * r:2 * r + 2, j, :].rearrange("p t (g s) -> p t g s", s=T)
                    v.tensor_tensor(p4, p4, spread(mx[:, 2 * r:2 * r + 2, j, :], 3, T), ALU.subtract).then_inc(s_diff, 1)
                if r == 0:
                    sums(2)
            own(v.tensor_scalar(rest[:], mx[:], -FMAX, None, ALU.is_le))
            sums(3)
            for r in range(2):
                for j in (1, 3):
                    dve.wait_ge(s_PT_ps, 4 * r + j + 1)
                    v.tensor_copy(PT[:, 2 * r:2 * r + 2, j, :],
                                  bank[[2, 3, 4, 5][j] if r == 0 else [6, 7, 0, 1][j]][:].rearrange("p (t n) -> p t n", t=2)
                                  ).then_inc(s_PT, 1)
            for i in range(4, 8):
                sums(i)
            dve.wait_ge(s_pv, NT)
            def heads(ap):
                return ap.rearrange("p j (c a) -> p c j a", a=2)
            for t in range(NT):
                d4 = den[:, t, :].rearrange("p (c j a) -> p c j a", c=2, a=2)
                last = mark(v.scalar_tensor_tensor(
                    den[:, t, 0:8].rearrange("p (j a) -> p j a", a=2), rest[:, t, :, 0:2], float(REST),
                    bank[2 + t][:, 0:272].rearrange("p (n w) -> p n w", w=34)[:, 0:4, 32:34], ALU.mult, ALU.add))
                last = mark(v.scalar_tensor_tensor(
                    den[:, t, 8:16].rearrange("p (j a) -> p j a", a=2), rest[:, t, :, 2:4], float(REST),
                    bank[2 + t][:, 0:272].rearrange("p (n w) -> p n w", w=34)[:, 4:8, 32:34], ALU.mult, ALU.add))
            dve.wait_ge(s_dve, last)
            own(v.reciprocal(den[:], den[:]))
            dve.wait_ge(s_vrb, 1)
            for t in range(NT):
                for c in range(NC):
                    last = mark(v.tensor_tensor(
                        vro[:, t, 128 * c:128 * c + 128].rearrange("p (j a e) -> p j a e", j=4, a=2),
                        bank[t // 2][:, 256 * (t % 2) + 128 * c:256 * (t % 2) + 128 * c + 128].rearrange(
                            "p (j a e) -> p j a e", j=4, a=2),
                        spread(rest[:, t, :, 2 * c:2 * c + 2], 3, HD), ALU.mult))
            dve.wait_ge(s_dve, last)
            for t in range(NT):
                last = mark(v.tensor_tensor(
                    vro[:, t, :].rearrange("p (n e) -> p n e", e=32), vro[:, t, :].rearrange("p (n e) -> p n e", e=32),
                    bank[2 + t][:, 0:272].rearrange("p (n w) -> p n w", w=34)[:, :, 0:32], ALU.add))
            dve.wait_ge(s_dve, last)
            for t in range(NT):
                v.tensor_tensor(oa[:, t, :].rearrange("p (h e) -> p h e", e=HD),
                                vro[:, t, :].rearrange("p (h e) -> p h e", e=HD),
                                spread(den[:, t, :], 2, HD), ALU.mult).then_inc(s_o, 1)
            dve.wait_ge(s_oT_ps, 1)
            v.tensor_scalar(oT[:, 1, :], bank[7][:], L("bv0", 1), None, ALU.add).then_inc(s_oT, 1)
            dve.wait_ge(s_xb, 1)
            for t in range(NT):
                dve.wait_ge(s_proj0, t + 1)
                ins = v.tensor_tensor(x_tok[:, t, :], xb[:, t, :], bank[t][:, 0:D], ALU.add)
                if t < NT - 1:
                    mark(ins)
            ins.then_inc(s_x, 1)
            dve.wait_ge(s_x, 1)
            dve.wait_ge(s_dve, steps[0])

            dve.wait_ge(s_an, 1)
            v.tensor_scalar(aneg[:], aneg[:], -1.0, None, ALU.mult).then_inc(s_aneg, 1)
            v.tensor_scalar(g2[:, 0:NC, 0:1], L("bg", 0, 2).unsqueeze(2), -1.0, None, ALU.mult).then_inc(s_aneg, 1)
            mark(v.tensor_scalar(R("bk1"), R("bk1"), 1.0, None, ALU.add))
            normalise(2)
            dve.wait_ge(s_xnT, 4)
            x3 = [xnT[:, c, :].rearrange("p (b t) -> p b t", t=T) for c in range(NC)]
            t3 = [tmp[:, c, :].rearrange("p (b t) -> p b t", t=T) for c in range(NC)]
            last = [None] * NC
            for c in range(NC):
                last[c] = mark(v.tensor_scalar(t3[c], x3[c], L("conv0", 4 * c + 3), L("conv0b", c), ALU.mult, ALU.add))
            for s in range(1, 4):
                for c in range(NC):
                    dve.wait_ge(s_dve, last[c])
                    ins = v.scalar_tensor_tensor(t3[c][:, :, s:T], x3[c][:, :, 0:T - s], L("conv0", 4 * c + 3 - s),
                                                 t3[c][:, :, s:T], ALU.mult, ALU.add)
                    if s < 3:
                        last[c] = mark(ins)
                    else:
                        ins.then_inc(s_conv0, 1)
            for c in range(NC):
                dve.wait_ge(s_ge, c + 1)
                own(v.tensor_scalar(gate[:, c, :], gate[:, c, :], 1.0, None, ALU.add))
                mark(v.reciprocal(gate[:, c, :], gate[:, c, :]))
            for c in range(NC):
                dve.wait_ge(s_m0_ps, c + 3)
                v.tensor_scalar(dt[:, c, :], bank[2 + c][:], L("bd", c), None, ALU.add).then_inc(s_abs, 1)
            dve.wait_ge(s_bc_ps, 1)
            own(v.tensor_copy(bc[0:32, :], bank[4][0:32, :]))
            own(v.tensor_copy(bcs[0:32, :], bc[0:32, :]))
            own(v.tensor_tensor(r1[0:32, :], bc[0:32, :], bcs[0:32, :], ALU.subtract))
            own(v.tensor_copy(mid[:], r1[0:32, :]))
            v.tensor_copy(bcs[32:64, :], mid[:]).then_inc(s_bcs, 1)
            v.tensor_tensor(bcs[64:96, :], r1[0:32, :], mid[:], ALU.subtract).then_inc(s_bcs, 1)
            for c in range(NC):
                dve.wait_ge(s_sp, c + 1)
                mark(v.scalar_tensor_tensor(dt[:, c, :], dt[:, c, :], 0.0, dtx[:, c, :], ALU.max, ALU.add))
            dve.wait_ge(s_dve, steps[0])
            v.tensor_tensor(dtx[:, 0, :], dt[:, 0, :], xc[:, 0, :], ALU.mult).then_inc(s_ssm, 6)
            v.tensor_tensor(dtx[:, 1, :], dt[:, 1, :], xc[:, 1, :], ALU.mult).then_inc(s_ssm, 6)
            dve.wait_ge(s_ssm, 12)
            v.memset(ek[0], 0.0).then_inc(s_z, 2)
            v.memset(ek[1], 0.0).then_inc(s_kt, 2)
            dve.wait_ge(s_z, 2)
            dve.wait_ge(s_kt, 2)
            v.memset(stats[:, 0, 0:1], 0.0).then_inc(s_loop, 1)
            with dve.Fori(0, B // 2) as j:
                for k in range(2):
                    def ssm(q):
                        m, op, c = q // 6, (q % 6) // 2, q % 2
                        n = 4 * j + (2 * k + m)
                        if op == 0:
                            dve.wait_ge(s_B, n + 1)
                            v.tensor_tensor(inp[c], dtx[:, c, :], bank[6][:], ALU.mult).then_inc(s_ssm, 1)
                        elif op == 1:
                            dve.wait_ge(s_decay, 2 * n + (c + 1))
                            dve.wait_ge(s_ssm, 6 * n + (12 + 1 + c))
                            v.tensor_tensor_scan(hst[c], dec[m][c], inp[c], 0.0, ALU.mult, ALU.add).then_inc(s_ssm, 1)
                        else:
                            dve.wait_ge(s_C, n + 1)
                            dve.wait_ge(s_ssm, 6 * n + (12 + 3 + c))
                            dve.wait_ge(s_yadd, 2 * n + (8 - 3 + c))
                            v.tensor_tensor(hc[m][c], hst[c], bank[7][:], ALU.mult).then_inc(s_ssm, 1)

                    for g in range(G):
                        i = (G * k + g) % 2
                        gg = 2 * G * j + (G * k + g)
                        p, w = (128, 512) if g < G - 1 else (KLAST, D)
                        reps = w // D
                        dve.wait_ge(s_kp, gg + 1)
                        v.tensor_tensor(zk[i][0:p, 0:w].rearrange("p (r d) -> p r d", r=reps),
                                        bank[i][0:p, 0:w].rearrange("p (r d) -> p r d", r=reps),
                                        spread(R("bk1", p=p), 1, reps), ALU.add).then_inc(s_z, 1)
                        if g < 6:
                            ssm(2 * g)
                        dve.wait_ge(s_e, gg + 1)
                        dve.wait_ge(s_kfree, gg + 1)
                        dve.wait_ge(s_z, gg + 3)
                        v.scalar_tensor_tensor(kk[i][0:p, 0:w], ek[i][0:p, 0:w], 1.0, zk[i][0:p, 0:w],
                                               ALU.min, ALU.max).then_inc(s_kt, 1)
                        if g < 6:
                            ssm(2 * g + 1)
            dve.wait_ge(s_yadd, 8 + 2 * N)
            for c in range(NC):
                v.tensor_tensor(ym[:, c, :], ym[:, c, :], gate[:, c, :], ALU.mult).then_inc(s_yg, 1)
            dve.wait_ge(s_xb, 2)
            for t in range(NT):
                dve.wait_ge(s_proj1, t + 1)
                ins = v.tensor_tensor(x_tok[:, t, :], xb[:, t, :], bank[t][:, 0:D], ALU.add)
                if t < NT - 1:
                    mark(ins)
            ins.then_inc(s_x, 1)
            dve.wait_ge(s_x, 2)
            dve.wait_ge(s_dve, steps[0])

            normalise(3)
            dve.wait_ge(s_xnT, 6)
            for c in range(NC):
                v.reduce_sum(msum[:, c, :], xnT[:, c, :].rearrange("p (b t) -> p b t", t=T), AX.X).then_inc(s_ms, 1)
            dve.wait_ge(s_rt_ps, 1)
            own(v.scalar_tensor_tensor(sc[:], bank[0][0:B, 0:E], 1.0 / T, R("br", p=B), ALU.mult, ALU.add))
            own(v.max(m8[0:B, 0, :], sc[:]))
            own(v.max_index(i8[0:B, 0, :], m8[0:B, 0, :], sc[:]))
            v.tensor_copy(topf[:], i8[0:B, 0, 0:1]).then_inc(s_topf, 1)
            dve.wait_ge(s_topT, 1)
            v.tensor_copy(top[:], bank[1][0:1, 0:B]).then_inc(s_top, 1)
            dve.wait_ge(s_topf, 1)
            v.tensor_scalar(hot[:], C("iota", p=B), topf[:], None, ALU.is_equal).then_inc(s_hot, 1)
            for t in range(NT + 1):
                if t < NT:
                    dve.wait_ge(s_h_ps, 2 * t + 2)
                    v.tensor_copy(hf[t % 2][:, 512:F0], bank[2 * (t % 2) + 1][:]).then_inc(s_hf1, 1)
                if t:
                    q = t - 1
                    dve.wait_ge(s_hT_ps, t)
                    for i in range(2):
                        for h in range(2):
                            k = (2 * q + h) % 4
                            dve.wait_ge(s_wb0[k], 16 * (q // 2 + 1))
                            v.tensor_tensor(hb[q % 2][:, 4 * i:4 * i + 4, T * h:T * h + T],
                                            bank[4 + i][:].rearrange("p (f t) -> p f t", t=128)[:, :, T * h:T * h + T],
                                            spread(wf0[k][:, W0N - 8 + 4 * i:W0N - 4 + 4 * i], 2, T), ALU.add).then_inc(s_hb, 1)
                    dve.wait_ge(s_y_ps, t)
                    ins = v.tensor_tensor(x_tok[:, q, :], x_tok[:, q, :], bank[6 + q % 2][:, 0:D], ALU.add)
                    if q < NT - 1:
                        mark(ins)
            ins.then_inc(s_x, 1)
            dve.wait_ge(s_x, 3)
            dve.wait_ge(s_dve, steps[0])

            normalise(4)
            for c in range(NC):
                dve.wait_ge(s_q1_ps, c + 1)
                v.tensor_scalar(z1[:, c, :], bank[c][:], L("bq1", c), 1.0, ALU.add, ALU.add).then_inc(s_z1, 1)
            dve.wait_ge(s_z1, 2)
            for c in range(NC):
                dve.wait_ge(s_e1, c + 1)
                v.scalar_tensor_tensor(QT[:, c, :], e1[:, c, :], 1.0, z1[:, c, :], ALU.min, ALU.max).then_inc(s_Q1, 1)
            dve.wait_ge(s_Q1, 2)
            for c in range(NC):
                last = mark(v.tensor_tensor(dn[:, c, :].rearrange("p (b t) -> p b t", t=T),
                                            QT[:, c, :].rearrange("p (b t) -> p b t", t=T),
                                            spread(ktc[:, :, c, D], 2, T), ALU.mult))
            dve.wait_ge(s_dve, last)
            own(v.tensor_scalar(dn[:], dn[:], 1e-6, None, ALU.add))
            mark(v.reciprocal(dn[:], dn[:]))
            for i in range(PIECES):
                split_low(0, i, 1 + i)
            dve.wait_ge(s_G_ps, 2)
            v.tensor_copy(GT[:, 1, :], bank[3][:]).then_inc(s_GT, 1)
            dve.wait_ge(s_dve, steps[0])
            for c in range(NC):
                dve.wait_ge(s_num, c + 1)
                v.tensor_tensor(aT[:, c, :], dn[:, c, :], bank[c][:], ALU.mult).then_inc(s_aT, 1)
            dve.wait_ge(s_xb, 3)
            for t in range(NT):
                dve.wait_ge(s_proj2, t + 1)
                last = mark(v.tensor_tensor(y1[:, t, :], xb[:, t, :], bank[2 + t][:, 0:D], ALU.add))
            dve.wait_ge(s_dve, last)
            moments(y1, s_var1)
            dve.wait_ge(s_rstd1, 1)
            dve.wait_ge(s_var1, 1)
            for t in range(NT):
                last = mark(v.tensor_scalar(y1[:, t, :], y1[:, t, :], mv[:, t, 0:1], rstd[:, t:t + 1],
                                            ALU.subtract, ALU.mult))
            dve.wait_ge(s_dve, last)
            own(v.tensor_tensor(y1[:], y1[:], spread(R("gamma"), 1, NT), ALU.mult))
            dve.wait_ge(s_x3b, 1)
            v.tensor_tensor(x_tok[:], x_tok[:], y1[:], ALU.add).then_inc(s_x, 1)
            dve.wait_ge(s_x, 4)

            dve.wait_ge(s_ea1, 1)
            own(v.tensor_scalar(da1[:, 0:1], da1[:, 0:1], 1.0, None, ALU.add))
            own(v.reciprocal(da1[:, 1:2], da1[:, 0:1]))
            own(v.tensor_copy(dec1[0:N, :], da1[:, 1:2].broadcast_to([N, TOK])))
            mark(v.memset(dec1[0:N, :].rearrange("p (b t) -> p b t", t=T)[:, :, 0:1], 0.0))
            normalise(5)
            for c in range(4):
                dve.wait_ge(s_in_ps, c + 1)
                xm = bank[c][:].rearrange("p (b t) -> p b t", t=T)
                xo = xc1[:, c, :].rearrange("p (b t) -> p b t", t=T)
                own(v.tensor_scalar(xo, xm, L("conv1", 3 * c + 1), L("conv1b", c), ALU.mult, ALU.add))
                own(v.scalar_tensor_tensor(xo[:, :, 1:T], xm[:, :, 0:T - 1], L("conv1", 3 * c), xo[:, :, 1:T],
                                           ALU.mult, ALU.add))
                v.scalar_tensor_tensor(xo[:, :, 0:T - 1], xm[:, :, 1:T], L("conv1", 3 * c + 2), xo[:, :, 0:T - 1],
                                       ALU.mult, ALU.add).then_inc(s_cv1, 1)
            dve.wait_ge(s_bc1, 1)
            own(v.tensor_tensor_scan(st1[0:N, :], dec1[0:N, :], bank[4][0:N, :], 0.0, ALU.mult, ALU.add))
            v.tensor_tensor(pr1[0:N, :], st1[0:N, :], bank[5][0:N, :], ALU.mult).then_inc(s_pr1, 1)
            dve.wait_ge(s_ys, 1)
            for c in range(4):
                last = mark(v.scalar_tensor_tensor(y2[:, c, :], xs1[:, c, :], L("D1", c), bank[6][:], ALU.mult, ALU.add))
            dve.wait_ge(s_dve, last)
            for c in range(4):
                v.tensor_tensor(y2[:, c, :], y2[:, c, :], sres[:, c, :], ALU.mult).then_inc(s_y2, 1)
            for t in range(NT):
                dve.wait_ge(s_proj3, t + 1)
                ins = v.tensor_tensor(x_tok[:, t, :], x_tok[:, t, :], bank[t][:, 0:D], ALU.add)
                if t < NT - 1:
                    mark(ins)
            ins.then_inc(s_x, 1)
            dve.wait_ge(s_x, 5)
            dve.wait_ge(s_dve, steps[0])

            v.memset(hid[0], 0.0).then_inc(s_hid, 2)
            dve.wait_ge(s_hid, 2)
            normalise(6)
            dve.wait_ge(s_xnT, 2 * 6)
            for c in range(NC):
                dve.wait_ge(s_xhi, c + 1)
                v.tensor_tensor(xlo[:, c, :], xnT[:, c, :], xhi[:, c, :].bitcast(f32), ALU.subtract).then_inc(s_xlo, 1)
            dve.wait_ge(s_lg, 1)
            v.tensor_copy(gtmp[:], bank[4][:, 0:NT * E].rearrange("p (t e) -> p t e", e=E)).then_inc(s_ofree, NT)
            dve.wait_ge(s_ofree, NT)
            for t in range(NT):
                last = mark(v.max(m8[:, t, :], gtmp[:, t, :]))
            dve.wait_ge(s_dve, last)
            v.tensor_tensor(g2[:, :, 0], m8[:, :, 1], m8[:, :, 0], ALU.subtract).then_inc(s_gd, 1)
            for t in range(NT):
                last = mark(v.max_index(i8[:, t, :], m8[:, t, :], gtmp[:, t, :]))
            dve.wait_ge(s_dve, last)
            own(v.tensor_copy(ixf[:], i8[:, :, 0:2]))
            dve.wait_ge(s_ge1, 1)
            own(v.tensor_scalar(g2[:, :, 2], g2[:, :, 1], 1.0, None, ALU.add))
            own(v.reciprocal(g2[:, :, 2], g2[:, :, 2]))
            own(v.tensor_tensor(g2[:, :, 1], g2[:, :, 1], g2[:, :, 2], ALU.mult))
            for t in range(NT):
                last = mark(v.tensor_scalar(gt[:, t, :], C("iota"), ixf[:, t, 0:1], g2[:, t, 2:3], ALU.is_equal, ALU.mult))
                last = mark(v.tensor_scalar(gtmp[:, t, :], C("iota"), ixf[:, t, 1:2], g2[:, t, 1:2], ALU.is_equal, ALU.mult))
            dve.wait_ge(s_dve, last)
            v.tensor_tensor(gt[:], gt[:], gtmp[:], ALU.add).then_inc(s_gate, 1)
            dve.wait_ge(s_gate, 1)

            def gather(j, k):
                for t in range(NT):
                    if t < NT - 1:
                        dve.wait_ge(s_o_ps, 6 * j + (3 * k + t + 1))
                    else:
                        dve.wait_ge(s_hfree, 12 * j + (6 * k + 8))
                    dve.wait_ge(s_ofree, 8 * j + (4 * k + t + 1))
                    e = 2 * j + k
                    g = gt[:, t, e:e + 1] if isinstance(j, int) else gt[:, t, bass.ds(e, 1)]
                    v.scalar_tensor_tensor(x_tok[:, t, :], bank[4 + t][:, 0:D], g, x_tok[:, t, :],
                                           ALU.mult, ALU.add).then_inc(s_ofree, 1)

            def expert(j, k, split):
                for f in range(6):
                    q, i, w = 6 * k + f, f % 2, F1C[f]
                    dve.wait_ge(s_sg, 12 * j + (q + 1))
                    v.tensor_tensor(hid[i][0:w, :], sg[i][0:w, :], bank[2 * i + 1][0:w, :], ALU.mult).then_inc(s_hid, 1)
                    dve.wait_ge(s_hid, 12 * j + (q + 3))
                    dve.wait_ge(s_hfree, 12 * j + (q + 1))
                    v.tensor_copy(hhi[i][0:w, :], hid[i][0:w, :]).then_inc(s_hhi, 1)
                    dve.wait_ge(s_hhi, 12 * j + (q + 1))
                    v.tensor_tensor(hlo[i][0:w, :], hid[i][0:w, :], hhi[i][0:w, :].bitcast(f32),
                                    ALU.subtract).then_inc(s_hlo, 1)
                    if f == 0 and k == 1:
                        gather(j, 0)
                    if split and 1 <= f <= PIECES:
                        split_low(1 - k, f - 1, 2 * PIECES * j + (PIECES * k + PIECES + f))

            with dve.Fori(0, E // 2 - 1) as j:
                for k in range(2):
                    expert(j, k, True)
                gather(j, 1)
            for k in range(2):
                expert(E // 2 - 1, k, k == 0)
            gather(E // 2 - 1, 1)
            dve.wait_ge(s_ofree, 4 + 4 * E)
            v.memset(stats[:, 0, 0:1], 0.0).then_inc(s_x, 1)

        @block.tensor
        def _(pe):
            te = nc.tensor
            mm = te.matmul

            def transposes(n):
                for t in range(NT):
                    pe.wait_ge(s_xn, NT * (n - 1) + t + 1)
                    for c in range(NC):
                        last = te.transpose(bank[6 + c][:, 128 * t:128 * t + 128], xn[:, t, 128 * c:128 * c + 128], ident)
                last.then_inc(s_xnT_ps, 1)
                pe.wait_ge(s_xnT, 2 * n)

            def project(dst, w, moving, m=0):
                for d in range(NC):
                    last = mm(dst, w[:, d, m:m + 128], moving[:, d, :], start=(d == 0), stop=(d == NC - 1))
                return last

            def token_major(dst, src, w, t, n=NC, at=0):
                for d in range(n):
                    last = mm(dst[:, at:at + D], src[:, d, 128 * t:128 * t + 128], w[:, d, :], start=(d == 0), stop=(d == n - 1))
                return last

            pe.wait_ge(s_in, IN)
            for c in range(NC):
                project(bank[c][:], wx0[:, 1], c0T, 128 * c).then_inc(s_k_ps, 1)
            for t in range(NT):
                last = token_major(bank[2 + t // 2], c0T, wx0[:, 2], t, at=D * (t % 2))
            last.then_inc(s_v_ps, 1)
            transposes(1)
            pe.wait_ge(s_kb, 4)
            for c in range(NC):
                project(bank[c][:], wx0[:, 0], xnT, 128 * c).then_inc(s_q_ps, 1)
            pe.wait_ge(s_qT, 2)
            pe.wait_ge(s_vbd, 8)
            for r in range(2):
                banks = [2, 3, 4, 5] if r == 0 else [6, 7, 0, 1]
                for j in range(4):
                    for tt in range(2):
                        for h in range(2):
                            b = 4 * r + 2 * tt + h
                            for c in range(NC):
                                at = 256 * tt + 128 * c
                                last = mm(bank[banks[j]][64 * h:64 * h + 64, at:at + 128],
                                          qT[32 * j:32 * j + 32, c, T * b:T * b + T],
                                          kb2[32 * j:32 * j + 32, c, b, :, :], start=True, stop=True)
                    last.then_inc(s_sc_ps, 1)
            for r in range(2):
                banks = [2, 3, 4, 5] if r == 0 else [6, 7, 0, 1]
                for j in range(4):
                    pe.wait_ge(s_exp, 4 * r + j + 1)
                    for tt in range(2):
                        for c in range(NC):
                            at = 256 * tt + 128 * c
                            last = te.transpose(bank[banks[j]][:, at:at + 128], P[:, 2 * r + tt, j, 128 * c:128 * c + 128],
                                                ident)
                    last.then_inc(s_PT_ps, 1)
            pe.wait_ge(s_PT, 8)
            for t in range(NT):
                for h in range(2):
                    for c in range(NC):
                        for j in range(4):
                            n = 4 * c + j
                            last = mm(bank[2 + t][64 * h:64 * h + 64, 34 * n:34 * n + 34],
                                      PT[:, t, j, 128 * c + 64 * h:128 * c + 64 * h + 64],
                                      vbd[:, 2 * t + h, n, :], start=True, stop=True)
                last.then_inc(s_pv, 1)
            pe.wait_ge(s_sum_act, 8)
            pe.wait_ge(s_sum_dve, 8)
            for d in range(NC):
                last = mm(bank[0][0:B, 0:D], csum[:, d, :], wx0[:, 2, d, :], start=(d == 0), stop=(d == 1))
            last.then_inc(s_vr, 1)
            pe.wait_ge(s_vr8, 1)
            for t in range(NT):
                last = mm(bank[t // 2][:, D * (t % 2):D * (t % 2) + D], C("batch", 128 * t, 128, p=B), vr8[0:B, :],
                          start=True, stop=True)
            last.then_inc(s_vrb, 1)
            for t in range(NT):
                pe.wait_ge(s_o, t + 1)
                for c in range(NC):
                    last = te.transpose(bank[6 + c][:, 128 * t:128 * t + 128], oa[:, t, 128 * c:128 * c + 128], ident)
            last.then_inc(s_oT_ps, 1)
            pe.wait_ge(s_oT, 2)
            for t in range(NT):
                token_major(bank[t], oT, wx0[:, 3], t).then_inc(s_proj0, 1)

            transposes(2)
            pe.wait_ge(s_w, 16 * 3)
            pe.wait_ge(s_x, 1)
            for c in range(NC):
                project(bank[c][:], wm0[:, 1], xnT, 128 * c).then_inc(s_m0_ps, 1)
            pe.wait_ge(s_xc0, 2)
            for c in range(NC):
                project(bank[2 + c][:], wm0[:, 0], xc, 128 * c).then_inc(s_m0_ps, 1)
            for d in range(NC):
                last = mm(bank[4][0:2 * N, :], wbc0[:, d, :], xc[:, d, :], start=(d == 0), stop=(d == 1))
            last.then_inc(s_bc_ps, 1)
            pe.wait_ge(s_bcs, 2)
            pe.wait_ge(s_sel, 1)
            pe.wait_ge(s_loop, 1)
            pe.wait_ge(s_yadd, 8)
            pe.sem_inc(s_kfree, 2)
            with pe.Fori(0, B // 2) as j:
                for k in range(2):
                    def broadcast_b(m):
                        n = 4 * j + (2 * k + m)
                        pe.wait_ge(s_ssm, 6 * n + 8)
                        mm(bank[6][:], sel[:, bass.ds(n, 1), :].rearrange("p o m -> p (o m)"), bcs[:],
                           start=True, stop=True).then_inc(s_B, 1)

                    def broadcast_c(m):
                        n = 4 * j + (2 * k + m)
                        pe.wait_ge(s_ssm, 6 * n + 12)
                        mm(bank[7][:], sel[:, bass.ds(n + N, 1), :].rearrange("p o m -> p (o m)"), bcs[:],
                           start=True, stop=True).then_inc(s_C, 1)

                    pe.wait_ge(s_ctxT[k], 16 * j + 32)
                    for g in range(G + 1):
                        if g == 0:
                            broadcast_b(0)
                        if g < G:
                            i = (G * k + g) % 2
                            gg = 2 * G * j + (G * k + g)
                            pe.wait_ge(s_z, gg + 1)
                            for a in range(2 if g < G - 1 else 1):
                                kt = 2 * g + a
                                p = 128 if kt < KT - 1 else KLAST
                                for d in range(NC):
                                    last = mm(bank[i][0:p, D * a:D * a + D], cT[k][:, d, 128 * kt:128 * kt + p],
                                              wx1[:, 1, d, :], start=(d == 0), stop=(d == 1))
                            last.then_inc(s_kp, 1)
                        if g:
                            gg = 2 * G * j + (G * k + g - 1)
                            i = (G * k + g - 1) % 2
                            if g == 1:
                                pe.wait_ge(s_ctxN[k], 16 * j + 16)
                                pe.wait_ge(s_ktc, 4 * j + (2 * k + 2))
                            pe.wait_ge(s_kt, gg + 3)
                            for a in range(2 if g < G else 1):
                                kt = 2 * (g - 1) + a
                                p = 128 if kt < KT - 1 else KLAST
                                for c in range(NC):
                                    last = mm(bank[2 + 2 * k + c][:, 0:D + 1], kk[i][0:p, D * a + 128 * c:D * a + 128 * c + 128],
                                              cN[k][0:p, kt, :], start=(kt == 0), stop=(kt == KT - 1))
                            last.then_inc(s_kfree, 1)
                        if g == 1:
                            broadcast_c(0)
                        if g == 2:
                            broadcast_b(1)
                        if g == 4:
                            broadcast_c(1)
            pe.wait_ge(s_yg, 2)
            for t in range(NT):
                token_major(bank[t], ym, wm0[:, 2], t).then_inc(s_proj1, 1)

            transposes(3)
            pe.wait_ge(s_ms, 2)
            pe.wait_ge(s_w2, 16 * 6)
            pe.wait_ge(s_x, 2)
            for d in range(NC):
                last = mm(bank[0][0:B, 0:E], msum[:, d, :], wr[:, d, :], start=(d == 0), stop=(d == 1))
            last.then_inc(s_rt_ps, 1)
            pe.wait_ge(s_topf, 1)
            te.transpose(bank[1][0:1, 0:B], topf[:], C("ident", 0, B, p=B)).then_inc(s_topT, 1)
            pe.wait_ge(s_hot, 1)
            mm(bank[2][0:E, :], hot[:], C("batch", p=B), start=True, stop=True).then_inc(s_hot_ps, 1)
            pe.wait_ge(s_hott, 1)

            def hidden0(t):
                for i in range(2):
                    for h in range(2):
                        b = 2 * t + h
                        k = b % 4
                        if i == 0:
                            pe.wait_ge(s_wa0[k], 16 * (b // 4 + 1))
                        if t >= 2:
                            pe.wait_ge((s_hf0, s_hf1)[i], t - 1)
                        for d in range(NC):
                            at = F0 * d + 512 * i
                            last = mm(bank[2 * (t % 2) + i][64 * h:64 * h + 64, :], xnT[:, d, T * b:T * b + T],
                                      wf0[k][:, at:at + 512], start=(d == 0), stop=(d == 1))
                    last.then_inc(s_h_ps, 1)

            hidden0(0)
            for t in range(NT):
                if t < NT - 1:
                    hidden0(t + 1)
                pe.wait_ge(s_hf0, t + 1)
                pe.wait_ge(s_hf1, t + 1)
                if t:
                    pe.wait_ge(s_hb, 4 * t)
                for f in range(8):
                    last = te.transpose(bank[4 + f // 4][:, 128 * (f % 4):128 * (f % 4) + 128],
                                        hf[t % 2][:, 128 * f:128 * f + 128], ident)
                last.then_inc(s_hT_ps, 1)
                mm(bank[6 + t % 2][:, 0:D], hott[0:E, 128 * t:128 * t + 128], b2t[:], start=True, stop=False)
                for i in range(2):
                    pe.wait_ge(s_hr, 2 * t + i + 1)
                    for h in range(2):
                        k = (2 * t + h) % 4
                        pe.wait_ge(s_wb0[k], 16 * (t // 2 + 1))
                        for f in range(4 * i, 4 * i + 4):
                            at = NC * F0 + D * f
                            last = mm(bank[6 + t % 2][64 * h:64 * h + 64, 0:D], hr[t % 2][:, f, T * h:T * h + T],
                                      wf0[k][:, at:at + D], start=False, stop=(f == 7))
                last.then_inc(s_y_ps, 1)

            transposes(4)
            pe.wait_ge(s_x, 3)
            for c in range(NC):
                project(bank[c][:], wx1[:, 0], xnT, 128 * c).then_inc(s_q1_ps, 1)
            pe.wait_ge(s_Q1, 2)
            pe.wait_ge(s_ktc, 4 + 2 * B)
            for m in range(NC + 1):
                for b in range(B):
                    for e in range(NC):
                        w = 128 if m < NC else 1
                        last = mm(bank[2 + m][0:w, T * b:T * b + T], ktc[:, b, e, 128 * m:128 * m + w],
                                  QT[:, e, T * b:T * b + T], start=(e == 0), stop=(e == 1))
                last.then_inc(s_G_ps, 1)
            pe.wait_ge(s_GT, 3)
            for c in range(NC):
                for d in range(NC):
                    mm(bank[c][:], wx1[:, 2, d, 128 * c:128 * c + 128], GT[:, d, :], start=(d == 0), stop=False)
                mm(bank[c][:], R("bv1", p=1)[:, 128 * c:128 * c + 128], sr[0:1, :], start=False, stop=True).then_inc(s_num, 1)
            pe.wait_ge(s_aT, 2)
            for t in range(NT):
                token_major(bank[2 + t], aT, wx1[:, 3], t).then_inc(s_proj2, 1)

            transposes(5)
            for m in range(8):
                project(bank[m][:], win, xnT, 128 * m).then_inc(s_in_ps, 1)
            pe.wait_ge(s_xs1, 4)
            pe.wait_ge(s_res, 4)
            for h in range(2):
                for i in range(4):
                    last = mm(bank[4 + h][0:N, :], wbc1[:, i, N * h:N * h + N], xs1[:, i, :], start=(i == 0), stop=(i == 3))
            last.then_inc(s_bc1, 1)
            pe.wait_ge(s_pr1, 1)
            mm(bank[6][:], C("ones", p=N), pr1[0:N, :], start=True, stop=True).then_inc(s_ys, 1)
            pe.wait_ge(s_y2, 4)
            for t in range(NT):
                token_major(bank[t], y2, wout, t, 4).then_inc(s_proj3, 1)

            transposes(6)
            for t in range(NT):
                for d in range(NC):
                    last = mm(bank[4][:, E * t:E * t + E], xnT[:, d, 128 * t:128 * t + 128], wg1[:, d, :],
                              start=(d == 0), stop=(d == 1))
            last.then_inc(s_lg, 1)
            pe.wait_ge(s_xlo, 2)
            pe.sem_inc(s_hfree, 2)

            def hidden(j, q):
                i, k, f = q % 2, q // 6, q % 6
                w = F1C[f]
                if f == 0:
                    pe.wait_ge(s_wlo, 2 * PIECES * j + PIECES * (k + 1))
                pe.wait_ge(s_hid, 12 * j + (q + 1))
                for h in range(2):
                    for d in range(NC):
                        at = (NC * h + d) * F1 + 128 * f
                        hi, lo = whi[k][:, at:at + w], wlo[k][:, at:at + w]
                        for p, (a, b) in enumerate(((hi, xhi), (hi, xlo), (lo, xhi))):
                            last = mm(bank[2 * i + h][0:w, :], a, b[:, d, :], start=(d == 0 and p == 0),
                                      stop=(d == 1 and p == 2))
                last.then_inc(s_h12, 1)

            def output(j, q):
                i, k, f = q % 2, q // 6, q % 6
                w = F1C[f]
                at = 2 * NC * F1 + f * D
                hi, lo = whi[k][0:w, at:at + D], wlo[k][0:w, at:at + D]
                for t in range(NT):
                    if f == 0:
                        pe.wait_ge(s_ofree, 8 * j + (4 * k + t + 1))
                    if t == 0:
                        pe.wait_ge(s_hlo, 12 * j + (q + 1))
                    for p, (a, b) in enumerate(((hhi, hi), (hhi, lo), (hlo, hi))):
                        last = mm(bank[4 + t][:, 0:D], a[i][0:w, 128 * t:128 * t + 128], b,
                                  start=(f == 0 and p == 0), stop=(f == 5 and p == 2))
                    if f == 5 and t < NT - 1:
                        last.then_inc(s_o_ps, 1)
                last.then_inc(s_hfree, 1)

            with pe.Fori(0, E // 2) as j:
                hidden(j, 0)
                for q in range(12):
                    if q < 11:
                        hidden(j, q + 1)
                    output(j, q)


_OUT = ((128, NT, D), "float32")


def kernel(**inputs):
    import ml_dtypes
    import numpy as np
    import concourse.bacc as bacc
    from concourse import mybir
    from concourse.bass_utils import run_bass_kernel_spmd

    a = {k: np.asarray(v) for k, v in inputs.items()}

    def feature_rows(w, n):
        return w.reshape(n, 128, -1).transpose(1, 0, 2)

    def columns(v):
        return v.reshape(-1, 128).T

    ctx = np.concatenate([a["ctx_1024"][:, T:], a["ctx_1024"][:, :T]], axis=1)
    ctx_t = ctx.transpose(0, 2, 1).reshape(B, NC, 128, S).transpose(0, 2, 1, 3)
    ctx_n = np.zeros((B, KT * 128, D), np.float32)
    ctx_n[:, :S] = ctx
    ctx_n = ctx_n.reshape(B, KT, 128, D).transpose(0, 2, 1, 3)
    first = a["ctx_1024"][:, :T].reshape(TOK, D).T

    a1 = np.zeros((128, 1), np.float32)
    a1[:N, 0] = a["L1_attn_A"]
    cols = {
        "bq0": columns(a["L0_xattn_bq"]), "bk0": columns(a["L0_xattn_bk"]), "bv0": columns(a["L0_xattn_bv"]),
        "conv0": feature_rows(a["L0_attn_conv_w"].reshape(D, 4), 2).reshape(128, 8),
        "conv0b": columns(a["L0_attn_conv_b"]), "bd": columns(a["L0_attn_bd"]), "bg": columns(a["L0_attn_bg"]),
        "log_a": feature_rows(a["L0_attn_log_a"], 2).reshape(128, 32), "bq1": columns(a["L1_xattn_bq"]),
        "conv1": feature_rows(a["L1_attn_conv_w"].reshape(DI, 3), 4).reshape(128, 12),
        "conv1b": columns(a["L1_attn_conv_b"]), "D1": columns(a["L1_attn_D"]), "A1": a1}
    rows = {"bo0": a["L0_xattn_bo"], "boa": a["L0_attn_bo"], "bk1": a["L1_xattn_bk"], "bv1": a["L1_xattn_bv"],
            "bo1": a["L1_xattn_bo"], "gamma": a["L1_xattn_gamma"], "beta": a["L1_xattn_beta"], "br": a["L0_ffn_br"]}

    p = np.arange(128)
    batch = np.zeros((128, NT, 128), np.float32)
    for t in range(NT):
        batch[2 * t + p // 64, t, p] = 1
    state = np.zeros((128, 2 * N), np.float32)
    state[p[:96], p[:96] % 32] = 1
    consts = {
        "ident": np.eye(128, dtype=np.float32),
        "causal": np.where(np.arange(T)[None] > (p % T)[:, None], -FMAX, 0).astype(np.float32),
        "parity": np.stack([(p // HD) % 2 == 0, (p // HD) % 2 == 1], 1).astype(np.float32),
        "iota": np.tile(np.arange(E, dtype=np.float32), (128, 1)),
        "eps": np.full((128, 1), 1e-5, np.float32), "one": np.ones((128, 1), np.float32),
        "minus1": np.full((128, 1), -1, np.float32), "batch": batch.reshape(128, -1), "state": state,
        "ones": np.ones((128, 128), np.float32)}

    def three(*names):
        return np.stack([feature_rows(a[n].T, 2) for n in names], 1)

    w0 = np.concatenate([
        a["L0_ffn_W1"].reshape(E, NC, 128, F0).transpose(0, 2, 1, 3).reshape(E, 128, -1),
        a["L0_ffn_W2"].reshape(E, 8, 128, D).transpose(0, 2, 1, 3).reshape(E, 128, -1),
        a["L0_ffn_b1"].reshape(E, 8, 128).transpose(0, 2, 1)], 2)
    w3 = np.zeros((E, 6 * 128, D), np.float32)
    w3[:, :F1] = a["L1_ffn_W3"].transpose(0, 2, 1)
    w1 = np.concatenate(
        [a[n].transpose(0, 2, 1).reshape(E, NC, 128, F1).transpose(0, 2, 1, 3).reshape(E, 128, -1)
         for n in ("L1_ffn_W1", "L1_ffn_W2")] + [w3.reshape(E, 6, 128, D).transpose(0, 2, 1, 3).reshape(E, 128, -1)], 2)

    arrays = {
        "x": a["x"].reshape(NT, 128, D).transpose(1, 0, 2),
        "first_ctx": feature_rows(first, 2), "ctx_t": ctx_t, "ctx_n": ctx_n,
        "mask": a["mask_BxS2_bf0"][:, :T],
        "cols": np.concatenate([cols[n] for n in COLS], 1),
        "rows": np.concatenate([rows[n] for n in ROWS])[None],
        "consts": np.concatenate([consts[n] for n in CONSTS], 1),
        "w_x0": three("L0_xattn_Wq", "L0_xattn_Wk", "L0_xattn_Wv", "L0_xattn_Wo"),
        "w_m0": three("L0_attn_Wd", "L0_attn_Wg", "L0_attn_Wo"),
        "w_bc0": feature_rows(np.concatenate([a["L0_attn_Wb"], a["L0_attn_Wc"]], 0).T, 2),
        "w_r": feature_rows(a["L0_ffn_Wr"], 2), "w0": w0,
        "b_f0": a["L0_ffn_b2"],
        "w_x1": three("L1_xattn_Wq", "L1_xattn_Wk", "L1_xattn_Wv", "L1_xattn_Wo"),
        "w_in": feature_rows(a["L1_attn_W_in"], 2), "w_out": feature_rows(a["L1_attn_W_out"], 4),
        "w_bc1": feature_rows(np.concatenate([a["L1_attn_W_B"], a["L1_attn_W_C"]], 1), 4),
        "w_g1": feature_rows(a["L1_ffn_Wg"].T, 2), "w1": w1}

    nc = bacc.Bacc("TRN2", target_bir_lowering=False, num_devices=1)
    fed, args = {}, []
    for name, v in arrays.items():
        v = np.ascontiguousarray(v)
        fed[f"in_{name}"] = v
        args.append(nc.dram_tensor(f"in_{name}", v.shape, mybir.dt.from_np(v.dtype), kind="ExternalInput").ap())
    shape, dtype = _OUT
    out = nc.dram_tensor("out", shape, mybir.dt.from_np(np.dtype(dtype)), kind="ExternalOutput").ap()
    perceiver(nc, *args, out)
    got = run_bass_kernel_spmd(nc, [fed], core_ids=[0]).results[0]["out"]
    return np.asarray(got).transpose(1, 0, 2).reshape(B, T, D)
```

```python
from contextlib import ExitStack

import concourse.bass as bass
import numpy as np
from concourse import mybir

B, T, D = 8, 64, 256
S = 1601
TOK = B * T
NT = TOK // 128
NC = D // 128
REST = S - T
KT = -(-S // 128)
KLAST = S - (KT - 1) * 128
G = 7
H, HD = 16, 16
N = 16
E = 8
F0 = 1024
F1 = 682
F1C = [128] * 5 + [F1 - 5 * 128]
TAIL = 108
DI = 512
FMAX = float(np.finfo(np.float32).max)



def _places(sizes):
    at, out = 0, {}
    for name, n in sizes:
        out[name] = (at, n)
        at += n
    return out, at


COLS, NCOLS = _places([
    ("bq0", 2), ("bk0", 2), ("bv0", 2), ("conv0", 8), ("conv0b", 2), ("bd", 2), ("bg", 2),
    ("log_a", 32), ("bq1", 2), ("conv1", 12), ("conv1b", 4), ("D1", 4), ("A1", 1)])
ROWS, NROWS = _places([
    ("bo0", D), ("boa", D), ("bk1", D), ("bv1", D), ("bo1", D), ("gamma", D), ("beta", D), ("br", E)])
CONSTS, NCONSTS = _places([
    ("ident", 128), ("causal", T), ("parity", 2), ("iota", E), ("eps", 1), ("one", 1), ("minus1", 1),
    ("batch", NT * 128), ("half", 2), ("ones", 128)])
W0SPLIT = NC * F0 + F0 // 128
W0N = W0SPLIT + (F0 // 128) * D
W1AT = 5 * 2 * NC * 128 + NC * TAIL
W1N = W1AT + 6 * D
BCW = 48
PIECES = 4
WP = W1N // PIECES
ARENA = 2 * W0N + 2 * W1N
WORK = 14720
NAT = KT * (D + 1)
CTT = NC * S
PITCH = (NAT + 7) // 8 * 8


def perceiver(nc, x, first_ctx, ctx_t, ctx_n, mask, cols, rows, consts, w_x0, w_m0, state, w_bc0, w_r, w0, b_f0,
              w_x1, w_in, w_out, w_bc1, w_g1, w1, out):
    f32, bf16, u8, u32 = mybir.dt.float32, mybir.dt.bfloat16, mybir.dt.uint8, mybir.dt.uint32
    i32, f32r = mybir.dt.int32, mybir.dt.float32r
    ALU, ACT, AX = mybir.AluOpType, mybir.ActivationFunctionType, mybir.AxisListType
    ctx = ExitStack()

    def sb(name, shape, dt=f32):
        return ctx.enter_context(nc.sbuf_tensor(name, shape, dt))

    def over(name, base, at, *shape):
        return nc.alloc_sbuf_tensor_at(name, [128, *shape], f32r, offset=base + 4 * at)

    def sem(name):
        return ctx.enter_context(nc.semaphore(name))

    def spread(ap, axis, n):
        ap = ap.unsqueeze(axis)
        shape = list(ap.shape)
        shape[axis] = n
        return ap.broadcast_to(shape)

    def one(n):
        return slice(n, n + 1) if isinstance(n, int) else bass.ds(n, 1)

    with ctx:
        x_tok = sb("x_tok", [128, NT, D])
        xb = sb("xb", [128, NT, D])
        xn = sb("xn", [128, NT, D])
        xnT = sb("xnT", [128, NC, TOK])
        stats = sb("stats", [128, NT, 6])
        mv = sb("mv", [128, NT, 2])
        lnv = sb("lnv", [128, NT])
        rstd = sb("rstd", [128, NT])
        cst = sb("cst", [128, NCONSTS])
        col = sb("col", [128, NCOLS])
        row = sb("row", [128, NROWS])
        wx0 = sb("wx0", [128, 4, NC, D])
        wx0_at = nc.sbuf_base - 4 * 4 * NC * D
        wm0 = sb("wm0", [128, 3, NC, D])
        wbc0 = sb("wbc0", [128, NC, 2 * N])
        wr = sb("wr", [128, NC, E])
        wx1 = sb("wx1", [128, 4, NC, D])
        late = sb("late", [128, 2 * NC * DI + DI // 128 * (D + BCW) + NC * E])
        late_at = nc.sbuf_base - 4 * late.shape[1]
        win = late[:, 0:2 * NC * DI].rearrange("p (c n) -> p c n", c=NC)
        at = 2 * NC * DI
        wout = late[:, at:at + DI // 128 * D].rearrange("p (c n) -> p c n", n=D)
        at += DI // 128 * D
        wbc1 = late[:, at:at + DI // 128 * BCW].rearrange("p (c n) -> p c n", n=BCW)
        at += DI // 128 * BCW
        wg1 = late[:, at:].rearrange("p (c n) -> p c n", n=E)
        arena_work = sb("arena_work", [128, ARENA + WORK])
        arena_at = nc.sbuf_base - 4 * (ARENA + WORK)
        arena = arena_work[:, 0:ARENA]
        cT = [arena[:, k * PITCH:k * PITCH + CTT].rearrange("p (c s) -> p c s", c=NC) for k in range(2)]
        cN = [arena[:, (2 + k) * PITCH:(2 + k) * PITCH + NAT].rearrange("p (k d) -> p k d", d=D + 1) for k in range(2)]
        cT2 = [arena[:, (2 + k) * PITCH:(2 + k) * PITCH + CTT].rearrange("p (c s) -> p c s", c=NC) for k in range(2)]
        wf0 = [arena[:, k * W0N:(k + 1) * W0N] for k in range(4)]
        wf1 = [arena[:, k * W1N:(k + 1) * W1N] for k in range(2)]
        tail = arena[:, 4 * PITCH:4 * PITCH + 6 * 512]
        inp = [tail[:, c * 512:(c + 1) * 512] for c in range(NC)]
        hst = [tail[:, (2 + c) * 512:(3 + c) * 512] for c in range(NC)]
        zk = [tail[:, (4 + k) * 512:(5 + k) * 512] for k in range(2)]
        ktc = sb("ktc", [128, B, NC, D + 1])
        work = arena_work[:, ARENA:]

        def area(at, *shape):
            n = int(np.prod(shape))
            v = work[:, at:at + n]
            names = "abcd"[:len(shape)]
            if len(shape) == 1:
                return v
            return v.rearrange(f"p ({' '.join(names)}) -> p {' '.join(names)}",
                               **{k: s for k, s in zip(names[1:], shape[1:])})

        c0T = area(0, NC, TOK)
        qT = area(1024, NC, TOK)
        kb2 = area(2048, NC, B, 2, T)
        vbd = area(4096, B, 8, 34)
        P = area(6272, NT, 4, 256)
        PT = area(10368, NT, 4, 256)
        vr8 = area(14464, D)
        maskf = sb("maskf", [128, NT, T])
        mask8 = sb("mask8", [128, NT, T], u8)
        csum = sb("csum", [128, NC, B])
        mx = sb("mx", [128, NT, 4, 4])
        rest = sb("rest", [128, NT, 4, 4])
        den = sb("den", [128, NT, H])
        vro = area(6272, NT, D)
        oa = area(6272 + 1024, NT, D)
        oT = area(1024, NC, TOK)
        xc = area(0, NC, TOK)
        dt = area(1024, NC, TOK)
        dtx = area(2048, NC, TOK)
        gate = area(3072, NC, TOK)
        dec = [[area(4096 + (2 * m + c) * 512, 512) for c in range(NC)] for m in range(2)]
        hc = [[area(6144 + (2 * m + c) * 512, 512) for c in range(NC)] for m in range(2)]
        ym = area(8192, NC, TOK)
        ek = [area(9216 + k * 512, 512) for k in range(2)]
        kk = [area(10240 + k * 512, 512) for k in range(2)]
        tmp = area(11264, NC, TOK)
        r1 = area(12800, 512)
        chi = over("chi", late_at, 0, NC, S)
        clo = [over(f"clo{k}", arena_at, k * PITCH, NC, S) for k in range(2)]
        wkhi, wklo = (over(f"wk_part{k}", arena_at, ARENA + 13312 + k * NC * D, NC, D) for k in range(2))
        aneg = sb("aneg", [128, NC, N])
        bcs = sb("bcs", [96, TOK], bf16)
        mid = sb("mid", [32, TOK], bf16)
        sel = wx0[0:96, :, :, :].rearrange("p a b c -> p (a b c)").bitcast(bf16).rearrange("p (n m) -> p n m", m=128)
        msum = sb("msum", [128, NC, B])
        sc = sb("sc", [B, E])
        m8 = sb("m8", [128, NT, 8])
        i8 = sb("i8", [128, NT, 8], u32)
        topf = sb("topf", [B, 1])
        hot = sb("hot", [B, E])
        top = sb("top", [1, B], i32)
        b2t = sb("b2t", [E, D])
        hf = [area(k * F0, F0) for k in range(2)]
        hb = [area(2048 + k * F0, 8, 128) for k in range(2)]
        hr = [area(4096 + k * F0, 8, 128) for k in range(2)]
        hott = area(6144, TOK)
        QT = area(0, NC, TOK)
        z1 = area(1024, NC, TOK)
        e1 = area(2048, NC, TOK)
        Gt = area(2048, NT, D)
        GT = area(3072, NC, TOK)
        qk = area(7680, NC, TOK)
        dn = area(4608, NC, TOK)
        aT = area(5632, NC, TOK)
        y1 = area(6656, NT, D)
        sres = area(0, 4, TOK)
        xc1 = area(2048, 4, TOK)
        xs1 = area(4096, 4, TOK)
        y2 = area(6144, 4, TOK)
        st1 = area(8192, TOK)
        pr1 = area(8704, TOK)
        dec1 = area(9216, TOK)
        da1 = sb("da1", [N, 2])
        wlo = [over(f"wlo{k}", arena_at, (2 + k) * W1N, W1N) for k in range(2)]
        free = 4 * W1N - ARENA
        whi = [over(f"whi{k}", arena_at, ARENA + at, W1N) for k, at in enumerate((9728, free + 4096))]
        xhi, xlo = (over(f"x_part{k}", wx0_at, k * NC * TOK, NC, TOK) for k in range(2))
        sg = [area(free + k * 512, 512) for k in range(2)]
        hid = [area(free + 1024 + k * 512, 512) for k in range(2)]
        hhi = [over(f"hhi{k}", arena_at, ARENA + free + 2048 + k * 512, 512) for k in range(2)]
        hlo = [over(f"hlo{k}", arena_at, ARENA + free + 3072 + k * 512, 512) for k in range(2)]
        gt = sb("gt", [128, NT, E])
        gtmp = sb("gtmp", [128, NT, E])
        g2 = sb("g2", [128, NT, 3])
        ixf = sb("ixf", [128, NT, 2])

        bank = [ctx.enter_context(nc.psum_tensor(f"bank{i}", [128, 512], f32)) for i in range(8)]

        def C(name, i=0, n=None, p=128):
            a, w = CONSTS[name]
            return cst[0:p, a + i:a + (w if n is None else i + n)]

        def L(name, i=0, n=1, p=128):
            a, _ = COLS[name]
            return col[0:p, a + i:a + i + n]

        def R(name, p=128):
            a, w = ROWS[name]
            return row[0:p, a:a + w]

        ident = C("ident")

        s_k_in, s_v_in = sem("s_k_in"), sem("s_v_in")
        s_o_in = sem("s_o_in")
        s_x_in = sem("s_x_in")
        s_in = sem("s_in")
        s_w = sem("s_w")
        s_w2 = sem("s_w2")
        s_w3 = sem("s_w3")
        s_chi, s_clo = sem("s_chi"), sem("s_clo")
        s_wkhi, s_wklo = sem("s_wkhi"), sem("s_wklo")
        s_ctxT = [sem(f"s_ctxT{k}") for k in range(4)]
        s_sum_act = sem("s_sum_act")
        s_sum_dve = sem("s_sum_dve")
        s_ctxN = [sem(f"s_ctxN{k}") for k in range(2)]
        s_wa0 = [sem(f"s_wa0{k}") for k in range(4)]
        s_wb0 = [sem(f"s_wb0{k}") for k in range(4)]
        s_wf1 = [sem(f"s_wf1{k}") for k in range(2)]
        s_dve = sem("s_dve")
        s_act = sem("s_act")
        s_pool = sem("s_pool")
        s_var = sem("s_var")
        s_rstd = sem("s_rstd")
        s_xn = sem("s_xn")
        s_xnT_ps = sem("s_xnT_ps")
        s_xnT = sem("s_xnT")
        s_xb = sem("s_xb")
        s_x = sem("s_x")
        s_k_ps, s_v_ps, s_q_ps = sem("s_k_ps"), sem("s_v_ps"), sem("s_q_ps")
        s_kb, s_vbd, s_vz, s_qT = sem("s_kb"), sem("s_vbd"), sem("s_vz"), sem("s_qT")
        s_sc_ps, s_sc = sem("s_sc_ps"), sem("s_sc")
        s_mx, s_diff_pool, s_diff, s_exp = sem("s_mx"), sem("s_diff_pool"), sem("s_diff"), sem("s_exp")
        s_PT_ps, s_PT = sem("s_PT_ps"), sem("s_PT")
        s_pv, s_vr, s_vr8, s_vrb = sem("s_pv"), sem("s_vr"), sem("s_vr8"), sem("s_vrb")
        s_o, s_oT_ps, s_oT, s_proj0 = sem("s_o"), sem("s_oT_ps"), sem("s_oT"), sem("s_proj0")

        s_conv0, s_xc0 = sem("s_conv0"), sem("s_xc0")
        s_m0_ps = sem("s_m0_ps")
        s_abs = sem("s_abs")
        s_sp, s_ge, s_gate0 = sem("s_sp"), sem("s_ge"), sem("s_gate0")
        s_bc_ps, s_bcs, s_sel = sem("s_bc_ps"), sem("s_bcs"), sem("s_sel")
        s_an, s_aneg = sem("s_an"), sem("s_aneg")
        s_decay = sem("s_decay")
        s_ssm = sem("s_ssm")
        s_yadd = sem("s_yadd")
        s_B, s_C = sem("s_B"), sem("s_C")
        s_z = sem("s_z")
        s_e = sem("s_e")
        s_kt = sem("s_kt")
        s_kp = sem("s_kp")
        s_kfree = sem("s_kfree")
        s_ktc = sem("s_ktc")
        s_yg, s_proj1 = sem("s_yg"), sem("s_proj1")

        s_ms_ps = sem("s_ms_ps")
        s_ms, s_rt_ps, s_topf, s_topT, s_top = (sem("s_ms"), sem("s_rt_ps"), sem("s_topf"), sem("s_topT"),
                                                sem("s_top"))
        s_hot, s_hot_ps, s_hott = sem("s_hot"), sem("s_hot_ps"), sem("s_hott")
        s_h_ps, s_hf0, s_hf1, s_hT_ps = sem("s_h_ps"), sem("s_hf0"), sem("s_hf1"), sem("s_hT_ps")
        s_hb, s_hr, s_y_ps = sem("s_hb"), sem("s_hr"), sem("s_y_ps")

        s_q1_ps, s_z1, s_e1, s_Q1, s_G_ps, s_GT, s_num = (sem("s_q1_ps"), sem("s_z1"), sem("s_e1"), sem("s_Q1"),
                                                          sem("s_G_ps"), sem("s_GT"), sem("s_num"))
        s_qk, s_G, s_GT_ps = sem("s_qk"), sem("s_G"), sem("s_GT_ps")
        s_aT, s_proj2, s_var1, s_rstd1, s_x3b = (sem("s_aT"), sem("s_proj2"), sem("s_var1"), sem("s_rstd1"),
                                                 sem("s_x3b"))

        s_in_ps, s_res, s_cv1, s_xs1, s_bc1, s_pr1, s_ys, s_y2, s_proj3 = (
            sem("s_in_ps"), sem("s_res"), sem("s_cv1"), sem("s_xs1"), sem("s_bc1"), sem("s_pr1"), sem("s_ys"),
            sem("s_y2"), sem("s_proj3"))
        s_ea1 = sem("s_ea1")

        s_lg, s_gd, s_ge1, s_gate = sem("s_lg"), sem("s_gd"), sem("s_ge1"), sem("s_gate")
        s_whi, s_wlo = sem("s_whi"), sem("s_wlo")
        s_xhi, s_xlo = sem("s_xhi"), sem("s_xlo")
        s_h12, s_sg = sem("s_h12"), sem("s_sg")
        s_hid = sem("s_hid")
        s_hhi, s_hlo = sem("s_hhi"), sem("s_hlo")
        s_hfree = sem("s_hfree")
        s_o_ps, s_ofree = sem("s_o_ps"), sem("s_ofree")
        s_out = sem("s_out")

        block = ctx.enter_context(nc.Block())
        ORDER = [7, 6, 5, 4, 3, 2, 0, 1]
        SLOT = [2, 3, 0, 1, 2, 3, 0, 1]
        slots = [cT[0], cT[1], cT2[0], cT2[1]]
        seen = [sum(1 for j in range(i) if SLOT[j] == SLOT[i]) for i in range(8)]
        IN = 16 * 5
        AHEAD = G - 2

        def columns(q):
            return slice(256 * (q % G), min(256 * (q % G) + 256, S))

        @block.sync
        def _(sp):
            for dst, src in ((c0T, first_ctx), (wx0[:, 1], w_x0[:, 1])):
                sp.dma_start(dst, src).then_inc(s_k_in, 16)
            sp.dma_start(wx0[:, 2], w_x0[:, 2]).then_inc(s_v_in, 16)
            sp.dma_start(x_tok[:], x).then_inc(s_x_in, 16)
            for dst, src in ((cst[:], consts), (col[:], cols), (wx0[:, 0], w_x0[:, 0])):
                sp.dma_start(dst, src).then_inc(s_in, 16)
            for h in range(2):
                sp.dma_start(mask8[64 * h:64 * h + 64, :, :],
                             mask.rearrange("(t h) s -> h t s", h=2)[h].unsqueeze(0).broadcast_to([64, NT, T])
                             ).then_inc(s_in, 16)
            for i, b in enumerate(ORDER):
                if seen[i]:
                    last = max(j for j in range(i) if SLOT[j] == SLOT[i])
                    sp.wait_ge(s_sum_act, last + 1)
                    sp.wait_ge(s_sum_dve, last + 1)
                sp.dma_start(slots[SLOT[i]], ctx_t[b]).then_inc(s_ctxT[SLOT[i]], 16)
                if i == 2:
                    for dst, src in ((row[:], rows.broadcast_to([128, NROWS])), (wx0[:, 3], w_x0[:, 3])):
                        sp.dma_start(dst, src).then_inc(s_o_in, 16)
                if i == 3:
                    for dst, src in ((wm0[:], w_m0), (wbc0[:], w_bc0)):
                        sp.dma_start(dst, src).then_inc(s_w, 16)
            sp.dma_start(wx1[:], w_x1).then_inc(s_w, 16)
            sp.wait_ge(s_proj0, NT)
            sp.dma_start(sel[:], state).then_inc(s_sel, 16)
            for k in range(2):
                if k == 0:
                    sp.wait_ge(s_sum_act, 6)
                    sp.wait_ge(s_sum_dve, 6)
                sp.dma_start(cN[k][:, :, 0:D], ctx_n[k]).then_inc(s_ctxN[k], 16)
            for dst, src in ((wr[:], w_r), (b2t[:], b_f0)):
                sp.dma_start(dst, src).then_inc(s_w2, 16)
            with sp.Fori(1, B // 2) as j:
                for k in range(2):
                    sp.wait_ge(s_kp, 2 * G * j + (G * k - G))
                    sp.dma_start(cT[k], ctx_t[bass.ds(2 * j + k, 1)].rearrange("o p c s -> (o p) c s")
                                 ).then_inc(s_ctxT[k], 16)
                    sp.wait_ge(s_kfree, 2 * G * j + (G * k - G + 2))
                    sp.dma_start(cN[k][:, :, 0:D], ctx_n[bass.ds(2 * j + k, 1)].rearrange("o p k d -> (o p) k d")
                                 ).then_inc(s_ctxN[k], 16)
            sp.wait_ge(s_kp, B * G)
            for dst, src in ((win, w_in), (wout, w_out), (wbc1, w_bc1), (wg1, w_g1)):
                sp.dma_start(dst, src).then_inc(s_w3, 16)
            sp.wait_ge(s_top, 1)
            chosen = []

            def matrices(t, part):
                lo, hi = ((0, W0SPLIT), (W0SPLIT, W0N))[part]
                if t >= 2:
                    if part == 0:
                        sp.wait_ge(s_h_ps, 2 * (t - 1))
                        sp.wait_ge(s_hb, 4 * (t - 1))
                    else:
                        sp.wait_ge(s_y_ps, t - 1)
                for h in range(2):
                    b = 2 * t + h
                    if part == 0:
                        chosen.append(sp.value_load(top[0:1, b:b + 1], min_val=0, max_val=E - 1))
                    e, k = chosen[b], b % 4
                    sp.dma_start(wf0[k][:, lo:hi], w0[bass.ds(e, 1), :, lo:hi].rearrange("o p n -> (o p) n")
                                 ).then_inc((s_wa0, s_wb0)[part][k], 16)

            matrices(0, 0)
            for t in range(NT):
                if t < NT - 1:
                    matrices(t + 1, 0)
                matrices(t, 1)
            sp.wait_ge(s_y_ps, NT)
            for k in range(2):
                sp.dma_start(wf1[k], w1[k]).then_inc(s_wf1[k], 16)
            with sp.Fori(1, E // 2) as j:
                for k in range(2):
                    sp.wait_ge(s_wlo, 2 * PIECES * j + (k - 1) * PIECES)
                    sp.dma_start(wf1[k], w1[bass.ds(2 * j + k, 1)].rearrange("o p n -> (o p) n")
                                 ).then_inc(s_wf1[k], 16)
            for t in range(NT):
                sp.wait_ge(s_ofree, NT + NT * (E - 1) + t + 1)
                sp.dma_start(out[:, t, :], x_tok[:, t, :]).then_inc(s_out, 16)
            sp.wait_ge(s_out, 16 * NT)

        @block.gpsimd
        def _(pool):
            gp = nc.gpsimd

            def low_part(j, q):
                pool.wait_ge(s_chi, 2 * G * j + (q + 1))
                k, at = q // G % 2, columns(q)
                gp.tensor_tensor(clo[k][:, :, at], cT[k][:, :, at], chi[:, :, at].bitcast(f32),
                                 ALU.subtract).then_inc(s_clo, 1)

            gp.memset(vbd[:], 0.0).then_inc(s_vz, 1)
            pool.wait_ge(s_vz, 1)
            gp.memset(vbd[0:64, :, :, 32:33], 1.0).then_inc(s_pool, 1)
            pool.wait_ge(s_pool, 1)
            gp.memset(vbd[64:128, :, :, 33:34], 1.0).then_inc(s_vz, 1)
            pool.wait_ge(s_vz, 2)
            for r in range(2):
                for j in range(2):
                    pool.wait_ge(s_mx, 2 * r + j + 1)
                    p4 = P[:, 2 * r:2 * r + 2, j, :].rearrange("p t (g s) -> p t g s", s=T)
                    gp.tensor_tensor(p4, p4, spread(mx[:, 2 * r:2 * r + 2, j, :], 3, T), ALU.subtract
                                     ).then_inc(s_diff_pool, 1)
            pool.wait_ge(s_o_in, 32)
            pool.wait_ge(s_x_in, 16)
            gp.tensor_tensor(xb[:], x_tok[:], spread(R("bo0"), 1, NT), ALU.add).then_inc(s_xb, 1)
            pool.wait_ge(s_x, 1)
            gp.tensor_tensor(xb[:], x_tok[:], spread(R("boa"), 1, NT), ALU.add).then_inc(s_xb, 1)
            gp.memset(ym[:], 0.0).then_inc(s_yadd, 2)
            for m in range(2):
                for c in range(NC):
                    gp.memset(dec[m][c].rearrange("p (b t) -> p b t", t=T)[:, :, 0:1], 0.0).then_inc(s_yadd, 1)
            pool.wait_ge(s_sum_act, 6)
            pool.wait_ge(s_sum_dve, 6)
            for k in range(2):
                gp.memset(cN[k][:, :, D:D + 1], 1.0).then_inc(s_yadd, 1)
            pool.wait_ge(s_yadd, 8)
            pool.wait_ge(s_wkhi, 1)
            gp.tensor_tensor(wklo[:], wx1[:, 1], wkhi[:].bitcast(f32), ALU.subtract).then_inc(s_wklo, 1)
            for g in range(AHEAD):
                low_part(0, g)

            def states(j, last):
                for k in range(2):
                    def y_add(m, c):
                        n = 4 * j + (2 * k + m)
                        pool.wait_ge(s_ssm, 6 * n + (12 + 5 + c))
                        pool.wait_ge(s_yadd, 2 * n + (8 + c - 1))
                        gp.tensor_tensor(ym[:, c, :], ym[:, c, :], hc[m][c], ALU.add).then_inc(s_yadd, 1)

                    for g in range(G):
                        if not (last and G * k + g + AHEAD >= 2 * G):
                            low_part(j, G * k + g + AHEAD)
                        if g in (2, 3):
                            y_add(0, g - 2)
                        if g in (5, 6):
                            y_add(1, g - 5)

            with pool.Fori(0, B // 2 - 1) as j:
                states(j, False)
            states(B // 2 - 1, True)
            pool.wait_ge(s_xn, 4 * NT)
            gp.tensor_tensor(xb[:], xn[:], spread(R("bo1"), 1, NT), ALU.add).then_inc(s_xb, 1)
            gp.tensor_tensor(x_tok[:], x_tok[:], spread(R("beta"), 1, NT), ALU.add).then_inc(s_x3b, 1)

        @block.scalar
        def _(act):
            sa = nc.scalar
            steps = [0]

            def own(ins):
                steps[0] += 1
                ins.then_inc(s_act, 1)
                act.wait_ge(s_act, steps[0])

            def rstd_of(n, s_ready, s_done):
                act.wait_ge(s_ready, n)
                own(sa.activation(lnv[:], mv[:, :, 1], ACT.Ln, bias=C("eps")))
                sa.activation(rstd[:], lnv[:], ACT.Exp, scale=-0.5).then_inc(s_done, 1)

            def xnT_evac(n):
                act.wait_ge(s_xnT_ps, n)
                sa.copy(xnT[:, 0, :], bank[6][:]).then_inc(s_xnT, 1)

            def sums(i):
                b = ORDER[i]
                act.wait_ge(s_ctxT[SLOT[i]], 16 * (seen[i] + 1))
                v = slots[SLOT[i]][:, 0, 0:S]
                sa.activation(v[:, 0:REST], v[:, 0:REST], ACT.Copy, accum_out=csum[:, 0, b:b + 1]).then_inc(s_sum_act, 1)

            sa.preload_act_table_set("natural_log_exp_and_others")
            act.wait_ge(s_in, IN)
            rstd_of(1, s_var, s_rstd)
            act.wait_ge(s_vz, 2)
            act.wait_ge(s_v_ps, 1)
            vb = vbd.rearrange("p (t h) n w -> p t h n w", h=2)
            for i in range(2):
                v = bank[2 + i][:].rearrange("p (t n e) -> p t n e", t=2, e=2 * HD)
                for h in range(2):
                    for a in range(2):
                        sa.copy(vb[64 * a:64 * a + 64, 2 * i:2 * i + 2, h, :, HD * a:HD * a + HD],
                                v[64 * h:64 * h + 64, :, :, HD * a:HD * a + HD]).then_inc(s_vbd, 1)
            xnT_evac(1)
            for i in range(4):
                sums(i)
            for r in range(2):
                for j in range(4):
                    if j < 2:
                        act.wait_ge(s_diff_pool, 2 * r + j + 1)
                    else:
                        act.wait_ge(s_diff, 2 * r + j - 1)
                    p = P[:, 2 * r:2 * r + 2, j, :]
                    sa.activation(p, p, ACT.Exp).then_inc(s_exp, 1)
            for r in range(2):
                for j in (0, 2):
                    act.wait_ge(s_PT_ps, 4 * r + j + 1)
                    sa.copy(PT[:, 2 * r:2 * r + 2, j, :],
                            bank[[2, 3, 4, 5][j] if r == 0 else [6, 7, 0, 1][j]][:].rearrange("p (t n) -> p t n", t=2)
                            ).then_inc(s_PT, 1)
            for i in range(4, 8):
                sums(i)
            act.wait_ge(s_vr, 1)
            sa.copy(vr8[0:B, :], bank[0][0:B, 0:D]).then_inc(s_vr8, 1)
            act.wait_ge(s_oT_ps, 1)
            sa.activation(oT[:, 0, :], bank[6][:], ACT.Identity, bias=L("bv0", 0)).then_inc(s_oT, 1)

            sa.activation(aneg[:], L("log_a", 0, 32), ACT.Exp).then_inc(s_an, 1)
            rstd_of(2, s_var, s_rstd)
            xnT_evac(2)

            def high_part(j, q):
                k, at = q // G % 2, columns(q)
                if q % G == 0:
                    act.wait_ge(s_ctxT[k], 16 * j + (16 * (q // (2 * G)) + 32))
                sa.copy(chi[:, :, at], cT[k][:, :, at]).then_inc(s_chi, 1)

            act.wait_ge(s_w, 16 * 3)
            sa.copy(wkhi[:], wx1[:, 1]).then_inc(s_wkhi, 1)
            for g in range(AHEAD):
                high_part(0, g)
            sa.preload_act_table(ACT.Silu)
            for c in range(NC):
                act.wait_ge(s_conv0, c + 1)
                sa.activation(xc[:, c, :], tmp[:, c, :], ACT.Silu).then_inc(s_xc0, 1)
            sa.preload_act_table_set("natural_log_exp_and_others")
            for c in range(NC):
                act.wait_ge(s_m0_ps, c + 1)
                act.wait_ge(s_aneg, 2)
                sa.activation(gate[:, c, :], bank[c][:], ACT.Exp, scale=-1.0, bias=g2[:, c, 0:1]).then_inc(s_ge, 1)
            for c in range(NC):
                act.wait_ge(s_ge, c + 1)
                own(sa.activation(gate[:, c, :], gate[:, c, :], ACT.Ln, bias=C("one")))
                sa.activation(gate[:, c, :], gate[:, c, :], ACT.Exp, scale=-1.0).then_inc(s_gate0, 1)
            for c in range(NC):
                act.wait_ge(s_abs, c + 1)
                sa.activation(dtx[:, c, :], dt[:, c, :], ACT.Abs).then_inc(s_act, 1)
            for c in range(NC):
                act.wait_ge(s_act, steps[0] + 1 + c)
                sa.activation(dtx[:, c, :], dtx[:, c, :], ACT.Exp, scale=-1.0).then_inc(s_act, 1)
            for c in range(NC):
                act.wait_ge(s_act, steps[0] + 3 + c)
                sa.activation(dtx[:, c, :], dtx[:, c, :], ACT.Ln, bias=C("one")).then_inc(s_sp, 1)
            steps[0] += 4
            act.wait_ge(s_yadd, 8)
            sa.copy(lnv[:, 0:1], rstd[:, 0:1]).then_inc(s_ktc, 4)

            def exponentials(j, q):
                p, w = (128, 512) if q % G < G - 1 else (KLAST, D)
                act.wait_ge(s_z, 2 * G * j + (q + 3))
                act.wait_ge(s_kt, 2 * G * j + (q + 1))
                sa.activation(ek[q % 2][0:p, 0:w], zk[q % 2][0:p, 0:w], ACT.Exp, bias=C("minus1", p=p)).then_inc(s_e, 1)

            def states(j, last):
                for k in range(2):
                    def decay(m):
                        n = 4 * j + (2 * k + m)
                        for c in range(NC):
                            act.wait_ge(s_ssm, 6 * n + (3 + c))
                            d3 = dec[m][c].rearrange("p (b t) -> p b t", t=T)[:, :, 1:T]
                            dt3 = dt[:, c, :].rearrange("p (b t) -> p b t", t=T)[:, :, 1:T]
                            sa.activation(d3, dt3, ACT.Exp, scale=aneg[:, c, one(n)]).then_inc(s_decay, 1)

                    decay(0)
                    for g in range(G):
                        if g:
                            exponentials(j, G * k + g)
                        if g == 2:
                            decay(1)
                        if not (last and G * k + g + AHEAD >= 2 * G):
                            high_part(j, G * k + g + AHEAD)
                    if not (last and k == 1):
                        exponentials(j, G * k + G)
                    act.wait_ge(s_kfree, 2 * G * j + (G * k + G + 2))
                    for c in range(NC):
                        sa.copy(ktc[:, one(2 * j + k), c, :].rearrange("p o d -> p (o d)"),
                                bank[2 + 2 * k + c][:, 0:D + 1]).then_inc(s_ktc, 1)

            exponentials(0, 0)
            with act.Fori(0, B // 2 - 1) as j:
                states(j, False)
            states(B // 2 - 1, True)
            rstd_of(3, s_var, s_rstd)
            xnT_evac(3)
            act.wait_ge(s_hot_ps, 1)
            sa.copy(hott[0:E, :], bank[2][0:E, :]).then_inc(s_hott, 1)
            for t in range(NT + 1):
                if t < NT:
                    act.wait_ge(s_h_ps, 2 * t + 1)
                    sa.copy(hf[t % 2][:, 0:512], bank[2 * (t % 2)][:]).then_inc(s_hf0, 1)
                if t:
                    for i in range(2):
                        act.wait_ge(s_hb, 4 * (t - 1) + 2 * i + 2)
                        sa.activation(hr[(t - 1) % 2][:, 4 * i:4 * i + 4, :], hb[(t - 1) % 2][:, 4 * i:4 * i + 4, :],
                                      ACT.Relu).then_inc(s_hr, 1)
            rstd_of(4, s_var, s_rstd)
            xnT_evac(4)
            for c in range(NC):
                act.wait_ge(s_z1, c + 1)
                sa.activation(e1[:, c, :], z1[:, c, :], ACT.Exp, bias=C("minus1")).then_inc(s_e1, 1)
            sa.activation(da1[:, 0:1], L("A1", p=N), ACT.Exp).then_inc(s_ea1, 1)
            for t in range(NT):
                act.wait_ge(s_G_ps, t + 1)
                sa.copy(Gt[:, t, :], bank[2 + t][:, 0:D]).then_inc(s_G, 1)
            act.wait_ge(s_GT_ps, NT)
            sa.copy(GT[:, 0, :], bank[6][:]).then_inc(s_GT, 1)
            act.wait_ge(s_wf1[0], 16)
            for i in range(PIECES):
                sa.copy(whi[0][:, WP * i:WP * i + WP], wf1[0][:, WP * i:WP * i + WP]).then_inc(s_whi, 1)
            rstd_of(1, s_var1, s_rstd1)
            rstd_of(5, s_var, s_rstd)
            xnT_evac(5)
            for c in range(4):
                act.wait_ge(s_cv1, c + 1)
                sa.activation(xs1[:, c, :], xc1[:, c, :], ACT.Silu).then_inc(s_xs1, 1)
            for c in range(4):
                act.wait_ge(s_in_ps, 5 + c)
                sa.activation(sres[:, c, :], bank[4 + c][:], ACT.Silu).then_inc(s_res, 1)
            sa.preload_act_table_set("natural_log_exp_and_others")
            rstd_of(6, s_var, s_rstd)
            xnT_evac(6)
            act.wait_ge(s_xnT, 2 * 6)
            sa.copy(xhi[:, 0, :], xnT[:, 0, :]).then_inc(s_xhi, 1)
            sa.copy(xhi[:, 1, :], xnT[:, 1, :]).then_inc(s_xhi, 1)
            act.wait_ge(s_gd, 1)
            sa.activation(g2[:, :, 1], g2[:, :, 0], ACT.Exp).then_inc(s_ge1, 1)
            sa.preload_act_table(ACT.Silu)

            def expert(j, k, split):
                for f in range(6):
                    q, i, w = 6 * k + f, f % 2, F1C[f]
                    act.wait_ge(s_h12, 12 * j + (q + 1))
                    act.wait_ge(s_hid, 12 * j + (q + 1))
                    sa.activation(sg[i][0:w, :], bank[2 * i][0:w, :], ACT.Silu).then_inc(s_sg, 1)
                    if split and 1 <= f <= PIECES:
                        if f == 1:
                            act.wait_ge(s_wf1[1 - k], 16 * j + (16 + 16 * k))
                            act.wait_ge(s_hfree, 12 * j + (6 * k + 2))
                        at = WP * (f - 1)
                        sa.copy(whi[1 - k][:, at:at + WP], wf1[1 - k][:, at:at + WP]).then_inc(s_whi, 1)

            with act.Fori(0, E // 2 - 1) as j:
                for k in range(2):
                    expert(j, k, True)
            for k in range(2):
                expert(E // 2 - 1, k, k == 0)

        @block.vector
        def _(dve):
            v = nc.vector
            steps = [0]

            def mark(ins):
                steps[0] += 1
                ins.then_inc(s_dve, 1)
                return steps[0]

            def own(ins):
                dve.wait_ge(s_dve, mark(ins))

            def moments(src, done, counted=False):
                for t in range(0 if counted else NT):
                    mark(v.bn_stats(stats[:, t, :], src[:, t, :]))
                dve.wait_ge(s_dve, steps[0])
                for t in range(NT):
                    ins = v.bn_aggr(mv[:, t, :], stats[:, t, :])
                    if t == NT - 1:
                        ins.then_inc(done, 1)
                    else:
                        mark(ins)

            def add_tiles(n, s_from, old, new, banks):
                at = {}
                for t in range(NT + 1):
                    if t < NT:
                        dve.wait_ge(s_from, t + 1)
                        ins = v.tensor_tensor(new[:, t, :], old[:, t, :], bank[banks[t]][:, 0:D], ALU.add)
                        if t == NT - 1 and n:
                            ins.then_inc(s_x, 1)
                        else:
                            at[t] = mark(ins)
                    if t:
                        dve.wait_ge(*((s_x, n) if t == NT and n else (s_dve, at[t - 1])))
                        mark(v.bn_stats(stats[:, t - 1, :], new[:, t - 1, :]))

            def normalise(n, evacuate=True):
                if n > 1:
                    moments(x_tok, s_var, n != 4)
                dve.wait_ge(s_rstd, n)
                dve.wait_ge(s_var, n)
                for t in range(NT):
                    v.tensor_scalar(xn[:, t, :], x_tok[:, t, :], mv[:, t, 0:1], rstd[:, t:t + 1],
                                    ALU.subtract, ALU.mult).then_inc(s_xn, 1)
                if evacuate:
                    evacuate_xnT(n)

            def evacuate_xnT(n):
                dve.wait_ge(s_xnT_ps, n)
                v.tensor_copy(xnT[:, 1, :], bank[7][:]).then_inc(s_xnT, 1)

            def sums(i):
                b = ORDER[i]
                dve.wait_ge(s_ctxT[SLOT[i]], 16 * (seen[i] + 1))
                v.reduce_sum(csum[:, 1, b:b + 1], slots[SLOT[i]][:, 1, 0:REST], AX.X).then_inc(s_sum_dve, 1)

            def split_low(k, i, n):
                dve.wait_ge(s_whi, n)
                at = WP * i
                v.tensor_tensor(wlo[k][:, at:at + WP], wf1[k][:, at:at + WP], whi[k][:, at:at + WP].bitcast(f32),
                                ALU.subtract).then_inc(s_wlo, 1)

            dve.wait_ge(s_x_in, 16)
            moments(x_tok, s_var)
            dve.wait_ge(s_in, IN)
            own(v.tensor_scalar(maskf[:], mask8[:], -FMAX, None, ALU.mult))
            own(v.tensor_tensor(maskf[:], maskf[:], spread(C("causal"), 1, NT), ALU.min))
            for c in range(NC):
                dve.wait_ge(s_k_ps, c + 1)
                for h in range(2):
                    v.tensor_scalar(kb2[:, c, :, h, :], bank[c][:].rearrange("p (b s) -> p b s", s=T),
                                    L("bk0", c), C("parity", h, 1), ALU.add, ALU.mult).then_inc(s_kb, 1)
            normalise(1)
            sums(0)
            sums(1)
            for c in range(NC):
                dve.wait_ge(s_q_ps, c + 1)
                v.tensor_scalar(qT[:, c, :], bank[c][:], L("bq0", c), HD ** -0.5, ALU.add, ALU.mult).then_inc(s_qT, 1)
            sums(2)
            for r in range(2):
                banks = [2, 3, 4, 5] if r == 0 else [6, 7, 0, 1]
                ready = {}
                for j in range(4):
                    dve.wait_ge(s_sc_ps, 4 * r + j + 1)
                    v.tensor_tensor(
                        P[:, 2 * r:2 * r + 2, j, :].rearrange("p t (g s) -> p t g s", s=T),
                        bank[banks[j]][:].rearrange("p (t g s) -> p t g s", t=2, s=T),
                        spread(maskf[:, 2 * r:2 * r + 2, :], 2, 4), ALU.add).then_inc(s_sc, 1)
                for j in range(4):
                    dve.wait_ge(s_sc, 4 * r + j + 1)
                    ins = v.tensor_reduce(
                        mx[:, 2 * r:2 * r + 2, j, :],
                        P[:, 2 * r:2 * r + 2, j, :].rearrange("p t (g s) -> p t g s", s=T), AX.X, ALU.max)
                    if j < 2:
                        ins.then_inc(s_mx, 1)
                    else:
                        ready[j] = mark(ins)
                for j in (2, 3):
                    dve.wait_ge(s_dve, ready[j])
                    p4 = P[:, 2 * r:2 * r + 2, j, :].rearrange("p t (g s) -> p t g s", s=T)
                    v.tensor_tensor(p4, p4, spread(mx[:, 2 * r:2 * r + 2, j, :], 3, T), ALU.subtract).then_inc(s_diff, 1)
                if r == 0:
                    sums(3)
            dve.wait_ge(s_mx, 4)
            own(v.tensor_scalar(rest[:], mx[:], -FMAX, None, ALU.is_le))
            sums(4)
            for r in range(2):
                for j in (1, 3):
                    dve.wait_ge(s_PT_ps, 4 * r + j + 1)
                    v.tensor_copy(PT[:, 2 * r:2 * r + 2, j, :],
                                  bank[[2, 3, 4, 5][j] if r == 0 else [6, 7, 0, 1][j]][:].rearrange("p (t n) -> p t n", t=2)
                                  ).then_inc(s_PT, 1)
            for i in range(5, 8):
                sums(i)
            dve.wait_ge(s_vrb, 1)
            for t in range(NT):
                for c in range(NC):
                    last = mark(v.tensor_tensor(
                        vro[:, t, 128 * c:128 * c + 128].rearrange("p (j a e) -> p j a e", j=4, a=2),
                        bank[t // 2][:, 256 * (t % 2) + 128 * c:256 * (t % 2) + 128 * c + 128].rearrange(
                            "p (j a e) -> p j a e", j=4, a=2),
                        spread(rest[:, t, :, 2 * c:2 * c + 2], 3, HD), ALU.mult))
            dve.wait_ge(s_pv, NT)
            for t in range(NT):
                last = mark(v.scalar_tensor_tensor(
                    den[:, t, 0:8].rearrange("p (j a) -> p j a", a=2), rest[:, t, :, 0:2], float(REST),
                    bank[2 + t][:, 0:272].rearrange("p (n w) -> p n w", w=34)[:, 0:4, 32:34], ALU.mult, ALU.add))
                last = mark(v.scalar_tensor_tensor(
                    den[:, t, 8:16].rearrange("p (j a) -> p j a", a=2), rest[:, t, :, 2:4], float(REST),
                    bank[2 + t][:, 0:272].rearrange("p (n w) -> p n w", w=34)[:, 4:8, 32:34], ALU.mult, ALU.add))
            dve.wait_ge(s_dve, last)
            own(v.reciprocal(den[:], den[:]))
            for t in range(NT):
                last = mark(v.tensor_tensor(
                    vro[:, t, :].rearrange("p (n e) -> p n e", e=32), vro[:, t, :].rearrange("p (n e) -> p n e", e=32),
                    bank[2 + t][:, 0:272].rearrange("p (n w) -> p n w", w=34)[:, :, 0:32], ALU.add))
            dve.wait_ge(s_dve, last)
            for t in range(NT):
                v.tensor_tensor(oa[:, t, :].rearrange("p (h e) -> p h e", e=HD),
                                vro[:, t, :].rearrange("p (h e) -> p h e", e=HD),
                                spread(den[:, t, :], 2, HD), ALU.mult).then_inc(s_o, 1)
            dve.wait_ge(s_oT_ps, 1)
            v.tensor_scalar(oT[:, 1, :], bank[7][:], L("bv0", 1), None, ALU.add).then_inc(s_oT, 1)
            dve.wait_ge(s_xb, 1)
            add_tiles(1, s_proj0, xb, x_tok, range(NT))

            dve.wait_ge(s_an, 1)
            v.tensor_scalar(aneg[:], aneg[:], -1.0, None, ALU.mult).then_inc(s_aneg, 1)
            v.tensor_scalar(g2[:, 0:NC, 0:1], L("bg", 0, 2).unsqueeze(2), -1.0, None, ALU.mult).then_inc(s_aneg, 1)
            v.memset(kk[0][:, 0:1], 0.0).then_inc(s_z, 2)
            v.memset(kk[1][:, 0:1], 0.0).then_inc(s_kt, 2)
            mark(v.tensor_scalar(R("bk1"), R("bk1"), 1.0, None, ALU.add))
            normalise(2)
            dve.wait_ge(s_xnT, 4)
            x3 = [xnT[:, c, :].rearrange("p (b t) -> p b t", t=T) for c in range(NC)]
            t3 = [tmp[:, c, :].rearrange("p (b t) -> p b t", t=T) for c in range(NC)]
            last = [None] * NC
            for c in range(NC):
                last[c] = mark(v.tensor_scalar(t3[c], x3[c], L("conv0", 4 * c + 3), L("conv0b", c), ALU.mult, ALU.add))
            for s in range(1, 4):
                for c in range(NC):
                    dve.wait_ge(s_dve, last[c])
                    ins = v.scalar_tensor_tensor(t3[c][:, :, s:T], x3[c][:, :, 0:T - s], L("conv0", 4 * c + 3 - s),
                                                 t3[c][:, :, s:T], ALU.mult, ALU.add)
                    if s < 3:
                        last[c] = mark(ins)
                    else:
                        ins.then_inc(s_conv0, 1)
            for c in range(NC):
                dve.wait_ge(s_m0_ps, c + 3)
                v.tensor_scalar(dt[:, c, :], bank[2 + c][:], L("bd", c), None, ALU.add).then_inc(s_abs, 1)
            dve.wait_ge(s_bc_ps, 1)
            own(v.tensor_copy(bcs[0:32, :], bank[4][0:32, :]))
            own(v.tensor_tensor(r1[0:32, :], bank[4][0:32, :], bcs[0:32, :], ALU.subtract))
            own(v.tensor_copy(mid[:], r1[0:32, :]))
            v.tensor_copy(bcs[32:64, :], mid[:]).then_inc(s_bcs, 1)
            v.tensor_tensor(bcs[64:96, :], r1[0:32, :], mid[:], ALU.subtract).then_inc(s_bcs, 1)
            for c in range(NC):
                dve.wait_ge(s_sp, c + 1)
                mark(v.scalar_tensor_tensor(dt[:, c, :], dt[:, c, :], 0.0, dtx[:, c, :], ALU.max, ALU.add))
            dve.wait_ge(s_dve, steps[0])
            v.tensor_tensor(dtx[:, 0, :], dt[:, 0, :], xc[:, 0, :], ALU.mult).then_inc(s_ssm, 6)
            v.tensor_tensor(dtx[:, 1, :], dt[:, 1, :], xc[:, 1, :], ALU.mult).then_inc(s_ssm, 6)
            dve.wait_ge(s_ssm, 12)
            with dve.Fori(0, B // 2) as j:
                for k in range(2):
                    def ssm(q):
                        m, op, c = q // 6, (q % 6) // 2, q % 2
                        n = 4 * j + (2 * k + m)
                        if op == 0:
                            dve.wait_ge(s_B, n + 1)
                            v.tensor_tensor(inp[c], dtx[:, c, :], bank[6][:], ALU.mult).then_inc(s_ssm, 1)
                        elif op == 1:
                            dve.wait_ge(s_decay, 2 * n + (c + 1))
                            dve.wait_ge(s_ssm, 6 * n + (12 + 1 + c))
                            v.tensor_tensor_scan(hst[c], dec[m][c], inp[c], 0.0, ALU.mult, ALU.add).then_inc(s_ssm, 1)
                        else:
                            dve.wait_ge(s_C, n + 1)
                            dve.wait_ge(s_ssm, 6 * n + (12 + 3 + c))
                            dve.wait_ge(s_yadd, 2 * n + (8 - 3 + c))
                            v.tensor_tensor(hc[m][c], hst[c], bank[7][:], ALU.mult).then_inc(s_ssm, 1)

                    for g in range(G):
                        i = (G * k + g) % 2
                        gg = 2 * G * j + (G * k + g)
                        p, w = (128, 512) if g < G - 1 else (KLAST, D)
                        reps = w // D
                        dve.wait_ge(s_kp, gg + 1)
                        v.tensor_tensor(zk[i][0:p, 0:w].rearrange("p (r d) -> p r d", r=reps),
                                        bank[i][0:p, 0:w].rearrange("p (r d) -> p r d", r=reps),
                                        spread(R("bk1", p=p), 1, reps), ALU.add).then_inc(s_z, 1)
                        if g < 6:
                            ssm(2 * g)
                        dve.wait_ge(s_e, gg + 1)
                        dve.wait_ge(s_kfree, gg + 1)
                        dve.wait_ge(s_z, gg + 3)
                        v.scalar_tensor_tensor(kk[i][0:p, 0:w], ek[i][0:p, 0:w], 1.0, zk[i][0:p, 0:w],
                                               ALU.min, ALU.max).then_inc(s_kt, 1)
                        if g < 6:
                            ssm(2 * g + 1)
            dve.wait_ge(s_yadd, 8 + 2 * N)
            dve.wait_ge(s_gate0, 2)
            for c in range(NC):
                v.tensor_tensor(ym[:, c, :], ym[:, c, :], gate[:, c, :], ALU.mult).then_inc(s_yg, 1)
            dve.wait_ge(s_xb, 2)
            add_tiles(2, s_proj1, xb, x_tok, range(NT))

            normalise(3, False)
            dve.wait_ge(s_ms_ps, 1)
            v.tensor_copy(msum[:], bank[3][:, 0:NC * B].rearrange("p (c b) -> p c b", b=B)).then_inc(s_ms, 1)
            dve.wait_ge(s_rt_ps, 1)
            own(v.scalar_tensor_tensor(sc[:], bank[0][0:B, 0:E], 1.0 / T, R("br", p=B), ALU.mult, ALU.add))
            own(v.max(m8[0:B, 0, :], sc[:]))
            own(v.max_index(i8[0:B, 0, :], m8[0:B, 0, :], sc[:]))
            v.tensor_copy(topf[:], i8[0:B, 0, 0:1]).then_inc(s_topf, 1)
            dve.wait_ge(s_topT, 1)
            v.tensor_copy(top[:], bank[1][0:1, 0:B]).then_inc(s_top, 1)
            evacuate_xnT(3)
            dve.wait_ge(s_topf, 1)
            v.tensor_scalar(hot[:], C("iota", p=B), topf[:], None, ALU.is_equal).then_inc(s_hot, 1)
            for t in range(NT + 1):
                if t < NT:
                    dve.wait_ge(s_h_ps, 2 * t + 2)
                    v.tensor_copy(hf[t % 2][:, 512:F0], bank[2 * (t % 2) + 1][:]).then_inc(s_hf1, 1)
                if t:
                    q = t - 1
                    dve.wait_ge(s_hT_ps, t)
                    for i in range(2):
                        for h in range(2):
                            k = (2 * q + h) % 4
                            v.tensor_tensor(hb[q % 2][:, 4 * i:4 * i + 4, T * h:T * h + T],
                                            bank[4 + i][:].rearrange("p (f t) -> p f t", t=128)[:, :, T * h:T * h + T],
                                            spread(wf0[k][:, NC * F0 + 4 * i:NC * F0 + 4 * i + 4], 2, T), ALU.add).then_inc(s_hb, 1)
                    dve.wait_ge(s_y_ps, t)
                    ins = v.tensor_tensor(x_tok[:, q, :], x_tok[:, q, :], bank[6 + q % 2][:, 0:D], ALU.add)
                    if q < NT - 1:
                        mark(ins)
            ins.then_inc(s_x, 1)
            dve.wait_ge(s_x, 3)
            dve.wait_ge(s_dve, steps[0])

            normalise(4)
            for c in range(NC):
                dve.wait_ge(s_q1_ps, c + 1)
                v.tensor_scalar(z1[:, c, :], bank[c][:], L("bq1", c), 1.0, ALU.add, ALU.add).then_inc(s_z1, 1)
            dve.wait_ge(s_z1, 2)
            for c in range(NC):
                dve.wait_ge(s_e1, c + 1)
                v.scalar_tensor_tensor(QT[:, c, :], e1[:, c, :], 1.0, z1[:, c, :], ALU.min, ALU.max).then_inc(s_Q1, 1)
            dve.wait_ge(s_Q1, 2)
            for c in range(NC):
                v.tensor_tensor(qk[:, c, :].rearrange("p (b t) -> p b t", t=T),
                                QT[:, c, :].rearrange("p (b t) -> p b t", t=T),
                                spread(ktc[:, :, c, D], 2, T), ALU.mult).then_inc(s_qk, 1)
            dve.wait_ge(s_qk, NC)
            own(v.tensor_scalar(dn[:], qk[:], 1e-6, None, ALU.add))
            mark(v.reciprocal(dn[:], dn[:]))
            dve.wait_ge(s_GT_ps, NT)
            v.tensor_copy(GT[:, 1, :], bank[7][:]).then_inc(s_GT, 1)
            dve.wait_ge(s_ea1, 1)
            own(v.tensor_scalar(da1[:, 0:1], da1[:, 0:1], 1.0, None, ALU.add))
            own(v.reciprocal(da1[:, 1:2], da1[:, 0:1]))
            own(v.tensor_copy(dec1[0:N, :], da1[:, 1:2].broadcast_to([N, TOK])))
            mark(v.memset(dec1[0:N, :].rearrange("p (b t) -> p b t", t=T)[:, :, 0:1], 0.0))
            dve.wait_ge(s_dve, steps[0])
            for c in range(NC):
                dve.wait_ge(s_num, c + 1)
                v.tensor_tensor(aT[:, c, :], dn[:, c, :], bank[c][:], ALU.mult).then_inc(s_aT, 1)
            dve.wait_ge(s_xb, 3)
            add_tiles(0, s_proj2, xb, y1, range(2, 2 + NT))
            moments(y1, s_var1, True)
            dve.wait_ge(s_var1, 1)
            for t in range(NT):
                last = mark(v.scalar_tensor_tensor(y1[:, t, :], y1[:, t, :], mv[:, t, 0:1], R("gamma"),
                                                   ALU.subtract, ALU.mult))
            dve.wait_ge(s_dve, last)
            dve.wait_ge(s_rstd1, 1)
            dve.wait_ge(s_x3b, 1)
            done = {}
            for t in range(NT + 1):
                if t < NT:
                    ins = v.scalar_tensor_tensor(x_tok[:, t, :], y1[:, t, :], rstd[:, t:t + 1], x_tok[:, t, :],
                                                 ALU.mult, ALU.add)
                    if t == NT - 1:
                        ins.then_inc(s_x, 1)
                    else:
                        done[t] = mark(ins)
                if t:
                    dve.wait_ge(*((s_x, 4) if t == NT else (s_dve, done[t - 1])))
                    mark(v.bn_stats(stats[:, t - 1, :], x_tok[:, t - 1, :]))

            normalise(5)
            for c in range(4):
                dve.wait_ge(s_in_ps, c + 1)
                xm = bank[c][:].rearrange("p (b t) -> p b t", t=T)
                xo = xc1[:, c, :].rearrange("p (b t) -> p b t", t=T)
                own(v.tensor_scalar(xo, xm, L("conv1", 3 * c + 1), L("conv1b", c), ALU.mult, ALU.add))
                own(v.scalar_tensor_tensor(xo[:, :, 1:T], xm[:, :, 0:T - 1], L("conv1", 3 * c), xo[:, :, 1:T],
                                           ALU.mult, ALU.add))
                v.scalar_tensor_tensor(xo[:, :, 0:T - 1], xm[:, :, 1:T], L("conv1", 3 * c + 2), xo[:, :, 0:T - 1],
                                       ALU.mult, ALU.add).then_inc(s_cv1, 1)
            for i in range(PIECES):
                split_low(0, i, 1 + i)
            dve.wait_ge(s_bc1, 1)
            own(v.tensor_tensor_scan(st1[0:N, :], dec1[0:N, :], bank[0][0:N, :], 0.0, ALU.mult, ALU.add))
            v.tensor_tensor(pr1[0:N, :], st1[0:N, :], bank[0][32:32 + N, :], ALU.mult).then_inc(s_pr1, 1)
            dve.wait_ge(s_ys, 1)
            dve.wait_ge(s_res, 4)
            for c in range(4):
                own(v.scalar_tensor_tensor(y2[:, c, :], xs1[:, c, :], L("D1", c), bank[1][:], ALU.mult, ALU.add))
                v.tensor_tensor(y2[:, c, :], y2[:, c, :], sres[:, c, :], ALU.mult).then_inc(s_y2, 1)
            add_tiles(5, s_proj3, x_tok, x_tok, range(4, 4 + NT))

            normalise(6)
            v.memset(hid[0][:, 0:1], 0.0).then_inc(s_hid, 2)
            dve.wait_ge(s_hid, 2)
            dve.wait_ge(s_xnT, 2 * 6)
            for c in range(NC):
                dve.wait_ge(s_xhi, c + 1)
                v.tensor_tensor(xlo[:, c, :], xnT[:, c, :], xhi[:, c, :].bitcast(f32), ALU.subtract).then_inc(s_xlo, 1)
            dve.wait_ge(s_lg, 1)
            v.tensor_copy(gtmp[:], bank[4][:, 0:NT * E].rearrange("p (t e) -> p t e", e=E)).then_inc(s_ofree, NT)
            dve.wait_ge(s_ofree, NT)
            for t in range(NT):
                last = mark(v.max(m8[:, t, :], gtmp[:, t, :]))
            dve.wait_ge(s_dve, last)
            v.tensor_tensor(g2[:, :, 0], m8[:, :, 1], m8[:, :, 0], ALU.subtract).then_inc(s_gd, 1)
            for t in range(NT):
                last = mark(v.max_index(i8[:, t, :], m8[:, t, :], gtmp[:, t, :]))
            dve.wait_ge(s_dve, last)
            own(v.tensor_copy(ixf[:], i8[:, :, 0:2]))
            dve.wait_ge(s_ge1, 1)
            own(v.tensor_scalar(g2[:, :, 2], g2[:, :, 1], 1.0, None, ALU.add))
            own(v.reciprocal(g2[:, :, 2], g2[:, :, 2]))
            own(v.tensor_tensor(g2[:, :, 1], g2[:, :, 1], g2[:, :, 2], ALU.mult))
            for t in range(NT):
                last = mark(v.tensor_scalar(gt[:, t, :], C("iota"), ixf[:, t, 0:1], g2[:, t, 2:3], ALU.is_equal, ALU.mult))
                last = mark(v.tensor_scalar(gtmp[:, t, :], C("iota"), ixf[:, t, 1:2], g2[:, t, 1:2], ALU.is_equal, ALU.mult))
            dve.wait_ge(s_dve, last)
            v.tensor_tensor(gt[:], gt[:], gtmp[:], ALU.add).then_inc(s_gate, 1)
            dve.wait_ge(s_gate, 1)

            def gather(j, k):
                for t in range(NT):
                    if t < NT - 1:
                        dve.wait_ge(s_o_ps, 6 * j + (3 * k + t + 1))
                    else:
                        dve.wait_ge(s_hfree, 12 * j + (6 * k + 8))
                    dve.wait_ge(s_ofree, 8 * j + (4 * k + t + 1))
                    e = 2 * j + k
                    g = gt[:, t, e:e + 1] if isinstance(j, int) else gt[:, t, bass.ds(e, 1)]
                    v.scalar_tensor_tensor(x_tok[:, t, :], bank[4 + t][:, 0:D], g, x_tok[:, t, :],
                                           ALU.mult, ALU.add).then_inc(s_ofree, 1)

            def expert(j, k, split):
                for f in range(6):
                    q, i, w = 6 * k + f, f % 2, F1C[f]
                    dve.wait_ge(s_sg, 12 * j + (q + 1))
                    second = bank[2 * i + 1][0:w, :] if f < 5 else bank[2 * i][64:64 + w, :]
                    v.tensor_tensor(hid[i][0:w, :], sg[i][0:w, :], second, ALU.mult).then_inc(s_hid, 1)
                    dve.wait_ge(s_hid, 12 * j + (q + 3))
                    dve.wait_ge(s_hfree, 12 * j + (q + 1))
                    v.tensor_copy(hhi[i][0:w, :], hid[i][0:w, :]).then_inc(s_hhi, 1)
                    dve.wait_ge(s_hhi, 12 * j + (q + 1))
                    v.tensor_tensor(hlo[i][0:w, :], hid[i][0:w, :], hhi[i][0:w, :].bitcast(f32),
                                    ALU.subtract).then_inc(s_hlo, 1)
                    if f == 0 and k == 1:
                        gather(j, 0)
                    if split and 1 <= f <= PIECES:
                        split_low(1 - k, f - 1, 2 * PIECES * j + (PIECES * k + PIECES + f))

            with dve.Fori(0, E // 2 - 1) as j:
                for k in range(2):
                    expert(j, k, True)
                gather(j, 1)
            for k in range(2):
                expert(E // 2 - 1, k, k == 0)
            gather(E // 2 - 1, 1)

        @block.tensor
        def _(pe):
            te = nc.tensor
            mm = te.matmul

            def transposes(n, wait=True):
                for t in range(NT):
                    pe.wait_ge(s_xn, NT * (n - 1) + t + 1)
                    for c in range(NC):
                        last = te.transpose(bank[6 + c][:, 128 * t:128 * t + 128], xn[:, t, 128 * c:128 * c + 128], ident)
                last.then_inc(s_xnT_ps, 1)
                if wait:
                    pe.wait_ge(s_xnT, 2 * n)

            def project(dst, w, moving, m=0):
                for d in range(NC):
                    last = mm(dst, w[:, d, m:m + 128], moving[:, d, :], start=(d == 0), stop=(d == NC - 1))
                return last

            def token_major(dst, src, w, t, n=NC, at=0):
                for d in range(n):
                    last = mm(dst[:, at:at + D], src[:, d, 128 * t:128 * t + 128], w[:, d, :], start=(d == 0), stop=(d == n - 1))
                return last

            pe.wait_ge(s_k_in, 32)
            for c in range(NC):
                project(bank[c][:], wx0[:, 1], c0T, 128 * c).then_inc(s_k_ps, 1)
            pe.wait_ge(s_v_in, 16)
            for t in range(NT):
                last = token_major(bank[2 + t // 2], c0T, wx0[:, 2], t, at=D * (t % 2))
            last.then_inc(s_v_ps, 1)
            pe.wait_ge(s_in, IN)
            transposes(1)
            pe.wait_ge(s_kb, 4)
            for c in range(NC):
                project(bank[c][:], wx0[:, 0], xnT, 128 * c).then_inc(s_q_ps, 1)
            pe.wait_ge(s_qT, 2)
            pe.wait_ge(s_vbd, 8)
            for r in range(2):
                banks = [2, 3, 4, 5] if r == 0 else [6, 7, 0, 1]
                for j in range(4):
                    for tt in range(2):
                        for h in range(2):
                            b = 4 * r + 2 * tt + h
                            for c in range(NC):
                                at = 256 * tt + 128 * c
                                last = mm(bank[banks[j]][64 * h:64 * h + 64, at:at + 128],
                                          qT[32 * j:32 * j + 32, c, T * b:T * b + T],
                                          kb2[32 * j:32 * j + 32, c, b, :, :], start=True, stop=True)
                    last.then_inc(s_sc_ps, 1)
            for r in range(2):
                banks = [2, 3, 4, 5] if r == 0 else [6, 7, 0, 1]
                for j in range(4):
                    pe.wait_ge(s_exp, 4 * r + j + 1)
                    for tt in range(2):
                        for c in range(NC):
                            at = 256 * tt + 128 * c
                            last = te.transpose(bank[banks[j]][:, at:at + 128], P[:, 2 * r + tt, j, 128 * c:128 * c + 128],
                                                ident)
                    last.then_inc(s_PT_ps, 1)
            pe.wait_ge(s_PT, 8)
            for t in range(NT):
                for h in range(2):
                    for c in range(NC):
                        for j in range(4):
                            n = 4 * c + j
                            last = mm(bank[2 + t][64 * h:64 * h + 64, 34 * n:34 * n + 34],
                                      PT[:, t, j, 128 * c + 64 * h:128 * c + 64 * h + 64],
                                      vbd[:, 2 * t + h, n, :], start=True, stop=True)
                last.then_inc(s_pv, 1)
                if t == 1:
                    pe.wait_ge(s_sum_act, 8)
                    pe.wait_ge(s_sum_dve, 8)
                    for d in range(NC):
                        last = mm(bank[0][0:B, 0:D], csum[:, d, :], wx0[:, 2, d, :], start=(d == 0), stop=(d == 1))
                    last.then_inc(s_vr, 1)
                if t == 2:
                    pe.wait_ge(s_vr8, 1)
                    for q in range(NT):
                        last = mm(bank[q // 2][:, D * (q % 2):D * (q % 2) + D], C("batch", 128 * q, 128, p=B), vr8[0:B, :],
                                  start=True, stop=True)
                    last.then_inc(s_vrb, 1)
            for t in range(NT):
                pe.wait_ge(s_o, t + 1)
                for c in range(NC):
                    last = te.transpose(bank[6 + c][:, 128 * t:128 * t + 128], oa[:, t, 128 * c:128 * c + 128], ident)
            last.then_inc(s_oT_ps, 1)
            pe.wait_ge(s_oT, 2)
            pe.wait_ge(s_o_in, 32)
            for t in range(NT):
                token_major(bank[t], oT, wx0[:, 3], t).then_inc(s_proj0, 1)

            transposes(2)
            pe.wait_ge(s_w, 16 * 3)
            pe.wait_ge(s_x, 1)
            for c in range(NC):
                project(bank[c][:], wm0[:, 1], xnT, 128 * c).then_inc(s_m0_ps, 1)
            pe.wait_ge(s_xc0, 2)
            for c in range(NC):
                project(bank[2 + c][:], wm0[:, 0], xc, 128 * c).then_inc(s_m0_ps, 1)
            for d in range(NC):
                last = mm(bank[4][0:2 * N, :], wbc0[:, d, :], xc[:, d, :], start=(d == 0), stop=(d == 1))
            last.then_inc(s_bc_ps, 1)
            pe.sem_inc(s_kfree, 2)
            pe.wait_ge(s_wklo, 1)

            def broadcast_b(j, k, m):
                n = 4 * j + (2 * k + m)
                pe.wait_ge(s_ssm, 6 * n + 8)
                mm(bank[6][:], sel[:, one(n), :].rearrange("p o m -> p (o m)"), bcs[:],
                   start=True, stop=True).then_inc(s_B, 1)

            def broadcast_c(j, k, m):
                n = 4 * j + (2 * k + m)
                pe.wait_ge(s_ssm, 6 * n + 12)
                mm(bank[7][:], sel[:, one(n + N), :].rearrange("p o m -> p (o m)"), bcs[:],
                   start=True, stop=True).then_inc(s_C, 1)

            def keys(j, q):
                k, g = q // G % 2, q % G
                pe.wait_ge(s_clo, 2 * G * j + (q + 1))
                pe.wait_ge(s_z, 2 * G * j + (q + 1))
                for a in range(2 if g < G - 1 else 1):
                    kt = 2 * g + a
                    p = 128 if kt < KT - 1 else KLAST
                    for d in range(NC):
                        hi, lo = chi[:, d, 128 * kt:128 * kt + p], clo[k][:, d, 128 * kt:128 * kt + p]
                        for i, (x, w) in enumerate(((hi, wkhi), (hi, wklo), (lo, wkhi))):
                            last = mm(bank[q % 2][0:p, D * a:D * a + D], x, w[:, d, :], start=(d == 0 and i == 0),
                                      stop=(d == 1 and i == 2))
                last.then_inc(s_kp, 1)

            def outer(j, q):
                k, g = q // G, q % G
                if g == 0:
                    pe.wait_ge(s_ctxN[k], 16 * j + 16)
                    pe.wait_ge(s_ktc, 4 * j + (2 * k + 2))
                pe.wait_ge(s_kt, 2 * G * j + (q + 3))
                for a in range(2 if g < G - 1 else 1):
                    kt = 2 * g + a
                    p = 128 if kt < KT - 1 else KLAST
                    for c in range(NC):
                        last = mm(bank[2 + 2 * k + c][:, 0:D + 1], kk[q % 2][0:p, D * a + 128 * c:D * a + 128 * c + 128],
                                  cN[k][0:p, kt, :], start=(kt == 0), stop=(kt == KT - 1))
                last.then_inc(s_kfree, 1)

            def states(j, last):
                for q in range(2 * G):
                    k, g = q // G, q % G
                    if g == 0:
                        broadcast_b(j, k, 0)
                    if not (last and q == 2 * G - 1):
                        keys(j, q + 1)
                    outer(j, q)
                    if g == 0:
                        broadcast_c(j, k, 0)
                    if g == 1:
                        broadcast_b(j, k, 1)
                    if g == 3:
                        broadcast_c(j, k, 1)

            pe.wait_ge(s_ge, 2)
            keys(0, 0)
            pe.wait_ge(s_bcs, 2)
            pe.wait_ge(s_sel, 16)
            pe.wait_ge(s_yadd, 8)
            with pe.Fori(0, B // 2 - 1) as j:
                states(j, False)
            states(B // 2 - 1, True)
            pe.wait_ge(s_yg, 2)
            for t in range(NT):
                token_major(bank[t], ym, wm0[:, 2], t).then_inc(s_proj1, 1)

            pe.wait_ge(s_w2, 16 * 2)
            pe.wait_ge(s_x, 2)
            for t in range(NT):
                pe.wait_ge(s_xn, NT * 2 + t + 1)
                for c in range(NC):
                    last = mm(bank[3][:, B * c + 2 * t:B * c + 2 * t + 2], xn[:, t, 128 * c:128 * c + 128], C("half"),
                              start=True, stop=True)
            last.then_inc(s_ms_ps, 1)
            transposes(3, False)
            pe.wait_ge(s_ms, 1)
            for d in range(NC):
                last = mm(bank[0][0:B, 0:E], msum[:, d, :], wr[:, d, :], start=(d == 0), stop=(d == 1))
            last.then_inc(s_rt_ps, 1)
            pe.wait_ge(s_topf, 1)
            te.transpose(bank[1][0:1, 0:B], topf[:], C("ident", 0, B, p=B)).then_inc(s_topT, 1)
            pe.wait_ge(s_hot, 1)
            mm(bank[2][0:E, :], hot[:], C("batch", p=B), start=True, stop=True).then_inc(s_hot_ps, 1)
            pe.wait_ge(s_hott, 1)
            pe.wait_ge(s_xnT, 2 * 3)

            def hidden0(t, h):
                b = 2 * t + h
                k = b % 4
                pe.wait_ge(s_wa0[k], 16 * (b // 4 + 1))
                for i in range(2):
                    if t >= 2 and h == 0:
                        pe.wait_ge((s_hf0, s_hf1)[i], t - 1)
                    for d in range(NC):
                        at = F0 * d + 512 * i
                        last = mm(bank[2 * (t % 2) + i][64 * h:64 * h + 64, :], xnT[:, d, T * b:T * b + T],
                                  wf0[k][:, at:at + 512], start=(d == 0), stop=(d == 1))
                    if h == 1:
                        last.then_inc(s_h_ps, 1)

            hidden0(0, 0)
            hidden0(0, 1)
            for t in range(NT):
                if t < NT - 1:
                    hidden0(t + 1, 0)
                pe.wait_ge(s_hf0, t + 1)
                pe.wait_ge(s_hf1, t + 1)
                if t:
                    pe.wait_ge(s_hb, 4 * t)
                for f in range(8):
                    last = te.transpose(bank[4 + f // 4][:, 128 * (f % 4):128 * (f % 4) + 128],
                                        hf[t % 2][:, 128 * f:128 * f + 128], ident)
                last.then_inc(s_hT_ps, 1)
                if t < NT - 1:
                    hidden0(t + 1, 1)
                mm(bank[6 + t % 2][:, 0:D], hott[0:E, 128 * t:128 * t + 128], b2t[:], start=True, stop=False)
                for h in range(2):
                    k = (2 * t + h) % 4
                    pe.wait_ge(s_wb0[k], 16 * (t // 2 + 1))
                    for f in range(8):
                        if h == 0 and f % 4 == 0:
                            pe.wait_ge(s_hr, 2 * t + f // 4 + 1)
                        at = W0SPLIT + D * f
                        last = mm(bank[6 + t % 2][64 * h:64 * h + 64, 0:D], hr[t % 2][:, f, T * h:T * h + T],
                                  wf0[k][:, at:at + D], start=False, stop=(f == 7))
                last.then_inc(s_y_ps, 1)

            transposes(4)
            pe.wait_ge(s_x, 3)
            for c in range(NC):
                project(bank[c][:], wx1[:, 0], xnT, 128 * c).then_inc(s_q1_ps, 1)
            pe.wait_ge(s_Q1, 2)
            pe.wait_ge(s_ktc, 4 + 2 * B)
            def weighted(t):
                for h in range(2):
                    b = 2 * t + h
                    for e in range(NC):
                        last = mm(bank[2 + t][64 * h:64 * h + 64, 0:D], QT[:, e, T * b:T * b + T], ktc[:, b, e, 0:D],
                                  start=(e == 0), stop=(e == 1))
                last.then_inc(s_G_ps, 1)

            def turn(t):
                pe.wait_ge(s_G, t + 1)
                for c in range(NC):
                    last = te.transpose(bank[6 + c][:, 128 * t:128 * t + 128], Gt[:, t, 128 * c:128 * c + 128], ident)
                last.then_inc(s_GT_ps, 1)

            weighted(0)
            for t in range(1, NT):
                weighted(t)
                turn(t - 1)
            turn(NT - 1)
            pe.wait_ge(s_qk, NC)
            for c in range(NC):
                for d in range(NC):
                    mm(bank[c][:], R("bv1")[:, 128 * c:128 * c + 128], qk[:, d, :], start=(d == 0), stop=False)
            pe.wait_ge(s_GT, NC)
            for c in range(NC):
                for d in range(NC):
                    last = mm(bank[c][:], wx1[:, 2, d, 128 * c:128 * c + 128], GT[:, d, :], start=False, stop=(d == 1))
                last.then_inc(s_num, 1)
            pe.wait_ge(s_aT, 2)
            for t in range(NT):
                token_major(bank[2 + t], aT, wx1[:, 3], t).then_inc(s_proj2, 1)

            transposes(5)
            pe.wait_ge(s_w3, 16 * 4)
            for m in range(8):
                project(bank[m][:], win, xnT, 128 * m).then_inc(s_in_ps, 1)
            pe.wait_ge(s_xs1, 4)
            for i in range(4):
                last = mm(bank[0][0:BCW, :], wbc1[:, i, :], xs1[:, i, :], start=(i == 0), stop=(i == 3))
            last.then_inc(s_bc1, 1)
            pe.wait_ge(s_pr1, 1)
            mm(bank[1][:], C("ones", p=N), pr1[0:N, :], start=True, stop=True).then_inc(s_ys, 1)
            pe.wait_ge(s_res, 4)
            for c in range(4):
                pe.wait_ge(s_y2, c + 1)
                for t in range(NT):
                    last = mm(bank[4 + t][:, 0:D], y2[:, c, 128 * t:128 * t + 128], wout[:, c, :], start=(c == 0), stop=(c == 3))
                    if c == 3:
                        last.then_inc(s_proj3, 1)

            transposes(6)
            for t in range(NT):
                for d in range(NC):
                    last = mm(bank[4][:, E * t:E * t + E], xnT[:, d, 128 * t:128 * t + 128], wg1[:, d, :],
                              start=(d == 0), stop=(d == 1))
            last.then_inc(s_lg, 1)
            pe.wait_ge(s_xlo, 2)
            pe.sem_inc(s_hfree, 2)

            def hidden(j, q):
                i, k, f = q % 2, q // 6 % 2, q % 6
                if f == 0:
                    pe.wait_ge(s_wlo, 2 * PIECES * j + PIECES * (q // 6 + 1))
                pe.wait_ge(s_hid, 12 * j + (q + 1))
                for h in range(2 if f < 5 else 1):
                    for d in range(NC):
                        m = 128 if f < 5 else TAIL
                        at = 4 * 128 * f + (NC * h + d) * m
                        hi, lo = whi[k][:, at:at + m], wlo[k][:, at:at + m]
                        for p, (a, b) in enumerate(((hi, xhi), (hi, xlo), (lo, xhi))):
                            last = mm(bank[2 * i + h][0:m, :], a, b[:, d, :], start=(d == 0 and p == 0),
                                      stop=(d == 1 and p == 2))
                last.then_inc(s_h12, 1)

            def output(j, q):
                i, k, f = q % 2, q // 6, q % 6
                w = F1C[f]
                at = W1AT + f * D
                hi, lo = whi[k][0:w, at:at + D], wlo[k][0:w, at:at + D]
                for t in range(NT):
                    if f == 0:
                        pe.wait_ge(s_ofree, 8 * j + (4 * k + t + 1))
                    if t == 0:
                        pe.wait_ge(s_hlo, 12 * j + (q + 1))
                    for p, (a, b) in enumerate(((hhi, hi), (hhi, lo), (hlo, hi))):
                        last = mm(bank[4 + t][:, 0:D], a[i][0:w, 128 * t:128 * t + 128], b,
                                  start=(f == 0 and p == 0), stop=(f == 5 and p == 2))
                    if f == 5 and t < NT - 1:
                        last.then_inc(s_o_ps, 1)
                last.then_inc(s_hfree, 1)

            hidden(0, 0)
            with pe.Fori(0, E // 2 - 1) as j:
                for q in range(12):
                    hidden(j, q + 1)
                    output(j, q)
            for q in range(12):
                if q < 11:
                    hidden(E // 2 - 1, q + 1)
                output(E // 2 - 1, q)


_OUT = ((128, NT, D), "float32")


def kernel(**inputs):
    import ml_dtypes
    import numpy as np
    import concourse.bacc as bacc
    from concourse import mybir
    from concourse.bass_utils import run_bass_kernel_spmd

    a = {k: np.asarray(v) for k, v in inputs.items()}

    def feature_rows(w, n):
        return w.reshape(n, 128, -1).transpose(1, 0, 2)

    def columns(v):
        return v.reshape(-1, 128).T

    ctx = np.concatenate([a["ctx_1024"][:, T:], a["ctx_1024"][:, :T]], axis=1)
    ctx_t = ctx.transpose(0, 2, 1).reshape(B, NC, 128, S).transpose(0, 2, 1, 3)
    ctx_n = np.zeros((B, KT * 128, D), np.float32)
    ctx_n[:, :S] = ctx
    ctx_n = ctx_n.reshape(B, KT, 128, D).transpose(0, 2, 1, 3)
    first = a["ctx_1024"][:, :T].reshape(TOK, D).T

    a1 = np.zeros((128, 1), np.float32)
    a1[:N, 0] = a["L1_attn_A"]
    cols = {
        "bq0": columns(a["L0_xattn_bq"]), "bk0": columns(a["L0_xattn_bk"]), "bv0": columns(a["L0_xattn_bv"]),
        "conv0": feature_rows(a["L0_attn_conv_w"].reshape(D, 4), 2).reshape(128, 8),
        "conv0b": columns(a["L0_attn_conv_b"]), "bd": columns(a["L0_attn_bd"]), "bg": columns(a["L0_attn_bg"]),
        "log_a": feature_rows(a["L0_attn_log_a"], 2).reshape(128, 32), "bq1": columns(a["L1_xattn_bq"]),
        "conv1": feature_rows(a["L1_attn_conv_w"].reshape(DI, 3), 4).reshape(128, 12),
        "conv1b": columns(a["L1_attn_conv_b"]), "D1": columns(a["L1_attn_D"]), "A1": a1}
    rows = {"bo0": a["L0_xattn_bo"], "boa": a["L0_attn_bo"], "bk1": a["L1_xattn_bk"], "bv1": a["L1_xattn_bv"],
            "bo1": a["L1_xattn_bo"], "gamma": a["L1_xattn_gamma"], "beta": a["L1_xattn_beta"], "br": a["L0_ffn_br"]}

    p = np.arange(128)
    batch = np.zeros((128, NT, 128), np.float32)
    for t in range(NT):
        batch[2 * t + p // 64, t, p] = 1
    state = np.zeros((3, 32, 2 * N, 128), ml_dtypes.bfloat16)
    state[:, np.arange(32), np.arange(32)] = 1
    consts = {
        "ident": np.eye(128, dtype=np.float32),
        "causal": np.where(np.arange(T)[None] > (p % T)[:, None], -FMAX, 0).astype(np.float32),
        "parity": np.stack([(p // HD) % 2 == 0, (p // HD) % 2 == 1], 1).astype(np.float32),
        "iota": np.tile(np.arange(E, dtype=np.float32), (128, 1)),
        "eps": np.full((128, 1), 1e-5, np.float32), "one": np.ones((128, 1), np.float32),
        "minus1": np.full((128, 1), -1, np.float32), "batch": batch.reshape(128, -1),
        "half": np.stack([p < 64, p >= 64], 1).astype(np.float32),
        "ones": np.ones((128, 128), np.float32)}

    def square(*names):
        return np.stack([feature_rows(a[n].T, 2) for n in names], 1)

    w0 = np.concatenate([
        a["L0_ffn_W1"].reshape(E, NC, 128, F0).transpose(0, 2, 1, 3).reshape(E, 128, -1),
        a["L0_ffn_b1"].reshape(E, 8, 128).transpose(0, 2, 1),
        a["L0_ffn_W2"].reshape(E, 8, 128, D).transpose(0, 2, 1, 3).reshape(E, 128, -1)], 2)
    w3 = np.zeros((E, 6 * 128, D), np.float32)
    w3[:, :F1] = a["L1_ffn_W3"].transpose(0, 2, 1)
    w12 = np.stack([a[n].transpose(0, 2, 1).reshape(E, NC, 128, F1) for n in ("L1_ffn_W1", "L1_ffn_W2")], 1)
    full = w12[..., :640].reshape(E, 2, NC, 128, 5, 128).transpose(0, 3, 4, 1, 2, 5).reshape(E, 128, -1)
    tail = np.zeros((E, NC, 128, TAIL), np.float32)
    for h in range(2):
        tail[..., 64 * h:64 * h + F1C[5]] = w12[:, h, ..., 640:]
    w1 = np.concatenate([full, tail.transpose(0, 2, 1, 3).reshape(E, 128, -1),
                         w3.reshape(E, 6, 128, D).transpose(0, 2, 1, 3).reshape(E, 128, -1)], 2)

    bc1 = np.zeros((DI, BCW), np.float32)
    bc1[:, :N], bc1[:, 32:32 + N] = a["L1_attn_W_B"], a["L1_attn_W_C"]

    arrays = {
        "x": a["x"].reshape(NT, 128, D).transpose(1, 0, 2),
        "first_ctx": feature_rows(first, 2), "ctx_t": ctx_t, "ctx_n": ctx_n,
        "mask": a["mask_BxS2_bf0"][:, :T],
        "cols": np.concatenate([cols[n] for n in COLS], 1),
        "rows": np.concatenate([rows[n] for n in ROWS])[None],
        "consts": np.concatenate([consts[n] for n in CONSTS], 1),
        "w_x0": square("L0_xattn_Wq", "L0_xattn_Wk", "L0_xattn_Wv", "L0_xattn_Wo"),
        "w_m0": square("L0_attn_Wd", "L0_attn_Wg", "L0_attn_Wo"),
        "state": state.reshape(96, 2 * N, 128),
        "w_bc0": feature_rows(np.concatenate([a["L0_attn_Wb"], a["L0_attn_Wc"]], 0).T, 2),
        "w_r": feature_rows(a["L0_ffn_Wr"], 2), "w0": w0,
        "b_f0": a["L0_ffn_b2"],
        "w_x1": square("L1_xattn_Wq", "L1_xattn_Wk", "L1_xattn_Wv", "L1_xattn_Wo"),
        "w_in": feature_rows(a["L1_attn_W_in"], 2), "w_out": feature_rows(a["L1_attn_W_out"], 4),
        "w_bc1": feature_rows(bc1, 4),
        "w_g1": feature_rows(a["L1_ffn_Wg"].T, 2), "w1": w1}

    nc = bacc.Bacc("TRN2", target_bir_lowering=False, num_devices=1)
    fed, args = {}, []
    for name, v in arrays.items():
        v = np.ascontiguousarray(v)
        fed[f"in_{name}"] = v
        args.append(nc.dram_tensor(f"in_{name}", v.shape, mybir.dt.from_np(v.dtype), kind="ExternalInput").ap())
    shape, dtype = _OUT
    out = nc.dram_tensor("out", shape, mybir.dt.from_np(np.dtype(dtype)), kind="ExternalOutput").ap()
    perceiver(nc, *args, out)
    got = run_bass_kernel_spmd(nc, [fed], core_ids=[0]).results[0]["out"]
    return np.asarray(got).transpose(1, 0, 2).reshape(B, T, D)
```
